# Optimizing a Trainium2 kernel written in Bass

```python
import numpy as np
import jax
import jax.numpy as jnp

def _softmax(x, axis=-1):
    return jax.nn.softmax(x, axis=axis)

def _gelu(x):
    return jax.nn.gelu(x, approximate=True)

def _silu(x):
    return jax.nn.silu(x)

def _sigmoid(x):
    return jax.nn.sigmoid(x)

def _layernorm(x, axis=-1, eps=1e-05):
    m = jnp.mean(x, axis=axis, keepdims=True)
    v = jnp.var(x, axis=axis, keepdims=True)
    return (x - m) / jnp.sqrt(v + eps)

def _scatter_add(tgt, idx, src, axis=0):
    return tgt.at[idx].add(src)

def _segment_sum(src, seg, n):
    return jax.ops.segment_sum(src, seg, n)
kernel_name = 'mk_gnn_preln_d4_gnn_r64_68c613'

def setup_inputs(seed: int=0):
    np.random.seed(seed)
    _w = jnp.asarray

    def _rec_inputs():
        import jax
        import jax.numpy as jnp
        _gk = jax.random.key(seed)
        x = -0.0001006 + 1 * jax.random.normal(jax.random.fold_in(_gk, 1), (50000, 96), jnp.float32)
        src = jax.random.randint(jax.random.fold_in(_gk, 2), (25000,), 0, 50000, jnp.int32)
        dst = jnp.minimum((50000 * jax.random.uniform(jax.random.fold_in(_gk, 3), (25000,)) ** 2.0).astype(jnp.int32), 49999)
        _o = jnp.argsort(dst, stable=True)
        src = src[_o]
        dst = dst[_o]
        edge_attr_3 = jax.random.uniform(jax.random.fold_in(_gk, 13), (25000, 3), jnp.float32, 0.0, 0.999999)
        return (x, src, dst, edge_attr_3)
    x, src, dst, edge_attr_3 = _rec_inputs()

    def _L0_gnn_setup():
        import jax, jax.numpy as jnp
        import numpy as np
        N, D = (50000, 96)
        E = 12500
        HID = 256
        EDGE_DIM = 3
        LN_EPS = 1e-05
        key = jax.random.key(seed)
        ks = jax.random.split(key, 14)
        x = jax.random.normal(ks[0], (N, D), dtype=jnp.float32)
        edge_index = jax.random.randint(ks[1], (2, E), 0, N, dtype=jnp.int64)
        edge_feat = jax.random.uniform(ks[2], (E, EDGE_DIM), dtype=jnp.float32)
        degrees = jax.random.uniform(ks[3], (N,), dtype=jnp.float32) * 32.0
        s1 = 1.0 / np.sqrt(EDGE_DIM)
        W1 = jax.random.uniform(ks[4], (EDGE_DIM, HID), jnp.float32, -s1, s1)
        b1 = jax.random.uniform(ks[5], (HID,), jnp.float32, -s1, s1)
        s2 = 1.0 / np.sqrt(HID)
        W2 = jax.random.uniform(ks[6], (HID, 1), jnp.float32, -s2, s2)
        b2 = jax.random.uniform(ks[7], (1,), jnp.float32, -s2, s2)
        sm1 = 1.0 / np.sqrt(2 * D + 1)
        Wm1 = jax.random.uniform(ks[8], (2 * D + 1, HID), jnp.float32, -sm1, sm1)
        bm1 = jax.random.uniform(ks[9], (HID,), jnp.float32, -sm1, sm1)
        sm2 = 1.0 / np.sqrt(HID)
        Wm2 = jax.random.uniform(ks[10], (HID, D), jnp.float32, -sm2, sm2)
        bm2 = jax.random.uniform(ks[11], (D,), jnp.float32, -sm2, sm2)
        gamma = jnp.ones((D,), dtype=jnp.float32)
        beta = jnp.zeros((D,), dtype=jnp.float32)
        return {'x': x, 'edge_index': edge_index, 'edge_feat': edge_feat, 'degrees': degrees, 'W1': W1, 'b1': b1, 'W2': W2, 'b2': b2, 'Wm1': Wm1, 'bm1': bm1, 'Wm2': Wm2, 'bm2': bm2, 'gamma': gamma, 'beta': beta}
    _L0_gnn_all = _L0_gnn_setup()
    _L0_gnn_in = {k: v for k, v in _L0_gnn_all.items() if k in ('W1', 'b1', 'W2', 'b2', 'Wm1', 'bm1', 'Wm2', 'bm2', 'gamma', 'beta')}
    del _L0_gnn_all

    def _L1_gnn_setup():
        import jax, jax.numpy as jnp
        import numpy as np
        N_NODES = 50000
        N_EDGES = 12500
        D_IN = 96
        D_OUT = 96
        key = jax.random.key(seed)
        k1, k2, k3, k4 = jax.random.split(key, 4)
        x = jax.random.normal(k1, (N_NODES, D_IN), dtype=jnp.float32)
        edge_index = jax.random.randint(k2, (2, N_EDGES), 0, N_NODES, dtype=jnp.int64)
        W = jax.random.normal(k3, (D_IN, D_OUT), dtype=jnp.float32) * (1.0 / np.sqrt(D_IN))
        b = jax.random.normal(k4, (D_OUT,), dtype=jnp.float32) * 0.01
        return {'x': x, 'edge_index': edge_index, 'W': W, 'b': b}
    _L1_gnn_all = _L1_gnn_setup()
    _L1_gnn_in = {k: v for k, v in _L1_gnn_all.items() if k in ('W', 'b')}
    del _L1_gnn_all

    def _L2_gnn_setup():
        import jax, jax.numpy as jnp
        import numpy as np
        N = 50000
        E = 12500
        C_IN = 96
        C_OUT = 96
        key = jax.random.key(seed)
        k1, k2, k3 = jax.random.split(key, 3)
        x = jax.random.normal(k1, (N, C_IN), dtype=jnp.float32)
        edge_index = jax.random.randint(k2, (2, E), 0, N, dtype=jnp.int64)
        W = jax.random.normal(k3, (C_IN, C_OUT), dtype=jnp.float32) / np.sqrt(C_IN)
        b = jnp.zeros((C_OUT,), dtype=jnp.float32)
        prelu_a = jnp.full((1,), 0.25, dtype=jnp.float32)
        return {'x': x, 'W': W, 'b': b, 'prelu_a': prelu_a, 'edge_index': edge_index}
    _L2_gnn_all = _L2_gnn_setup()
    _L2_gnn_in = {k: v for k, v in _L2_gnn_all.items() if k in ('W', 'b', 'prelu_a')}
    del _L2_gnn_all

    def _L3_gnn_setup():
        import jax, jax.numpy as jnp
        import numpy as np
        EPS = 1e-07
        BETA = 1.0
        key = jax.random.key(seed)
        k1, k2, k3, k4 = jax.random.split(key, 4)
        N, E, D_IN, D_OUT = (50000, 12500, 96, 96)
        feat = jax.random.normal(k1, (N, D_IN), dtype=jnp.float32)
        src = jax.random.randint(k2, (E,), 0, N, dtype=jnp.int32)
        dst = jax.random.randint(k3, (E,), 0, N, dtype=jnp.int32)
        W = jax.random.normal(k4, (D_IN, D_OUT), dtype=jnp.float32) / np.sqrt(D_IN)
        b = jnp.zeros((D_OUT,), dtype=jnp.float32)
        return {'feat': feat, 'src': src, 'dst': dst, 'W': W, 'b': b}
    _L3_gnn_all = _L3_gnn_setup()
    _L3_gnn_in = {k: v for k, v in _L3_gnn_all.items() if k in ('W', 'b')}
    del _L3_gnn_all
    return {'x': x, 'src': src, 'dst': dst, 'edge_attr_3': edge_attr_3, 'L0_gnn_W1': _L0_gnn_in['W1'], 'L0_gnn_b1': _L0_gnn_in['b1'], 'L0_gnn_W2': _L0_gnn_in['W2'], 'L0_gnn_b2': _L0_gnn_in['b2'], 'L0_gnn_Wm1': _L0_gnn_in['Wm1'], 'L0_gnn_bm1': _L0_gnn_in['bm1'], 'L0_gnn_Wm2': _L0_gnn_in['Wm2'], 'L0_gnn_bm2': _L0_gnn_in['bm2'], 'L0_gnn_gamma': _L0_gnn_in['gamma'], 'L0_gnn_beta': _L0_gnn_in['beta'], 'L1_gnn_W': _L1_gnn_in['W'], 'L1_gnn_b': _L1_gnn_in['b'], 'L2_gnn_W': _L2_gnn_in['W'], 'L2_gnn_b': _L2_gnn_in['b'], 'L2_gnn_prelu_a': _L2_gnn_in['prelu_a'], 'L3_gnn_W': _L3_gnn_in['W'], 'L3_gnn_b': _L3_gnn_in['b']}

def reference(x, src, dst, edge_attr_3, L0_gnn_W1, L0_gnn_b1, L0_gnn_W2, L0_gnn_b2, L0_gnn_Wm1, L0_gnn_bm1, L0_gnn_Wm2, L0_gnn_bm2, L0_gnn_gamma, L0_gnn_beta, L1_gnn_W, L1_gnn_b, L2_gnn_W, L2_gnn_b, L2_gnn_prelu_a, L3_gnn_W, L3_gnn_b):
    import jax
    import jax.numpy as jnp

    def _L0_gnn_ref(x, edge_index, edge_feat, degrees, W1, b1, W2, b2, Wm1, bm1, Wm2, bm2, gamma, beta):
        import jax, jax.numpy as jnp
        import numpy as np
        N, D = (50000, 96)
        E = 12500
        HID = 256
        EDGE_DIM = 3
        LN_EPS = 1e-05
        src, dst = (edge_index[0], edge_index[1])
        h = jax.nn.relu(edge_feat @ W1 + b1)
        w = jax.nn.sigmoid((h @ W2 + b2)[:, 0])
        msg = x[dst] * w[:, None]
        agg = jax.ops.segment_sum(msg, src, num_segments=N)
        deg = jnp.clip(degrees, 1.0, None)[:, None]
        agg = agg / deg
        feat = jnp.concatenate([x, agg, degrees[:, None]], axis=-1)
        out = jax.nn.relu(feat @ Wm1 + bm1) @ Wm2 + bm2
        y = x + out
        mu = jnp.mean(y, axis=-1, keepdims=True)
        var = jnp.var(y, axis=-1, keepdims=True)
        return (y - mu) * jax.lax.rsqrt(var + LN_EPS) * gamma + beta

    def _L1_gnn_ref(x, edge_index, W, b):
        import jax, jax.numpy as jnp
        import numpy as np
        N_NODES = 50000
        N_EDGES = 12500
        D_IN = 96
        D_OUT = 96
        num_nodes = x.shape[0]
        src, dst = (edge_index[0], edge_index[1])
        messages = x[src] @ W + b
        out = jax.ops.segment_sum(messages, dst, num_segments=num_nodes)
        deg = jax.ops.segment_sum(jnp.ones((dst.shape[0],), dtype=x.dtype), dst, num_segments=num_nodes)
        deg = jnp.clip(deg, 1.0, None)
        return out / deg[:, None]

    def _L2_gnn_ref(x, W, b, prelu_a, edge_index):
        import jax, jax.numpy as jnp
        import numpy as np
        N = 50000
        E = 12500
        C_IN = 96
        C_OUT = 96
        n = x.shape[0]
        row, col = (edge_index[0], edge_index[1])
        loop = jnp.arange(n, dtype=edge_index.dtype)
        row = jnp.concatenate([row, loop])
        col = jnp.concatenate([col, loop])
        deg = jax.ops.segment_sum(jnp.ones_like(col, dtype=x.dtype), col, num_segments=n)
        dinv = jnp.where(deg > 0, jax.lax.rsqrt(deg), jnp.zeros_like(deg))
        norm = dinv[row] * dinv[col]
        h = x @ W
        msg = h[row] * norm[:, None]
        out = jax.ops.segment_sum(msg, col, num_segments=n) + b
        return jnp.where(out >= 0, out, prelu_a * out)

    def _L3_gnn_ref(feat, src, dst, W, b):
        import jax, jax.numpy as jnp
        import numpy as np
        EPS = 1e-07
        BETA = 1.0
        N = feat.shape[0]
        m = jax.nn.relu(feat[src]) + EPS
        logits = BETA * m
        seg_max = jax.ops.segment_max(logits, dst, num_segments=N)
        ex = jnp.exp(logits - seg_max[dst])
        denom = jax.ops.segment_sum(ex, dst, num_segments=N)
        a = ex / denom[dst]
        msg = jax.ops.segment_sum(a * m, dst, num_segments=N)
        feats = feat + msg
        return feats @ W + b
    edge_index = jnp.stack([src, dst])
    deg = jnp.maximum(jax.ops.segment_sum(jnp.ones(dst.shape, jnp.float32), dst, num_segments=50000), 1.0)
    h = jnp.maximum(_layernorm(x, axis=-1), 0.0)
    x = x + _L0_gnn_ref(h, edge_index, edge_attr_3, deg, L0_gnn_W1, L0_gnn_b1, L0_gnn_W2, L0_gnn_b2, L0_gnn_Wm1, L0_gnn_bm1, L0_gnn_Wm2, L0_gnn_bm2, L0_gnn_gamma, L0_gnn_beta)
    h = jnp.maximum(_layernorm(x, axis=-1), 0.0)
    x = x + _L1_gnn_ref(h, edge_index, L1_gnn_W, L1_gnn_b)
    h = jnp.maximum(_layernorm(x, axis=-1), 0.0)
    x = x + _L2_gnn_ref(h, L2_gnn_W, L2_gnn_b, L2_gnn_prelu_a, edge_index)
    h = jnp.maximum(_layernorm(x, axis=-1), 0.0)
    x = x + _L3_gnn_ref(h, src, dst, L3_gnn_W, L3_gnn_b)
    return x

_drawn_inputs = setup_inputs


def setup_inputs(seed=0):
    import zlib

    import numpy as np

    out = dict(_drawn_inputs(seed))
    spreads = {'L0_gnn_gamma': (1.0, 0.2),
     'L0_gnn_beta': (0.0, 0.1),
     'L2_gnn_b': (0.0, 0.1),
     'L3_gnn_b': (0.0, 0.1)}
    factors = {'edge_attr_3': 64.0,
     'L0_gnn_W1': 8.0,
     'L0_gnn_b1': 64.0,
     'L0_gnn_W2': 40.868,
     'L0_gnn_bm1': 3.794,
     'L1_gnn_b': 21.923}
    for name, (base, spread) in spreads.items():
        noise = np.random.default_rng([zlib.crc32(name.encode()), seed]).standard_normal(out[name].shape)
        drawn = base * np.exp(spread * noise) if base else spread * noise
        out[name] = jnp.asarray(drawn.astype(out[name].dtype))
    for name, factor in factors.items():
        out[name] = (out[name] * factor).astype(out[name].dtype)
    return out
```

```python
import concourse.bass as bass
from concourse import mybir
from contextlib import ExitStack

F32 = mybir.dt.float32
I32 = mybir.dt.int32
BF16 = mybir.dt.bfloat16
ALU = mybir.AluOpType
ACT = mybir.ActivationFunctionType

P = 128
N, D, E = 50000, 96, 25000
HID = 256
LN_EPS, MSG_EPS = 1e-5, 1e-7

ROWS = N // P
MAIN = P * ROWS
TAIL = N - MAIN
G = 6
SUB = 3
GROUPS = ROWS // G
assert ROWS % G == 0 and GROUPS % 2 == 1

SORT, COLS = 32768, 256
TILES = -(-E // P)
CT = 7
CHUNKS = TILES // CT
CW = CT * P
assert TILES % CT == 0 and CHUNKS % 2 == 0

SRC_OFF = 256
SRC_PAD = 65024 - SRC_OFF
DST_LOW = 32768 + 128
DST_HALF = 25000
DST_HIGH = 128 - DST_HALF
DST_PAD = 32512 - DST_HIGH
SKIP = 100000

WCOLS = 500
WPAIRS = E // (2 * WCOLS)


class Group:

    def __init__(self, i, c):
        self.i, self.c = i, c
        self.known = isinstance(i, int)
        self.slot = c % 2
        self.num = 2 * i + c
        self.uses = i + c // 2
        self.live = not self.known or 0 <= self.num <= GROUPS
        self.tail = self.known and self.num == GROUPS
        self.w = 1 if self.tail else G

    def __add__(self, d):
        return Group(self.i, self.c + d)

    def tiles(self):
        return bass.ds(self.num * G, self.w)

    def cols(self):
        return bass.ds(self.num * G * D, self.w * D)


def wait(eng, sem, value):
    if not isinstance(value, int) or value > 0:
        eng.wait_ge(sem, value)


def over_groups(eng, step):
    for c in range(-3, 6):
        step(Group(0, c))
    with eng.Fori(0, (GROUPS - 9) // 2) as i:
        step(Group(i, 6))
        step(Group(i, 7))
    for c in range(GROUPS - 3, GROUPS + 6):
        step(Group(0, c))


class Chain:

    def __init__(self, eng, sem, base=0):
        self.eng, self.sem, self.base, self.k = eng, sem, base, 0

    def note(self, ins):
        ins.then_inc(self.sem, 1)
        self.k += 1

    def settle(self):
        self.eng.wait_ge(self.sem, self.base + self.k)

    def link(self, ins):
        self.note(ins)
        self.settle()


class Kernel:

    def __init__(self, nc):
        self.nc, self.stage, self.steps = nc, "", []

    def sem(self, name):
        self.steps.append(self.nc.alloc_semaphore(f"{self.stage}_{name}"))
        return self.steps[-1]

    def dma(self, name):
        return self.nc.alloc_semaphore(f"{self.stage}_{name}")

    def dmas(self, name):
        return [self.dma(f"{name}{s}") for s in range(2)]

    def end(self):
        self.nc.clear_and_free_semaphores(self.steps)
        self.nc.all_engine_barrier()
        self.steps = []


def group_rows(dram, g):
    if g.tail:
        return dram[MAIN:N, :]
    return dram[0:MAIN, :].rearrange("(p j) d -> p (j d)", p=P)[:, g.cols()]


def group_buf(buf, g):
    rows = TAIL if g.tail else P
    return buf[0:rows, 0:g.w, :].rearrange("p j d -> p (j d)")


def sort_stage(k, a, keep):
    nc = k.nc
    k.stage = "sort"
    with ExitStack() as mem:
        def sb(name, shape, dt=F32):
            return mem.enter_context(nc.sbuf_tensor(f"{k.stage}_{name}_sb", shape, dt))

        def ps(name, shape):
            return mem.enter_context(nc.psum_tensor(f"{k.stage}_{name}_ps", shape, F32))

        ends = sb("ends", [P, 2, COLS], I32)
        keys = [sb(f"keys{b}", [P, 2, COLS]) for b in range(2)]
        place = sb("place", [P, COLS], I32)
        part_i = sb("part_i", [P, 1], I32)
        sign = sb("sign", [P, 1])
        zeros = keep["node"][:, :, :].rearrange("p t j -> p (t j)")[:, 0:ROWS * D // 20]
        tmp = sb("tmp", [P, COLS], I32)
        tgt = sb("tgt", [P, 2, COLS], I32)
        nxt = sb("nxt", [P, 2, COLS], I32)
        prv = sb("prv", [P, 2, COLS], I32)
        same = sb("same", [P, 2, COLS], BF16)
        fidx = sb("fidx", [P, 5, COLS])
        none = sb("none", [2, 2], I32)
        feat = sb("feat", [4, 2, 2, WCOLS])
        w1 = sb("w1", [4, HID])
        w2 = sb("w2", [P, 2])
        b2 = sb("b2", [1, 1])
        hid = sb("hid", [P, 2, 2, WCOLS])
        wrow = sb("wrow", [1, 2, 2, WCOLS])
        wsq = keep["payload"][:, :, :].rearrange("p t c -> p (t c)").bitcast(F32)[:, 0:COLS]
        pay = sb("pay", [P, COLS, 2], I32)
        turn = ps("turn", [P, 2, 2, P])
        turn2 = ps("turn2", [P, 2, 2, P])
        turn3 = ps("turn3", [P, 2, 2, P])
        psh = ps("psh", [P, 2, 512])
        psw = ps("psw", [1, 2, 512])

        s_ends, s_x, s_zero, s_zfill = k.dma("ends"), k.dma("x"), k.sem("zero"), k.dma("zfill")
        s_const, s_key, s_ident = k.sem("const"), k.sem("key"), k.sem("ident")
        s_turn, s_flat = k.sem("turned"), k.sem("flat")
        s_tgt, s_near, s_same, s_none, s_pad = k.sem("tgt"), k.dma("near"), k.sem("same"), k.sem("none"), k.dma("pad")
        s_weights, s_ones = k.dma("weights"), k.sem("ones")
        s_feat, s_hid, s_relu, s_lin, s_sig, s_wst = k.dmas("feat"), k.sem("hid"), k.sem("relu"), k.sem("lin"), k.sem("sig"), k.dmas("wst")
        s_wsq, s_wz, s_pay, s_payst = k.dma("wsq"), k.sem("wz"), k.sem("pay"), k.dma("payst")
        s_fidx, s_xtail, s_store = k.sem("fidx"), k.sem("xtail"), k.dma("store")

        LEVELS = 15
        HALF_ROWS = E // COLS
        LAST_COLS = E - HALF_ROWS * COLS

        with nc.Block() as block:
            @block.sync
            def _(sp):
                sp.dma_start(ends[:, 0, :], a["src"]).then_inc(s_ends, 16)
                sp.dma_start(ends[:, 1, :], a["dst"]).then_inc(s_ends, 16)
                sp.dma_start(w1[0:1, :], a["L0_gnn_b1"].rearrange("(a n) -> a n", a=1)).then_inc(s_weights, 16)
                sp.dma_start(w1[1:4, :], a["L0_gnn_W1"]).then_inc(s_weights, 16)
                sp.dma_start(w2[:, 0:1], a["L0_gnn_W2"][0:P, :]).then_inc(s_weights, 16)
                sp.dma_start(w2[:, 1:2], a["L0_gnn_W2"][P:HID, :]).then_inc(s_weights, 16)
                sp.dma_start(b2[:, :], a["L0_gnn_b2"].rearrange("(a n) -> a n", a=1)).then_inc(s_weights, 16)

                def feat_load(i, s):
                    sp.dma_start(feat[1:4, s, :, :].rearrange("p a n -> p (a n)"),
                                 a["edge_attr_T"][:, bass.ds(i * (2 * WCOLS), 2 * WCOLS)]).then_inc(s_feat[s], 16)
                sp.wait_ge(s_ones, 1)
                feat_load(0, 0)
                step = ROWS // 10
                for n in range(10):
                    sp.dma_start(keep["x"][:, n * step * D:(n + 1) * step * D],
                                 a["x"][0:MAIN, :].rearrange("(p j) d -> p (j d)", p=P)[:, n * step * D:(n + 1) * step * D]
                                 ).then_inc(s_x, 16)
                sp.wait_ge(s_xtail, 1)
                sp.dma_start(keep["x"][0:TAIL, ROWS * D:(ROWS + 1) * D], a["x"][MAIN:N, :]).then_inc(s_x, 16)
                sp.wait_ge(s_zero, 1)
                zw = ROWS * D // 20
                for agg in (a["agg0"], a["agg"]):
                    flat = agg[0:MAIN, :].rearrange("(p j) d -> p (j d)", p=P)
                    for n in range(20):
                        sp.dma_start(flat[:, n * zw:(n + 1) * zw], zeros).then_inc(s_zfill, 16)
                    sp.dma_start(agg[MAIN:N, :], zeros[0:TAIL, 0:D]).then_inc(s_zfill, 16)
                sp.wait_ge(s_none, 1)
                for n in range(2):
                    for at in (0, SORT + 1):
                        sp.dma_start(a["targets"][n:n + 1, at:at + 1], none[0:1, 0:1]).then_inc(s_pad, 16)
                sp.wait_ge(s_tgt, 2)
                for n in range(2):
                    sp.dma_start(a["targets"][n, 1:SORT + 1].rearrange("(p f) -> p f", f=COLS),
                                 tgt[:, n, :]).then_inc(s_pad, 16)
                sp.wait_ge(s_pad, 16 * 6)
                for n in range(2):
                    sp.dma_start(nxt[:, n, :], a["targets"][n, 2:SORT + 2].rearrange("(p f) -> p f", f=COLS)).then_inc(s_near, 16)
                    sp.dma_start(prv[:, n, :], a["targets"][n, 0:SORT].rearrange("(p f) -> p f", f=COLS)).then_inc(s_near, 16)
                sp.wait_ge(s_same, 1)
                for n in range(2):
                    sp.dma_start(a["same"][n, :].rearrange("(p f) -> p f", f=COLS), same[:, n, :]).then_inc(s_store, 16)
                sp.wait_ge(s_x, 16 * 11)
                sp.wait_ge(s_zfill, 16 * 42)
                sp.wait_ge(s_store, 32)

            @block.gpsimd
            def _(pool):
                pool.memset(feat[:, :, :, :], 1.0).then_inc(s_ones, 1)
                pool.memset(keep["x"][:, ROWS * D:(ROWS + 1) * D], 0.0).then_inc(s_xtail, 1)
                pool.memset(none[:, :], -1).then_inc(s_none, 1)
                pool.memset(zeros, 0.0).then_inc(s_zero, 1)
                pool.memset(keep["ident"][:, :], 0.0).then_inc(s_ident, 1)
                pool.iota(place[:, :], pattern=[[1, COLS]], base=0, channel_multiplier=COLS).then_inc(s_const, 1)
                pool.iota(part_i[:, :], pattern=[[0, 1]], base=0, channel_multiplier=1).then_inc(s_const, 1)
                pool.wait_ge(s_ident, 1)
                pool.affine_select(out=keep["ident"][:, :], in_=keep["ident"][:, :], compare_op=ALU.not_equal,
                                   fill=1.0, base=0, pattern=[[-1, P]], channel_multiplier=1).then_inc(s_ident, 1)
                pool.memset(wsq, 0.0).then_inc(s_wz, 1)
                pool.wait_ge(s_wst[0], 16 * (WPAIRS // 2 + 1))
                pool.wait_ge(s_wst[1], 16 * (WPAIRS // 2))
                pool.wait_ge(s_wz, 1)
                pool.dma_start(wsq[0:HALF_ROWS, :], a["weights"][0:HALF_ROWS * COLS].rearrange("(p f) -> p f", f=COLS)).then_inc(s_wsq, 16)
                pool.dma_start(wsq[HALF_ROWS:HALF_ROWS + 1, 0:LAST_COLS],
                               a["weights"][HALF_ROWS * COLS:E].rearrange("(a f) -> a f", a=1)).then_inc(s_wsq, 16)
                pool.wait_ge(s_wsq, 32)
                pool.tensor_copy(pay[:, :, 0], ends[:, 1, :]).then_inc(s_pay, 1)
                pool.tensor_copy(pay[:, :, 1].bitcast(F32), wsq).then_inc(s_pay, 1)
                pool.wait_ge(s_pay, 2)
                rows = HALF_ROWS + 1
                pool.dma_start(a["payload"][:, :].rearrange("(p f) c -> p (f c)", p=rows),
                               pay[0:rows, :, :].rearrange("p f c -> p (f c)")).then_inc(s_payst, 16)
                pool.wait_ge(s_payst, 16)

            @block.tensor
            def _(pe):
                pe.wait_ge(s_ident, 2)

                def turns(cur, dst):
                    pe.wait_ge(s_key, cur)
                    for arr in range(2):
                        for h in range(2):
                            last = pe.transpose(turn[:, arr, h, :], dst[:, arr, h * P:(h + 1) * P], keep["ident"][:, :])
                    last.then_inc(s_turn, 1)

                for cur, b in k.turn_points:
                    turns(cur, keys[b])
                for n in range(5):
                    pe.wait_ge(s_fidx, n + 1)
                    for h in range(2):
                        bank = (turn, turn2, turn3)[n // 2]
                        last = pe.transpose(bank[:, n % 2, h, :], fidx[:, n, h * P:(h + 1) * P], keep["ident"][:, :])
                last.then_inc(s_turn, 1)
                pe.wait_ge(s_weights, 16 * 5)

                def pair(i, s, first):
                    pe.wait_ge(s_feat[s], 16 * (i + 1))
                    for c in range(2):
                        n = (2 * i + s) * 2 + c
                        if not (first and c == 0):
                            pe.wait_ge(s_relu, n * 1)
                        for h in range(2):
                            last = pe.matmul(psh[:, h, 0:WCOLS], w1[:, h * P:(h + 1) * P], feat[:, s, c, :], start=True, stop=True)
                        last.then_inc(s_hid, 1)
                        pe.wait_ge(s_relu, n + 1)
                        if not first:
                            pe.wait_ge(s_sig, n - 1)
                        for h in range(2):
                            last = pe.matmul(psw[:, c, 0:WCOLS], w2[:, h:h + 1], hid[:, c, h, :], start=(h == 0), stop=(h == 1))
                        last.then_inc(s_lin, 1)
                pair(0, 0, True)
                with pe.Fori(0, WPAIRS // 2) as i:
                    pair(i, 1, False)
                    pair(i + 1, 0, False)

            @block.scalar
            def _(act):
                act.wait_ge(s_weights, 16 * 5)
                act.wait_ge(s_ones, 1)

                def feat_load(i, s):
                    act.dma_start(feat[1:4, s, :, :].rearrange("p a n -> p (a n)"),
                                  a["edge_attr_T"][:, bass.ds((2 * i + s) * (2 * WCOLS), 2 * WCOLS)]).then_inc(s_feat[s], 16)

                def pair(i, s, first, more):
                    if more:
                        if not first:
                            act.wait_ge(s_lin, (2 * i + s) * 2)
                        feat_load(i + s, 1 - s)
                    for c in range(2):
                        n = (2 * i + s) * 2 + c
                        act.wait_ge(s_hid, n + 1)
                        if not first:
                            act.wait_ge(s_lin, n - 1)
                        act.activation(hid[:, c, :, :], psh[:, :, 0:WCOLS], ACT.Relu).then_inc(s_relu, 1)
                        act.wait_ge(s_lin, n + 1)
                        if c == 0:
                            if s == 1 or not first:
                                wait(act, s_wst[s], 16 * i)
                        act.activation(wrow[:, s, c, :], psw[:, c, 0:WCOLS], ACT.Sigmoid, bias=b2[0:1, 0:1]).then_inc(s_sig, 1)
                    act.wait_ge(s_sig, (2 * i + s) * 2 + 2)
                    act.dma_start(a["weights"][bass.ds((2 * i + s) * (2 * WCOLS), 2 * WCOLS)].rearrange("(a n) -> a n", a=1),
                                  wrow[:, s, :, :].rearrange("p a n -> p (a n)")).then_inc(s_wst[s], 16)
                pair(0, 0, True, True)
                pair(0, 1, False, True)
                pair(1, 0, False, True)
                with act.Fori(1, WPAIRS // 2 - 1) as i:
                    pair(i, 1, False, True)
                    pair(i + 1, 0, False, True)
                pair(WPAIRS // 2 - 1, 1, False, True)
                pair(WPAIRS // 2, 0, False, False)

            @block.vector
            def _(dve):
                ch = [0]

                def link(ins):
                    ch[0] += 1
                    ins.then_inc(s_key, 1)

                def settle():
                    dve.wait_ge(s_key, ch[0])

                dve.wait_ge(s_ends, 32)
                dve.wait_ge(s_const, 2)
                ki = [b[:, :, :].bitcast(I32) for b in keys]
                link(dve.tensor_scalar(tmp[:, :], ends[:, 0, :], float(SRC_OFF), None, ALU.add))
                link(dve.tensor_scalar(nxt[:, 1, :], ends[:, 1, :], float(DST_HALF), float(DST_HIGH - DST_LOW), ALU.is_ge, ALU.mult))
                link(dve.tensor_scalar(part_i[:, :], part_i[:, :], 1, None, ALU.bitwise_and))
                settle()
                link(dve.tensor_scalar(nxt[:, 0, :], tmp[:, :], 15, None, ALU.logical_shift_left))
                link(dve.scalar_tensor_tensor(prv[:, 1, :], ends[:, 1, :], float(DST_LOW), nxt[:, 1, :], ALU.add, ALU.add))
                link(dve.tensor_scalar(sign[:, :], part_i[:, :], -2.0, 1.0, ALU.mult, ALU.add))
                settle()
                link(dve.tensor_tensor(ki[0][:, 0, :], nxt[:, 0, :], place[:, :], ALU.bitwise_or))
                link(dve.tensor_scalar(prv[:, 0, :], prv[:, 1, :], 16, None, ALU.logical_shift_left))
                settle()
                link(dve.tensor_tensor(ki[0][:, 1, :], prv[:, 0, :], ends[:, 0, :], ALU.bitwise_or))
                settle()
                cur = 0

                def compare(cur, d):
                    x = keys[cur][:, :, :].rearrange("p a (b t k) -> p (a b) t k", t=2, k=d)
                    y = keys[1 - cur][:, :, :].rearrange("p a (b t k) -> p (a b) t k", t=2, k=d)
                    link(dve.tensor_tensor(y[:, :, 0, :], x[:, :, 0, :], x[:, :, 1, :], ALU.min))
                    link(dve.tensor_tensor(y[:, :, 1, :], x[:, :, 0, :], x[:, :, 1, :], ALU.max))
                    settle()
                    return 1 - cur

                def negate(cur, width, lo, hi):
                    v = keys[cur][:, :, :].rearrange("p a (b m) -> p (a b) m", m=width)[:, :, lo:hi]
                    link(dve.tensor_scalar(v, v, -1.0, None, ALU.mult))
                    settle()

                points = []

                def turn_over(cur):
                    points.append((ch[0], cur))
                    dve.wait_ge(s_turn, len(points))
                    link(dve.tensor_copy(keys[1 - cur][:, :, :], turn[:, :, :, :].rearrange("p a h m -> p a (h m)")))
                    settle()
                    return 1 - cur

                for m in range(1, LEVELS + 1):
                    if m == 1:
                        negate(cur, 4, 2, 4)
                    elif m <= 7:
                        negate(cur, 2 << m, 1 << (m - 1), 3 << (m - 1))
                    elif m == 8:
                        for f0, sg in ((0, 1.0), (P, -1.0)):
                            v = keys[cur][:, :, f0:f0 + P]
                            link(dve.tensor_scalar(v, v, sign[:, 0:1], sg, ALU.mult, ALU.mult))
                        settle()
                    if m <= 8:
                        for j in reversed(range(m)):
                            cur = compare(cur, 1 << j)
                        continue
                    cur = turn_over(cur)
                    if m < LEVELS:
                        negate(cur, 2 << (m - 8), 1 << (m - 9), 3 << (m - 9))
                    else:
                        negate(cur, P, P // 2, P)
                    for j in reversed(range(8, m)):
                        cur = compare(cur, 1 << (j - 8))
                    cur = turn_over(cur)
                    for j in reversed(range(8)):
                        cur = compare(cur, 1 << j)
                assert points == k.turn_points, points

                v = ki[cur]
                fr = ki[1 - cur]
                link(dve.tensor_scalar(tmp[:, :], v[:, 0, :], 15, None, ALU.logical_shift_right))
                link(dve.tensor_scalar(fr[:, 1, :], v[:, 1, :], 16, None, ALU.logical_shift_right))
                link(dve.tensor_scalar(fr[:, 0, :], v[:, 0, :], (1 << 15) - 1, None, ALU.bitwise_and))
                settle()
                dve.tensor_scalar(tgt[:, 0, :], tmp[:, :], float(-SRC_OFF), None, ALU.add).then_inc(s_tgt, 1)
                link(dve.tensor_scalar(nxt[:, 1, :], fr[:, 1, :], 32768.0, float(DST_HIGH - DST_LOW), ALU.is_ge, ALU.mult))
                dve.tensor_scalar(fidx[:, 0, :], fr[:, 0, :], float(E - 1), None, ALU.min).then_inc(s_fidx, 1)
                settle()
                dve.scalar_tensor_tensor(tgt[:, 1, :], fr[:, 1, :], float(-DST_HIGH), nxt[:, 1, :], ALU.add, ALU.add).then_inc(s_tgt, 1)
                dve.wait_ge(s_fidx, 1)
                link(dve.tensor_scalar(fr[:, 0, :], v[:, 1, :], (1 << 16) - 1, None, ALU.bitwise_and))
                settle()
                dve.wait_ge(s_tgt, 2)
                dve.tensor_scalar(fidx[:, 1, :], fr[:, 0, :], float(N - 1), None, ALU.min).then_inc(s_fidx, 1)
                dve.wait_ge(s_near, 64)
                dve.tensor_tensor(same[:, :, :], tgt[:, :, :], prv[:, :, :], ALU.is_equal).then_inc(s_same, 1)
                dve.wait_ge(s_same, 1)
                link(dve.tensor_tensor(prv[:, :, :], tgt[:, :, :], nxt[:, :, :], ALU.is_equal))
                settle()
                for n in range(2):
                    dve.scalar_tensor_tensor(fidx[:, 2 + n, :], prv[:, n, :], float(SKIP), tgt[:, n, :],
                                             ALU.mult, ALU.add).then_inc(s_fidx, 1)
                dve.tensor_copy(fidx[:, 4, :], tgt[:, 1, :]).then_inc(s_fidx, 1)
                dve.wait_ge(s_turn, len(points) + 1)
                half = TILES // 2
                for n in range(5):
                    bank = (turn, turn2, turn3)[n // 2]
                    out = keep["index"][:, n, :] if n < 4 else keep["dst"][:, :]
                    for h in range(2):
                        dve.tensor_copy(out[:, h:TILES:2], bank[:, n % 2, h, 0:half]).then_inc(s_fidx, 1)


def turn_points():
    out, ch, cur = [], 9, 0
    for m in range(1, 16):
        if m <= 7:
            ch += 1
        elif m == 8:
            ch += 2
        if m <= 8:
            ch += 2 * m
            cur ^= m & 1
            continue
        out.append((ch, cur))
        ch, cur = ch + 2 + 2 * (m - 8), cur ^ 1 ^ (m & 1)
        out.append((ch, cur))
        ch, cur = ch + 1 + 16, cur ^ 1
    return out


class Norm:

    SUM, DIFF, SQ, M2, VAR, STD, RSTD, SHIFT = range(8)
    STATS = G + 4
    SCALES = 1

    def __init__(self, sb, name):
        self.bn = [sb(f"{name}_bn{s}", [P, G, 6]) for s in range(2)]
        self.st = [sb(f"{name}_st{s}", [P, 8, G]) for s in range(2)]


def ln_stats(nc, ch, norm, g, tile):
    bn, st, w = norm.bn[g.slot], norm.st[g.slot], g.w
    for j in range(w):
        ch.note(nc.vector.bn_stats(bn[:, j, :], tile(j)))
    ch.settle()
    ch.note(nc.vector.tensor_tensor(st[:, norm.SUM, 0:w], bn[:, 0:w, 1], bn[:, 0:w, 4], ALU.add))
    ch.note(nc.vector.tensor_tensor(st[:, norm.DIFF, 0:w], bn[:, 0:w, 1], bn[:, 0:w, 4], ALU.subtract))
    ch.note(nc.vector.tensor_tensor(st[:, norm.M2, 0:w], bn[:, 0:w, 2], bn[:, 0:w, 5], ALU.add))
    ch.settle()
    ch.link(nc.vector.tensor_tensor(st[:, norm.SQ, 0:w], st[:, norm.DIFF, 0:w], st[:, norm.DIFF, 0:w], ALU.mult))
    return nc.vector.scalar_tensor_tensor(st[:, norm.VAR, 0:w], st[:, norm.SQ, 0:w], D / 4, st[:, norm.M2, 0:w],
                                          ALU.mult, ALU.add)


def ln_sqrt(nc, norm, g, eps):
    st, w = norm.st[g.slot], g.w
    return nc.scalar.activation(st[:, norm.STD, 0:w], st[:, norm.VAR, 0:w], ACT.Sqrt, bias=eps[:, 0:1], scale=1.0 / D)


def ln_scales(nc, ch, norm, g):
    st, w = norm.st[g.slot], g.w
    ch.link(nc.vector.reciprocal(st[:, norm.RSTD, 0:w], st[:, norm.STD, 0:w]))
    return nc.vector.scalar_tensor_tensor(st[:, norm.SHIFT, 0:w], st[:, norm.SUM, 0:w], -0.5, st[:, norm.RSTD, 0:w],
                                          ALU.mult, ALU.mult)


def ln_apply(nc, norm, g, func, out, tile, factors=None, tiles=None):
    st = norm.st[g.slot]
    by, add = (st[:, norm.RSTD, :], st[:, norm.SHIFT, :]) if factors is None else (factors[g.slot][:, 0, :], factors[g.slot][:, 1, :])
    for j in range(g.w) if tiles is None else tiles:
        last = nc.scalar.activation(out(j), tile(j), func, bias=add[:, j:j + 1], scale=by[:, j:j + 1])
    return last


def x_tile(keep, g, j):
    return keep["x"][:, bass.ds(g.num * (G * D) + j * D, D)]


def first_stage(k, a, keep):
    nc = k.nc
    k.stage = "first"
    with ExitStack() as mem:
        def sb(name, shape, dt=F32):
            return mem.enter_context(nc.sbuf_tensor(f"{k.stage}_{name}_sb", shape, dt))

        gidx = [sb(f"gidx{s}", [P, CT], I32) for s in range(2)]
        gbuf = [sb(f"gbuf{s}", [P, CT, 2], I32) for s in range(2)]
        iota_i = sb("iota_i", [P, ROWS + 1], I32)
        iota_f = sb("iota_f", [P, ROWS + 1])
        hi, lo, t0, t1 = (sb(n, [P, TILES]) for n in ("hi", "lo", "t0", "t1"))
        HOT = 4
        hot_lo = [sb(f"hot_lo{s}", [P, P], BF16) for s in range(HOT)]
        hot_hi = [sb(f"hot_hi{s}", [P, ROWS + 1], BF16) for s in range(HOT)]
        c1 = sb("c1", [P, ROWS + 1])
        norm = Norm(sb, "norm")
        hout = [sb(f"hout{s}", [P, G, D]) for s in range(2)]
        count = mem.enter_context(nc.psum_tensor("first_count_ps", [P, 512], F32))

        s_idx, s_out, s_alone = k.sem("idx"), k.sem("out"), k.sem("alone")
        s_gath = k.dmas("gath")
        s_iota, s_hot, s_used = k.sem("iota"), k.sem("hot"), k.sem("used")
        s_dve, s_c1, s_sq, s_eps = k.sem("dve"), k.sem("c1"), k.sem("sq"), k.sem("eps")
        s_var, s_std, s_scale, s_norm = k.sem("var"), k.sem("std"), k.sem("scale"), k.sem("norm")
        s_store = k.dmas("store")

        with nc.Block() as block:
            @block.gpsimd
            def _(pool):
                pool.iota(iota_i[:, :], pattern=[[1, ROWS + 1]], base=0, channel_multiplier=0).then_inc(s_iota, 1)
                pool.memset(keep["eps"][:, 0:1], LN_EPS).then_inc(s_eps, 1)
                pool.memset(keep["eps"][:, 1:2], MSG_EPS)

                def gather(i, s):
                    pool.tensor_copy(gidx[s][:, :], keep["index"][:, 0, bass.ds((2 * i + s) * CT, CT)]).then_inc(s_idx, 1)
                    pool.wait_ge(s_idx, 2 * i + s + 1)
                    alone(pool, s_alone)
                    for j in range(CT):
                        pool.indirect_dma_start(gbuf[s][:, j, :], None, a["payload"],
                                                bass.IndirectOffsetOnAxis(gidx[s][:, j:j + 1], 0)).then_inc(s_gath[s], 16)

                def keep_it(i, s):
                    pool.wait_ge(s_gath[s], (i + 1) * (16 * CT))
                    pool.tensor_copy(keep["payload"][:, bass.ds((2 * i + s) * CT, CT), :], gbuf[s][:, :, :]).then_inc(s_out, 1)
                    pool.wait_ge(s_out, 2 * i + s + 1)
                gather(0, 0)
                with pool.Fori(0, CHUNKS // 2 - 1) as i:
                    gather(i, 1)
                    keep_it(i, 0)
                    gather(i + 1, 0)
                    keep_it(i, 1)
                gather(CHUNKS // 2 - 1, 1)
                keep_it(CHUNKS // 2 - 1, 0)
                keep_it(CHUNKS // 2 - 1, 1)

            @block.tensor
            def _(pe):
                def add(i, s, start, stop):
                    pe.wait_ge(s_hot, (i * HOT + s + 1) * 2)
                    pe.matmul(count[:, 0:ROWS + 1], hot_lo[s][:, :], hot_hi[s][:, :], start=start, stop=stop).then_inc(s_used, 1)
                for s in range(HOT):
                    add(0, s, s == 0, False)
                with pe.Fori(1, TILES // HOT - 1) as i:
                    for s in range(HOT):
                        add(i, s, False, False)
                for s in range(HOT):
                    add(TILES // HOT - 1, s, False, s == HOT - 1)

            @block.vector
            def _(dve):
                ch = Chain(dve, s_dve)
                dve.wait_ge(s_iota, 1)
                magic = 1.5 * 2 ** 23
                n = keep["dst"]
                ch.note(dve.tensor_copy(iota_f[:, :], iota_i[:, :]))
                ch.note(dve.tensor_scalar(t0[:, :], n[:, :], -(ROWS - 1) / 2, 1.0 / ROWS, ALU.add, ALU.mult))
                ch.settle()
                ch.link(dve.tensor_scalar(t1[:, :], t0[:, :], magic, None, ALU.add))
                ch.link(dve.tensor_scalar(lo[:, :], t1[:, :], -magic, None, ALU.add))
                ch.link(dve.scalar_tensor_tensor(hi[:, :], lo[:, :], float(-ROWS), n[:, :], ALU.mult, ALU.add))
                ch.note(dve.tensor_tensor(t0[:, :], hi[:, :], lo[:, :], ALU.subtract))
                ch.note(dve.tensor_scalar(t1[:, :], n[:, :], float(MAIN), None, ALU.is_ge))
                ch.settle()
                ch.link(dve.tensor_tensor(t0[:, :], t0[:, :], t1[:, :], ALU.mult))
                ch.link(dve.tensor_tensor(lo[:, :], lo[:, :], t0[:, :], ALU.add))
                ch.link(dve.tensor_scalar(t0[:, :], hi[:, :], -1.0, float(ROWS), ALU.mult, ALU.add))
                ch.link(dve.tensor_tensor(t0[:, :], t0[:, :], t1[:, :], ALU.mult))
                ch.link(dve.tensor_tensor(hi[:, :], hi[:, :], t0[:, :], ALU.add))
                ch.link(dve.tensor_scalar(t0[:, :], n[:, :], float(N), 1000.0, ALU.is_ge, ALU.mult))
                ch.link(dve.tensor_tensor(lo[:, :], lo[:, :], t0[:, :], ALU.add))
                ch.link(dve.tensor_scalar(t0[:, :], n[:, :], float(N), 1000.0, ALU.is_ge, ALU.mult))

                def hot(i, s, first):
                    if not first:
                        dve.wait_ge(s_used, (i - 1) * HOT + s + 1)
                    t = i * HOT + s
                    dve.tensor_scalar(hot_lo[s][:, :], iota_f[:, 0:P], lo[:, bass.ds(t, 1)], None, ALU.is_equal).then_inc(s_hot, 1)
                    dve.tensor_scalar(hot_hi[s][:, :], iota_f[:, :], hi[:, bass.ds(t, 1)], None, ALU.is_equal).then_inc(s_hot, 1)
                for s in range(HOT):
                    hot(0, s, True)
                with dve.Fori(1, TILES // HOT) as i:
                    for s in range(HOT):
                        hot(i, s, False)
                dve.wait_ge(s_used, TILES)
                ch.link(dve.tensor_copy(keep["cnt"][:, :], count[:, 0:ROWS + 1]))
                dve.tensor_scalar(c1[:, :], keep["cnt"][:, :], 1.0, None, ALU.add).then_inc(s_c1, 1)
                ch.link(dve.tensor_scalar(keep["deg"][:, :], keep["cnt"][:, :], 1.0, None, ALU.max))
                ch.link(dve.reciprocal(keep["inv_deg"][:, :], keep["deg"][:, :]))
                dve.wait_ge(s_sq, 1)
                ch.link(dve.reciprocal(keep["dinv"][:, :], keep["sqrt_c1"][:, :]))
                base = ch.k
                per = Norm.STATS + Norm.SCALES

                def step(g):
                    c = Chain(dve, s_dve, base + g.num * per)
                    if g.live:
                        wait(dve, s_norm, g.num - 1)
                        ln_stats(nc, c, norm, g, lambda j: x_tile(keep, g, j)).then_inc(s_var, 1)
                        dve.wait_ge(s_std, g.num + 1)
                        ln_scales(nc, c, norm, g).then_inc(s_scale, 1)
                over_groups(dve, step)

            @block.scalar
            def _(act):
                act.wait_ge(s_c1, 1)
                act.activation(keep["sqrt_c1"][:, :], c1[:, :], ACT.Sqrt).then_inc(s_sq, 1)
                act.wait_ge(s_eps, 1)

                def step(g):
                    if g.live:
                        act.wait_ge(s_var, g.num + 1)
                        ln_sqrt(nc, norm, g, keep["eps"]).then_inc(s_std, 1)
                        act.wait_ge(s_scale, g.num + 1)
                        wait(act, s_store[g.slot], g.uses * 16)
                        ln_apply(nc, norm, g, ACT.Relu, lambda j: hout[g.slot][:, j, :],
                                 lambda j: x_tile(keep, g, j)).then_inc(s_norm, 1)
                over_groups(act, step)

            @block.sync
            def _(sp):
                def step(g):
                    if g.live:
                        sp.wait_ge(s_norm, g.num + 1)
                        sp.dma_start(group_rows(a["table"], g), group_buf(hout[g.slot], g)).then_inc(s_store[g.slot], 16)
                over_groups(sp, step)
                for s in range(2):
                    sp.wait_ge(s_store[s], 16 * ((GROUPS + 1) // 2))


def over_chunks(eng, step):
    for c in range(4):
        step(Chunk(0, c))
    with eng.Fori(0, (CHUNKS - 4) // 2) as i:
        step(Chunk(i, 4))
        step(Chunk(i, 5))
    for c in range(CHUNKS, CHUNKS + 2):
        step(Chunk(0, c))


def alone(eng, sem):
    eng.sem_inc(sem, 1)


def edge_stage(k, a, keep, layer):
    nc = k.nc
    k.stage = f"edges{layer}"
    by = 0 if layer == 0 else 1
    soft = layer == 3
    agg = a["agg0"] if layer == 0 else a["agg"]
    with ExitStack() as mem:
        def sb(name, shape, dt=F32):
            return mem.enter_context(nc.sbuf_tensor(f"{k.stage}_{name}_sb", shape, dt))

        def two(name, shape, dt=F32):
            return [sb(f"{name}{s}", shape, dt) for s in range(2)]

        gidx, sidx = two("gidx", [P, CT], I32), two("sidx", [P, CT], I32)
        rows = two("rows", [P, CT, D])
        same = two("same", [D, CW], BF16)
        sums = two("sums", [D, CW])
        back = two("back", [P, CT, D])
        turned = [mem.enter_context(nc.psum_tensor(f"{k.stage}_turned{s}_ps", [D, 1024], F32)) for s in range(2)]
        again = [mem.enter_context(nc.psum_tensor(f"{k.stage}_again{s}_ps", [P, 2, 512], F32)) for s in range(2)]
        BANK = 4
        if soft:
            most = sb("most", [D, CW + 1])
            logit = sb("logit", [D, CW])
            decay = sb("decay", [D, CW])
            ex = sb("ex", [D, CW])
            den, num = sb("den", [D, CW]), sb("num", [D, CW])
            carry = sb("carry", [D, 2])

        s_gidx, s_sidx, s_alone = k.sem("gidx"), k.sem("sidx"), k.sem("alone")
        s_gath, s_scat, s_same = k.dmas("gath"), k.dmas("scat"), k.dmas("same")
        s_rows, s_turned, s_sums, s_again, s_back = k.sem("rows"), k.sem("turned"), k.sem("sums"), k.sem("again"), k.sem("back")
        if soft:
            s_logit, s_arg, s_exp, s_dve, s_read = k.sem("logit"), k.sem("arg"), k.sem("exp"), k.sem("dve"), k.sem("read")

        with nc.Block() as block:
            @block.gpsimd
            def _(pool):
                def step(c):
                    if c.live:
                        s = c.slot
                        if layer == 0:
                            src = keep["payload"][:, c.tiles(), 0]
                        else:
                            src = keep["index"][:, 1, c.tiles()]
                        wait(pool, s_turned, c.num - 1)
                        pool.tensor_copy(gidx[s][:, :], src).then_inc(s_gidx, 1)
                        pool.wait_ge(s_gidx, c.num + 1)
                        alone(pool, s_alone)
                        for j in range(CT):
                            pool.indirect_dma_start(rows[s][:, j, :], None, a["table"],
                                                    bass.IndirectOffsetOnAxis(gidx[s][:, j:j + 1], 0)).then_inc(s_gath[s], 16)
                    c = c + -2
                    if c.live:
                        s = c.slot
                        wait(pool, s_scat[s], c.uses * (16 * CT))
                        pool.tensor_copy(sidx[s][:, :], keep["index"][:, 2 + by, c.tiles()]).then_inc(s_sidx, 1)
                        pool.wait_ge(s_sidx, c.num + 1)
                        pool.wait_ge(s_back, c.num + 1)
                        alone(pool, s_alone)
                        for j in range(CT):
                            pool.indirect_dma_start(agg, bass.IndirectOffsetOnAxis(sidx[s][:, j:j + 1], 0),
                                                    back[s][:, j, :], None, bounds_check=N - 1,
                                                    oob_is_err=False).then_inc(s_scat[s], 16)
                over_chunks(pool, step)
                for s in range(2):
                    pool.wait_ge(s_scat[s], 16 * CT * CHUNKS // 2)

            @block.sync
            def _(sp):
                def step(c):
                    if c.live:
                        wait(sp, s_sums, c.num - 1)
                        sp.dma_start(same[c.slot][:, :], a["same"][by:by + 1, bass.ds(c.num * CW, CW)].to_broadcast([D, CW])
                                     ).then_inc(s_same[c.slot], 16)
                over_chunks(sp, step)

            @block.tensor
            def _(pe):
                def step(c):
                    if c.live:
                        if layer == 0:
                            pe.wait_ge(s_rows, c.num + 1)
                        else:
                            pe.wait_ge(s_gath[c.slot], (c.uses + 1) * (16 * CT))
                        wait(pe, s_logit if soft else s_sums, c.num - 1)
                        for j in range(CT):
                            last = pe.transpose(turned[c.slot][:, j * P:(j + 1) * P], rows[c.slot][:, j, :], keep["ident"][:, :])
                        last.then_inc(s_turned, 1)
                    c = c + -1
                    if c.live:
                        pe.wait_ge(s_sums, c.num + 1)
                        wait(pe, s_back, c.num - 1)
                        for j in range(CT):
                            last = pe.transpose(again[c.slot][:, j // BANK, (j % BANK) * D:(j % BANK + 1) * D],
                                                sums[c.slot][:, j * P:(j + 1) * P], keep["ident"][0:D, 0:D])
                        last.then_inc(s_again, 1)
                over_chunks(pe, step)

            @block.scalar
            def _(act):
                def step(c):
                    if c.live and soft:
                        act.wait_ge(s_turned, c.num + 1)
                        wait(act, s_read, c.num)
                        act.activation(logit[:, :], turned[c.slot][:, 0:CW], ACT.Identity,
                                       bias=keep["eps"][0:D, 1:2]).then_inc(s_logit, 1)
                        act.wait_ge(s_arg, c.num * 2 + 1)
                        act.activation(ex[:, :], ex[:, :], ACT.Exp).then_inc(s_exp, 1)
                        act.wait_ge(s_arg, c.num * 2 + 2)
                        act.activation(decay[:, :], decay[:, :], ACT.Exp).then_inc(s_exp, 1)
                    c = c + -1
                    if c.live:
                        act.wait_ge(s_again, c.num + 1)
                        wait(act, s_scat[c.slot], c.uses * (16 * CT))
                        act.activation(back[c.slot][:, 0:BANK, :].rearrange("p j d -> p (j d)"),
                                       again[c.slot][:, 0, 0:BANK * D], ACT.Copy)
                        act.activation(back[c.slot][:, BANK:CT, :].rearrange("p j d -> p (j d)"),
                                       again[c.slot][:, 1, 0:(CT - BANK) * D], ACT.Copy).then_inc(s_back, 1)
                over_chunks(act, step)

            @block.vector
            def _(dve):
                if soft:
                    dve.memset(most[:, CW:CW + 1], 0.0).then_inc(s_dve, 1)
                    dve.memset(carry[:, :], 0.0).then_inc(s_dve, 1)

                def step(c):
                    if not c.live:
                        return
                    s = c.slot
                    if layer == 0:
                        dve.wait_ge(s_gath[s], (c.uses + 1) * (16 * CT))
                        weight = keep["payload"][:, c.tiles(), 1:2].bitcast(F32).to_broadcast([P, CT, D])
                        dve.tensor_tensor(rows[s][:, :, :], rows[s][:, :, :], weight, ALU.mult).then_inc(s_rows, 1)
                    dve.wait_ge(s_same[s], (c.uses + 1) * 16)
                    if not soft:
                        dve.wait_ge(s_turned, c.num + 1)
                        wait(dve, s_again, c.num - 1)
                        before = sums[1 - s][:, CW - 1:CW]
                        if c.known and c.num == 0:
                            before = 0.0
                        else:
                            dve.wait_ge(s_sums, c.num)
                        dve.tensor_tensor_scan(sums[s][:, :], same[s][:, :], turned[s][:, 0:CW], before,
                                               ALU.mult, ALU.add).then_inc(s_sums, 1)
                        return
                    per = 9
                    ch = Chain(dve, s_dve, c.num * per + 2)
                    ch.settle()
                    ch.link(dve.tensor_copy(most[:, 0:1], most[:, CW:CW + 1]))
                    dve.wait_ge(s_logit, c.num + 1)
                    ch.link(dve.tensor_tensor_scan(most[:, 1:CW + 1], same[s][:, :], logit[:, :], most[:, 0:1], ALU.mult, ALU.max))
                    dve.tensor_tensor(ex[:, :], logit[:, :], most[:, 1:CW + 1], ALU.subtract).then_inc(s_arg, 1)
                    ch.link(dve.tensor_tensor(decay[:, :], most[:, 0:CW], same[s][:, :], ALU.mult))
                    dve.tensor_tensor(decay[:, :], decay[:, :], most[:, 1:CW + 1], ALU.subtract).then_inc(s_arg, 1)
                    dve.wait_ge(s_exp, c.num * 2 + 1)
                    ch.note(dve.tensor_tensor(logit[:, :], logit[:, :], ex[:, :], ALU.mult))
                    dve.wait_ge(s_exp, c.num * 2 + 2)
                    ch.link(dve.tensor_tensor(decay[:, :], decay[:, :], same[s][:, :], ALU.mult))
                    ch.note(dve.tensor_tensor_scan(den[:, :], decay[:, :], ex[:, :], carry[:, 0:1], ALU.mult, ALU.add))
                    dve.tensor_tensor_scan(num[:, :], decay[:, :], logit[:, :], carry[:, 1:2], ALU.mult, ALU.add).then_inc(s_read, 1)
                    ch.settle()
                    ch.note(dve.tensor_copy(carry[:, 0:1], den[:, CW - 1:CW]))
                    dve.wait_ge(s_read, c.num + 1)
                    ch.note(dve.tensor_copy(carry[:, 1:2], num[:, CW - 1:CW]))
                    ch.settle()
                    ch.link(dve.reciprocal(den[:, :], den[:, :]))
                    wait(dve, s_again, c.num - 1)
                    dve.tensor_tensor(sums[s][:, :], num[:, :], den[:, :], ALU.mult).then_inc(s_sums, 1)
                    dve.wait_ge(s_sums, c.num + 1)
                    assert ch.k == per, ch.k
                over_chunks(dve, step)


def bcast(column, w):
    return column.unsqueeze(2).to_broadcast([P, w, D])


def node_cols(keep, name, g):
    return keep[name][:, g.tiles()]


def node_stage(k, a, keep, layer):
    nc = k.nc
    k.stage = f"nodes{layer}"
    final = layer == 3
    with ExitStack() as mem:
        def sb(name, shape, dt=F32):
            return mem.enter_context(nc.sbuf_tensor(f"{k.stage}_{name}_sb", shape, dt))

        def two(name, shape, dt=F32):
            return [sb(f"{name}{s}", shape, dt) for s in range(2)]

        K = D + 1
        weight = sb("weight", [K, D])
        slope = sb("slope", [P, 1])
        agg = two("agg", [P, G, K])
        own = two("own", [P, G, D]) if layer > 1 else None
        aggT = two("aggT", [K, 2, SUB * P])
        y = two("y", [P, G, D])
        neg = sb("neg", [P, G, D]) if layer == 2 else None
        hout = two("hout", [P, G, D]) if not final else y
        norm = Norm(sb, "norm")
        scale = two("scale", [P, 2, G]) if layer == 1 else None
        turned = [mem.enter_context(nc.psum_tensor(f"{k.stage}_turned{s}_ps", [P, 2, 512], F32)) for s in range(2)]
        prod = [mem.enter_context(nc.psum_tensor(f"{k.stage}_prod{s}_ps", [P, 2, 512], F32)) for s in range(2)]

        s_weight, s_ones, s_sum = k.dma("weight"), k.sem("ones"), k.sem("sum")
        s_agg, s_own, s_store = k.dmas("agg"), k.dmas("own"), k.dmas("store")
        s_turned, s_aggT, s_prod, s_y, s_x = k.sem("turned"), k.sem("aggT"), k.sem("prod"), k.sem("y"), k.sem("x")
        s_dve, s_var, s_std, s_scale, s_norm = k.sem("dve"), k.sem("var"), k.sem("std"), k.sem("scale"), k.sem("norm")
        s_in, s_act = k.sem("in"), k.sem("act")

        def halves(g):
            return [(u, u * SUB, min(SUB, g.w - u * SUB)) for u in range(2) if g.w > u * SUB]

        with nc.Block() as block:
            @block.sync
            def _(sp):
                sp.dma_start(weight[0:D, :], a[f"L{layer}_gnn_W"]).then_inc(s_weight, 16)
                sp.dma_start(weight[D:K, :], a[f"L{layer}_gnn_b"].rearrange("(a n) -> a n", a=1)).then_inc(s_weight, 16)
                if layer == 2:
                    sp.dma_start(slope[:, :], a["L2_gnn_prelu_a"].rearrange("(a n) -> a n", a=1).to_broadcast([P, 1])).then_inc(s_weight, 16)

                def load(g):
                    wait(sp, s_turned, g.num - 1)
                    rows = TAIL if g.tail else P
                    src = group_rows(a["agg"], g).rearrange("p (j d) -> p j d", d=D)
                    sp.dma_start(agg[g.slot][0:rows, 0:g.w, 0:D], src).then_inc(s_agg[g.slot], 16)
                    if own:
                        sp.dma_start(group_buf(own[g.slot], g), group_rows(a["table"], g)).then_inc(s_own[g.slot], 16)

                def step(g):
                    if (g + 3).live:
                        load(g + 3)
                    g = g + (-1 if final else -3)
                    if g.live:
                        sp.wait_ge(s_y if final else s_norm, g.num + 1)
                        sp.dma_start(group_rows(a["out"] if final else a["table"], g), group_buf(hout[g.slot], g)
                                     ).then_inc(s_store[g.slot], 16)
                over_groups(sp, step)
                for s in range(2):
                    sp.wait_ge(s_store[s], 16 * ((GROUPS + 1) // 2))

            @block.gpsimd
            def _(pool):
                if layer == 3:
                    for s in range(2):
                        pool.memset(agg[s][:, :, D:K], 1.0).then_inc(s_ones, 1)

                def factor(g):
                    if not g.live:
                        return
                    s, w = g.slot, g.w
                    if layer < 3:
                        wait(pool, s_turned, g.num - 1)
                        pool.tensor_copy(agg[s][:, 0:w, D], node_cols(keep, "cnt" if layer == 1 else "sqrt_c1", g)).then_inc(s_in, 1)
                    if own:
                        pool.wait_ge(s_agg[s], (g.uses + 1) * 16)
                        pool.wait_ge(s_own[s], (g.uses + 1) * 16)
                        pool.tensor_tensor(agg[s][:, 0:w, 0:D], agg[s][:, 0:w, 0:D], own[s][:, 0:w, :], ALU.add).then_inc(s_sum, 1)

                def step(g):
                    factor(g + 3)
                    g = g + -1
                    if g.live and not final:
                        pool.wait_ge(s_y, g.num + 1)
                        xs = keep["x"][:, g.cols()]
                        pool.tensor_tensor(xs, xs, y[g.slot][:, 0:g.w, :].rearrange("p j d -> p (j d)"), ALU.add).then_inc(s_x, 1)
                over_groups(pool, step)

            @block.tensor
            def _(pe):
                pe.wait_ge(s_weight, 48 if layer == 2 else 32)
                if layer == 3:
                    pe.wait_ge(s_ones, 2)

                def step(g):
                    n = g + 2
                    if n.live:
                        if layer < 3:
                            pe.wait_ge(s_in, n.num + 1)
                        if own:
                            pe.wait_ge(s_sum, n.num + 1)
                        else:
                            pe.wait_ge(s_agg[n.slot], (n.uses + 1) * 16)
                        wait(pe, s_aggT, n.num - 1)
                        for u, j0, m in halves(n):
                            for j in range(m):
                                last = pe.transpose(turned[n.slot][0:K, u, j * P:(j + 1) * P], agg[n.slot][:, j0 + j, :], keep["ident"][:, :])
                        last.then_inc(s_turned, 1)
                    if g.live:
                        pe.wait_ge(s_aggT, g.num + 1)
                        wait(pe, s_y, g.num - 1)
                        for u, j0, m in halves(g):
                            for j in range(m):
                                last = pe.matmul(prod[g.slot][:, u, j * D:(j + 1) * D], aggT[g.slot][:, u, j * P:(j + 1) * P],
                                                 weight[:, :], start=True, stop=True)
                        last.then_inc(s_prod, 1)
                over_groups(pe, step)

            @block.scalar
            def _(act):
                def step(g):
                    p = g + -3
                    if p.live and not final:
                        act.wait_ge(s_var, p.num + 1)
                        ln_sqrt(nc, norm, p, keep["eps"]).then_inc(s_std, 1)
                    n = g + 1
                    if n.live:
                        act.wait_ge(s_turned, n.num + 1)
                        wait(act, s_prod, n.num - 1)
                        if n.tail:
                            act.activation(aggT[n.slot][:, 0, 0:P], turned[n.slot][0:K, 0, 0:P], ACT.Copy).then_inc(s_aggT, 1)
                        else:
                            act.activation(aggT[n.slot][:, :, :], turned[n.slot][0:K, :, 0:SUB * P], ACT.Copy).then_inc(s_aggT, 1)
                    if p.live and not final:
                        act.wait_ge(s_scale, p.num + 1)
                        wait(act, s_store[p.slot], p.uses * 16)
                        ln_apply(nc, norm, p, ACT.Relu, lambda j: hout[p.slot][:, j, :], lambda j: x_tile(keep, p, j),
                                 factors=scale).then_inc(s_norm, 1)
                over_groups(act, step)

            @block.vector
            def _(dve):
                per = Norm.STATS + Norm.SCALES + (2 if layer == 1 else 0)

                def product(g):
                    c = Chain(dve, s_act, g.num * 3)
                    s, w = g.slot, g.w
                    dve.wait_ge(s_prod, g.num + 1)
                    if final:
                        wait(dve, s_store[s], g.uses * 16)
                    else:
                        wait(dve, s_x, g.num - 1)
                    xs = keep["x"][:, g.cols()].rearrange("p (j d) -> p j d", d=D)
                    cols = {1: "inv_deg", 2: "dinv"}.get(layer)
                    parts = halves(g)
                    for u, j0, m in parts:
                        pr = prod[s][:, u, 0:m * D].rearrange("p (j d) -> p j d", d=D)
                        out = y[s][:, j0:j0 + m, :]
                        if final:
                            ins = dve.tensor_tensor(out, pr, xs[:, j0:j0 + m, :], ALU.add)
                        else:
                            col = keep[cols][:, bass.ds(g.num * G + j0, m)]
                            ins = dve.tensor_tensor(out, pr, bcast(col, m), ALU.mult)
                        if layer == 2:
                            c.note(ins)
                    if layer == 2:
                        c.settle()
                        flat = y[s][:, 0:w, :].rearrange("p j d -> p (j d)")
                        below = neg[:, 0:w, :].rearrange("p j d -> p (j d)")
                        c.link(dve.tensor_scalar(below, flat, 0.0, slope[:, 0:1], ALU.min, ALU.mult))
                        ins = dve.scalar_tensor_tensor(flat, flat, 0.0, below, ALU.max, ALU.add)
                    ins.then_inc(s_y, 1)

                def step(g):
                    q = g + -3
                    if q.live and not final:
                        dve.wait_ge(s_std, q.num + 1)
                        c = Chain(dve, s_dve, q.num * per + Norm.STATS - (G - q.w))
                        ins = ln_scales(nc, c, norm, q)
                        if layer == 1:
                            c.link(ins)
                            dinv = node_cols(keep, "dinv", q)
                            st = norm.st[q.slot]
                            c.note(dve.tensor_tensor(scale[q.slot][:, 0, 0:q.w], st[:, Norm.RSTD, 0:q.w], dinv, ALU.mult))
                            c.settle()
                            ins = dve.tensor_tensor(scale[q.slot][:, 1, 0:q.w], st[:, Norm.SHIFT, 0:q.w], dinv, ALU.mult)
                        ins.then_inc(s_scale, 1)
                    if (g + -1).live:
                        product(g + -1)
                    p = g + -2
                    if p.live and not final:
                        dve.wait_ge(s_x, p.num + 1)
                        wait(dve, s_norm, p.num - 1)
                        c = Chain(dve, s_dve, p.num * per)
                        ln_stats(nc, c, norm, p, lambda j: x_tile(keep, p, j)).then_inc(s_var, 1)
                over_groups(dve, step)


def mlp_stage(k, a, keep):
    nc = k.nc
    k.stage = "mlp"
    with ExitStack() as mem:
        def sb(name, shape, dt=F32):
            return mem.enter_context(nc.sbuf_tensor(f"{k.stage}_{name}_sb", shape, dt))

        def two(name, shape, dt=F32):
            return [sb(f"{name}{s}", shape, dt) for s in range(2)]

        def ps(name, shape):
            return mem.enter_context(nc.psum_tensor(f"{k.stage}_{name}_ps", shape, F32))

        K = D + 2
        wh = sb("wh", [D, HID])
        wa = sb("wa", [K, HID])
        wo = sb("wo", [P, 2, D])
        rows = {n: sb(n, [P, D]) for n in ("bias", "gamma", "beta")}
        agg = two("agg", [P, G, K])
        h = two("h", [P, G, D])
        hb = two("hb", [P, G, D])
        aggT, hT = two("aggT", [K, SUB * P]), two("hT", [D, SUB * P])
        hid = two("hid", [P, 2, SUB * P])
        y = two("y", [P, G, D])
        hout = two("hout", [P, G, D])
        norm1, norm2 = Norm(sb, "norm1"), Norm(sb, "norm2")
        turned_a, turned_h, prod = ([ps(f"{n}{u}", [P, 512]) for u in range(2)] for n in ("ta", "th", "prod"))
        hidp = [ps(f"hidp{v}", [P, 512]) for v in range(2)]

        s_weight, s_rows, s_ones = k.dma("weight"), k.dma("rows"), k.sem("ones")
        s_agg, s_h, s_store = k.dmas("agg"), k.dmas("h"), k.dmas("store")
        s_div, s_deg, s_hb, s_turned, s_copied = k.sem("div"), k.sem("deg"), k.sem("hb"), k.sem("turned"), k.sem("copied")
        s_hidp, s_hid, s_prod, s_y, s_z, s_xb, s_x = (k.sem(n) for n in ("hidp", "hid", "prod", "y", "z", "xb", "x"))
        s_dve, s_var1, s_std1, s_scale1 = k.sem("dve"), k.sem("var1"), k.sem("std1"), k.sem("scale1")
        s_dve2, s_gamma, s_var2, s_std2, s_scale2, s_norm = k.sem("dve2"), k.sem("gamma"), k.sem("var2"), k.sem("std2"), k.sem("scale2"), k.sem("norm")

        def halves(g):
            return [(u, u * SUB, min(SUB, g.w - u * SUB)) for u in range(2) if g.w > u * SUB]

        def upto(g, u):
            return g.num * 2 + u + 1

        def last(g):
            return g.num * 2 + len(halves(g))

        with nc.Block() as block:
            @block.sync
            def _(sp):
                wm = a["L0_gnn_Wm1"]
                sp.dma_start(wh[:, :], wm[0:D, :]).then_inc(s_weight, 16)
                sp.dma_start(wa[0:D, :], wm[D:2 * D, :]).then_inc(s_weight, 16)
                sp.dma_start(wa[D:D + 1, :], a["L0_gnn_bm1"].rearrange("(a n) -> a n", a=1)).then_inc(s_weight, 16)
                sp.dma_start(wa[D + 1:K, :], wm[2 * D:2 * D + 1, :]).then_inc(s_weight, 16)
                sp.dma_start(wo[:, :, :], a["L0_gnn_Wm2"].rearrange("(v p) d -> p v d", p=P)).then_inc(s_weight, 16)
                for n, name in (("bias", "bm2"), ("gamma", "gamma"), ("beta", "beta")):
                    sp.dma_start(rows[n][:, :], a[f"L0_gnn_{name}"].rearrange("(a n) -> a n", a=1).to_broadcast([P, D])).then_inc(s_rows, 16)

                def load(g):
                    wait(sp, s_turned, (g.num - 1) * 2)
                    wait(sp, s_hb, g.num - 1)
                    part = TAIL if g.tail else P
                    src = group_rows(a["agg0"], g).rearrange("p (j d) -> p j d", d=D)
                    sp.dma_start(agg[g.slot][0:part, 0:g.w, 0:D], src).then_inc(s_agg[g.slot], 16)
                    sp.dma_start(group_buf(h[g.slot], g), group_rows(a["table"], g)).then_inc(s_h[g.slot], 16)

                def step(g):
                    if (g + 2).live:
                        load(g + 2)
                    n = g + -4
                    if n.live:
                        sp.wait_ge(s_norm, last(n))
                        sp.dma_start(group_rows(a["table"], n), group_buf(hout[n.slot], n)).then_inc(s_store[n.slot], 16)
                over_groups(sp, step)
                for s in range(2):
                    sp.wait_ge(s_store[s], 16 * ((GROUPS + 1) // 2))

            @block.gpsimd
            def _(pool):
                for s in range(2):
                    pool.memset(agg[s][:, :, D:D + 1], 1.0).then_inc(s_ones, 1)
                pool.wait_ge(s_rows, 48)

                def step(g):
                    if g.live:
                        s, w = g.slot, g.w
                        pool.wait_ge(s_h[s], (g.uses + 1) * 16)
                        wait(pool, s_y, (g.num - 1) * 2)
                        pool.tensor_tensor(hb[s][:, 0:w, :], h[s][:, 0:w, :], rows["bias"][:, :].unsqueeze(1).to_broadcast([P, w, D]),
                                           ALU.add).then_inc(s_hb, 1)
                    n = g + 2
                    if n.live:
                        wait(pool, s_turned, (n.num - 1) * 2)
                        pool.tensor_copy(agg[n.slot][:, 0:n.w, D + 1], node_cols(keep, "deg", n)).then_inc(s_deg, 1)
                    n = g + -2
                    if n.live:
                        xs = keep["x"][:, n.cols()].rearrange("p (j d) -> p j d", d=D)
                        pool.tensor_tensor(xs, xs, rows["beta"][:, :].unsqueeze(1).to_broadcast([P, n.w, D]), ALU.add).then_inc(s_xb, 1)
                over_groups(pool, step)

            @block.tensor
            def _(pe):
                pe.wait_ge(s_weight, 16 * 5)
                pe.wait_ge(s_ones, 2)

                def turn(n, u):
                    if u == 0:
                        pe.wait_ge(s_div, n.num + 1)
                        pe.wait_ge(s_deg, n.num + 1)
                        pe.wait_ge(s_h[n.slot], (n.uses + 1) * 16)
                    _, j0, m = halves(n)[u]
                    wait(pe, s_copied, (n.num - 1) * 2 + u + 1)
                    for j in range(m):
                        pe.transpose(turned_a[u][0:K, j * P:(j + 1) * P], agg[n.slot][:, j0 + j, :], keep["ident"][:, :])
                    for j in range(m):
                        ins = pe.transpose(turned_h[u][0:D, j * P:(j + 1) * P], h[n.slot][:, j0 + j, :], keep["ident"][:, :])
                    ins.then_inc(s_turned, 1)

                def step(g):
                    n = g + 1
                    for u in range(2):
                        mine = g.live and u < len(halves(g))
                        if mine:
                            _, j0, m = halves(g)[u]
                            pe.wait_ge(s_copied, upto(g, u))
                            for v in range(2):
                                wait(pe, s_hid, g.num * 4 + u * 2 + v - 1)
                                pe.matmul(hidp[v][:, 0:m * P], wh[:, v * P:(v + 1) * P], hT[u][:, 0:m * P], start=True, stop=False)
                                pe.matmul(hidp[v][:, 0:m * P], wa[:, v * P:(v + 1) * P], aggT[u][:, 0:m * P],
                                          start=False, stop=True).then_inc(s_hidp, 1)
                        if n.live and u < len(halves(n)):
                            turn(n, u)
                        if mine:
                            wait(pe, s_y, (g.num - 1) * 2 + u + 1)
                            pe.wait_ge(s_hid, g.num * 4 + u * 2 + 2)
                            for j in range(m):
                                for v in range(2):
                                    ins = pe.matmul(prod[u][:, j * D:(j + 1) * D], hid[u][:, v, j * P:(j + 1) * P],
                                                    wo[:, v, :], start=(v == 0), stop=(v == 1))
                            ins.then_inc(s_prod, 1)
                over_groups(pe, step)

            @block.scalar
            def _(act):
                def normed1(n, u):
                    if n.live and u < len(halves(n)):
                        _, j0, m = halves(n)[u]
                        act.wait_ge(s_scale1, n.num + 1)
                        ys = y[n.slot]
                        ln_apply(nc, norm1, n, ACT.Identity, lambda j: ys[:, j, :], lambda j: ys[:, j, :],
                                 tiles=range(j0, j0 + m)).then_inc(s_z, 1)

                def normed2(n, u):
                    if n.live and u < len(halves(n)):
                        _, j0, m = halves(n)[u]
                        act.wait_ge(s_scale2, n.num + 1)
                        wait(act, s_store[n.slot], n.uses * 16)
                        ln_apply(nc, norm2, n, ACT.Relu, lambda j: hout[n.slot][:, j, :], lambda j: x_tile(keep, n, j),
                                 tiles=range(j0, j0 + m)).then_inc(s_norm, 1)

                def step(g):
                    z, q = g + -2, g + -4
                    if z.live:
                        act.wait_ge(s_var1, z.num + 1)
                        ln_sqrt(nc, norm1, z, keep["eps"]).then_inc(s_std1, 1)
                    if q.live:
                        act.wait_ge(s_var2, q.num + 1)
                        ln_sqrt(nc, norm2, q, keep["eps"]).then_inc(s_std2, 1)
                    n = g + 1
                    for u in range(2):
                        if g.live and u < len(halves(g)):
                            m = halves(g)[u][2]
                            wait(act, s_prod, (g.num - 1) * 2 + u + 1)
                            for v in range(2):
                                act.wait_ge(s_hidp, g.num * 4 + u * 2 + v + 1)
                                act.activation(hid[u][:, v, 0:m * P], hidp[v][:, 0:m * P], ACT.Relu).then_inc(s_hid, 1)
                        normed1(z, u)
                        if n.live and u < len(halves(n)):
                            m = halves(n)[u][2]
                            act.wait_ge(s_turned, upto(n, u))
                            wait(act, s_hidp, (n.num - 1) * 4 + u * 2 + 2)
                            act.activation(aggT[u][:, 0:m * P], turned_a[u][0:K, 0:m * P], ACT.Copy)
                            act.activation(hT[u][:, 0:m * P], turned_h[u][0:D, 0:m * P], ACT.Copy).then_inc(s_copied, 1)
                        normed2(q, u)
                over_groups(act, step)

            @block.vector
            def _(dve):
                per = Norm.STATS + Norm.SCALES

                def step(g):
                    n = g + -3
                    if n.live:
                        s = n.slot
                        dve.wait_ge(s_z, last(n))
                        dve.wait_ge(s_xb, n.num + 1)
                        ys = y[s][:, 0:n.w, :]
                        dve.tensor_tensor(ys, ys, rows["gamma"][:, :].unsqueeze(1).to_broadcast([P, n.w, D]), ALU.mult).then_inc(s_gamma, 1)
                        dve.wait_ge(s_gamma, n.num + 1)
                        xs = keep["x"][:, n.cols()]
                        dve.tensor_tensor(xs, xs, ys.rearrange("p j d -> p (j d)"), ALU.add).then_inc(s_x, 1)
                    n = g + -1
                    if n.live:
                        s = n.slot
                        dve.wait_ge(s_prod, last(n))
                        dve.wait_ge(s_hb, n.num + 1)
                        wait(dve, s_x, n.num - 1)
                        for u, j0, m in halves(n):
                            dve.tensor_tensor(y[s][:, j0:j0 + m, :], prod[u][:, 0:m * D].rearrange("p (j d) -> p j d", d=D),
                                              hb[s][:, j0:j0 + m, :], ALU.add).then_inc(s_y, 1)
                    n = g + -2
                    if n.live:
                        dve.wait_ge(s_std1, n.num + 1)
                        c = Chain(dve, s_dve, n.num * per + Norm.STATS - (G - n.w))
                        ln_scales(nc, c, norm1, n).then_inc(s_scale1, 1)
                    n = g + -4
                    if n.live:
                        dve.wait_ge(s_std2, n.num + 1)
                        c = Chain(dve, s_dve2, n.num * per + Norm.STATS - (G - n.w))
                        ln_scales(nc, c, norm2, n).then_inc(s_scale2, 1)
                    n = g + -3
                    if n.live:
                        dve.wait_ge(s_x, n.num + 1)
                        wait(dve, s_norm, (n.num - 1) * 2)
                        c = Chain(dve, s_dve2, n.num * per)
                        ln_stats(nc, c, norm2, n, lambda j: x_tile(keep, n, j)).then_inc(s_var2, 1)
                    n = g + -1
                    if n.live:
                        dve.wait_ge(s_y, last(n))
                        c = Chain(dve, s_dve, n.num * per)
                        ln_stats(nc, c, norm1, n, lambda j: y[n.slot][:, j, :]).then_inc(s_var1, 1)
                    n = g + 2
                    if n.live:
                        dve.wait_ge(s_agg[n.slot], (n.uses + 1) * 16)
                        v = agg[n.slot][:, 0:n.w, 0:D]
                        dve.tensor_tensor(v, v, bcast(node_cols(keep, "inv_deg", n), n.w), ALU.mult).then_inc(s_div, 1)
                over_groups(dve, step)


class Chunk:

    def __init__(self, i, c):
        self.i, self.c = i, c
        self.known = isinstance(i, int)
        self.slot = c % 2
        self.num = 2 * i + c
        self.uses = i + c // 2
        self.live = not self.known or 0 <= self.num < CHUNKS

    def __add__(self, d):
        return Chunk(self.i, self.c + d)

    def tiles(self):
        return bass.ds(self.num * CT, CT)


_WEIGHTS = ["L0_gnn_W1", "L0_gnn_b1", "L0_gnn_W2", "L0_gnn_b2", "L0_gnn_Wm1", "L0_gnn_bm1", "L0_gnn_Wm2", "L0_gnn_bm2",
            "L0_gnn_gamma", "L0_gnn_beta", "L1_gnn_W", "L1_gnn_b", "L2_gnn_W", "L2_gnn_b", "L2_gnn_prelu_a",
            "L3_gnn_W", "L3_gnn_b"]


def build(nc, a):
    a = dict(a)
    for name, shape, dt in (("table", (N, D), F32), ("agg0", (N, D), F32), ("agg", (N, D), F32),
                            ("targets", (2, SORT + 2), I32), ("same", (2, SORT), BF16),
                            ("weights", (E,), F32), ("payload", ((E // COLS + 1) * COLS, 2), I32)):
        a[name] = nc.dram_tensor(name, shape, dt).ap()
    with ExitStack() as ctx:
        k = Kernel(nc)
        k.turn_points = turn_points()

        def sb(name, shape, dt=F32):
            return ctx.enter_context(nc.sbuf_tensor(f"{name}_keep", shape, dt))

        keep = {
            "x": sb("x_all", [P, (ROWS + 1) * D]),
            "ident": sb("ident", [P, P]),
            "index": sb("index", [P, 4, TILES], I32),
            "dst": sb("dst_sorted", [P, TILES]),
            "payload": sb("payload", [P, TILES, 2], I32),
            "eps": sb("eps", [P, 2]),
        }
        names = ("cnt", "deg", "inv_deg", "sqrt_c1", "dinv")
        keep["node"] = sb("node", [P, len(names), ROWS + 1])
        for n, name in enumerate(names):
            keep[name] = keep["node"][:, n, :]
        keep.update({
        })
        for stage in STAGES:
            stage(k, a, keep)
            k.end()


def edges(layer):
    return lambda k, a, keep: edge_stage(k, a, keep, layer)


def nodes(layer):
    return lambda k, a, keep: node_stage(k, a, keep, layer)


STAGES = [sort_stage, first_stage, edges(0), mlp_stage, edges(1), nodes(1), edges(2), nodes(2), edges(3), nodes(3)]


def kernel(**inputs):
    import numpy as _np
    import concourse.bacc as _bacc
    from concourse import mybir as _mybir
    from concourse.bass_utils import run_bass_kernel_spmd as _run

    nc = _bacc.Bacc("TRN2", target_bir_lowering=False, num_devices=1)
    pad = SORT - E
    laid = {
        "x": inputs["x"],
        "src": _np.concatenate([inputs["src"], _np.full(pad, SRC_PAD, _np.int32)]).reshape(P, COLS),
        "dst": _np.concatenate([inputs["dst"], _np.full(pad, DST_PAD, _np.int32)]).reshape(P, COLS),
        "edge_attr_T": _np.asarray(inputs["edge_attr_3"]).T,
    }
    laid.update({name: inputs[name] for name in _WEIGHTS})
    arrays, args = {}, {}
    for name, value in laid.items():
        value = _np.ascontiguousarray(value)
        arrays[f"in_{name}"] = value
        args[name] = nc.dram_tensor(f"in_{name}", value.shape, _mybir.dt.from_np(value.dtype), kind="ExternalInput").ap()
    args["out"] = nc.dram_tensor("out_0", (N, D), F32, kind="ExternalOutput").ap()
    build(nc, args)
    r = _run(nc, [arrays], core_ids=[0])
    return r.results[0]["out_0"]
```

```python
import concourse.bass as bass
from concourse import mybir
from contextlib import ExitStack

F32 = mybir.dt.float32
I32 = mybir.dt.int32
BF16 = mybir.dt.bfloat16
ALU = mybir.AluOpType
ACT = mybir.ActivationFunctionType

P = 128
N, D, E = 50000, 96, 25000
HID = 256
LN_EPS, MSG_EPS = 1e-5, 1e-7

ROWS = N // P
MAIN = P * ROWS
TAIL = N - MAIN
G = 6
SUB = 3
GROUPS = ROWS // G
assert ROWS % G == 0 and GROUPS % 2 == 1

SORT, COLS = 32768, 256
TILES = -(-E // P)
CT = 7
CHUNKS = TILES // CT
CW = CT * P
assert TILES % CT == 0 and CHUNKS % 2 == 0

SRC_OFF = 256
SRC_PAD = 65024 - SRC_OFF
DST_LOW = 32768 + 128
DST_HALF = 25000
DST_HIGH = 128 - DST_HALF
DST_PAD = 32512 - DST_HIGH
FILLS = 36
SKIP = 100000

UNIT, LOAD = 512, 6
UT = UNIT // P
UNITS = TILES // UT
LOADS = UNITS // LOAD
EDGES = UNITS * UNIT
assert LOADS * LOAD + 1 == UNITS and UT * UNITS == TILES and LOAD % 2 == 0
FEATS, PARTS = 3, 3
SPLIT = 32


class Group:

    def __init__(self, i, c):
        self.i, self.c = i, c
        self.known = isinstance(i, int)
        self.slot = c % 2
        self.num = 2 * i + c
        self.uses = i + c // 2
        self.live = not self.known or 0 <= self.num <= GROUPS
        self.tail = self.known and self.num == GROUPS
        self.w = 1 if self.tail else G

    def __add__(self, d):
        return Group(self.i, self.c + d)

    def tiles(self):
        return bass.ds(self.num * G, self.w)

    def cols(self):
        return bass.ds(self.num * G * D, self.w * D)


def wait(eng, sem, value):
    if not isinstance(value, int) or value > 0:
        eng.wait_ge(sem, value)


def over_groups(eng, step):
    for c in range(-3, 6):
        step(Group(0, c))
    with eng.Fori(0, (GROUPS - 9) // 2) as i:
        step(Group(i, 6))
        step(Group(i, 7))
    for c in range(GROUPS - 3, GROUPS + 6):
        step(Group(0, c))


class Chain:

    def __init__(self, eng, sem, base=0):
        self.eng, self.sem, self.base, self.k = eng, sem, base, 0

    def note(self, ins):
        ins.then_inc(self.sem, 1)
        self.k += 1

    def settle(self):
        self.eng.wait_ge(self.sem, self.base + self.k)

    def link(self, ins):
        self.note(ins)
        self.settle()


class Kernel:

    def __init__(self, nc):
        self.nc, self.stage, self.steps = nc, "", []

    def sem(self, name):
        self.steps.append(self.nc.alloc_semaphore(f"{self.stage}_{name}"))
        return self.steps[-1]

    def dma(self, name):
        return self.nc.alloc_semaphore(f"{self.stage}_{name}")

    def dmas(self, name):
        return [self.dma(f"{name}{s}") for s in range(2)]

    def end(self):
        self.nc.clear_and_free_semaphores(self.steps)
        self.nc.all_engine_barrier()
        self.steps = []


def group_rows(dram, g):
    if g.tail:
        return dram[MAIN:N, :]
    return dram[0:MAIN, :].rearrange("(p j) d -> p (j d)", p=P)[:, g.cols()]


def group_buf(buf, g):
    rows = TAIL if g.tail else P
    return buf[0:rows, 0:g.w, :].rearrange("p j d -> p (j d)")


def zero_fill(eng, keep, agg):
    flat = agg[0:MAIN, :].rearrange("(p j) d -> p (j d)", p=P)
    w = keep["zeros"].shape[1]
    sems = keep["zfill"]
    for n in range(FILLS):
        keep["zfills"] += 1
        if keep["zfills"] > 2:
            eng.wait_ge(sems[keep["zfills"] % 2], 16 * ((keep["zfills"] - 1) // 2))
        eng.dma_start(flat[:, n * w:(n + 1) * w], keep["zeros"][:, :]).then_inc(sems[keep["zfills"] % 2], 16)
    eng.dma_start(agg[MAIN:N, :], keep["zeros"][0:TAIL, 0:D]).then_inc(keep["zfill_tail"], 16)


def sort_stage(k, a, keep):
    nc = k.nc
    k.stage = "sort"
    with ExitStack() as mem:
        def sb(name, shape, dt=F32):
            return mem.enter_context(nc.sbuf_tensor(f"{k.stage}_{name}_sb", shape, dt))

        def ps(name, shape):
            return mem.enter_context(nc.psum_tensor(f"{k.stage}_{name}_ps", shape, F32))

        ends = sb("ends", [P, 2, COLS], I32)
        keys = [sb(f"keys{b}", [P, 2, COLS]) for b in range(2)]
        place = sb("place", [P, COLS], I32)
        part_i = sb("part_i", [P, 1], I32)
        sign = sb("sign", [P, 1])
        tmp = sb("tmp", [P, COLS], I32)
        tgt = sb("tgt", [P, 2, COLS], I32)
        nxt = sb("nxt", [P, 2, COLS], I32)
        prv = sb("prv", [P, 2, COLS], I32)
        same = sb("same", [P, 2, COLS], BF16)
        none = sb("none", [2, 2], I32)
        K = PARTS * PARTS * FEATS + PARTS
        assert FEATS == PARTS
        hid = sb("hid", [P, 2, UT * HID])
        cut = EDGES // SPLIT
        early = {n: keep[n][:, :, :].rearrange("p a b -> p (a b)") for n in ("node", "index", "payload")}
        attr, rest = (hid[0:FEATS * SPLIT, s, 0:cut] for s in range(2))
        words = (PARTS + 1) * cut // 2
        parts = early["node"][0:FEATS * SPLIT, 0:words].bitcast(BF16).rearrange("p (i n) -> p i n", i=PARTS + 1)
        wb = early["node"][0:FEATS + 1, words:words + HID]
        wb_rest = early["index"][0:FEATS + 1, 0:HID].bitcast(F32)
        wb_parts = early["payload"][0:FEATS + 1, 0:PARTS * HID // 2].bitcast(BF16).rearrange("p (i n) -> p i n", i=PARTS)
        feat = sb("feat", [K, 2, (LOAD + 1) * UNIT], BF16)
        w1 = sb("w1", [K, HID], BF16)
        w2 = sb("w2", [P, HID])
        b2 = sb("b2", [P, 1])
        wcol = sb("wcol", [P, TILES])
        fidx = hid[:, :, :].rearrange("p s n -> p (s n)")[:, 0:5 * COLS].rearrange("p (n f) -> p n f", f=COLS)
        HALF = TILES // 2
        dst_q = sb("dst_q", [HALF, 2, P], I32)
        pay = sb("pay", [HALF, 2, P, 2], I32)
        turn = ps("turn", [P, 2, 2, P])
        turn2 = ps("turn2", [P, 2, 2, P])
        turn3 = ps("turn3", [P, 2, 2, P])
        psh = [ps(f"psh{s}", [P, UT * HID]) for s in range(2)]

        s_ends, s_x, s_zero, s_xtail = k.dma("ends"), k.dmas("x"), k.sem("zero"), k.sem("xtail")
        s_const, s_key, s_ident, s_turn = k.sem("const"), k.sem("key"), k.sem("ident"), k.sem("turned")
        s_tgt, s_near, s_same, s_none, s_pad = k.sem("tgt"), k.dma("near"), k.sem("same"), k.sem("none"), k.dma("pad")
        s_fidx, s_store, s_ones = k.sem("fidx"), k.dma("store"), k.sem("ones")
        s_attr, s_wb, s_weights, s_dstq = k.dma("attr"), k.dma("wb"), k.dma("weights"), k.dma("dstq")
        s_part, s_left = k.sem("part"), k.sem("left")
        s_wparts, s_w1, s_parts, s_feat = k.dma("wparts"), k.dma("w1"), k.dma("parts"), k.dmas("feat")
        s_hid, s_relu, s_mul, s_sum, s_wcol, s_wturn = (k.sem(n) for n in ("hid", "relu", "mul", "sum", "wcol", "wturn"))
        s_pay, s_payst = k.sem("pay"), k.dma("payst")

        LEVELS = 15

        def first_unit(n):
            return n * LOAD + (n > 0)

        def feat_load(eng, n):
            cols = slice(first_unit(n) * UNIT, first_unit(n + 1) * UNIT)
            eng.dma_start(feat[:, n % 2, 0:cols.stop - cols.start], a["feat_parts"][:, cols]).then_inc(s_feat[n % 2], 16)

        def over_pairs(eng, first, pairs, unit):
            if pairs == 1:
                unit(first, 1)
                unit(first + 1, 0)
            else:
                with eng.Fori(0, pairs) as i:
                    unit(2 * i + first, 1)
                    unit(2 * i + (first + 1), 0)

        with nc.Block() as block:
            @block.sync
            def _(sp):
                sp.dma_start(ends[:, 0, :], a["src"]).then_inc(s_ends, 16)
                sp.dma_start(ends[:, 1, :], a["dst"]).then_inc(s_ends, 16)
                sp.dma_start(wb[0:FEATS, :], a["L0_gnn_W1"]).then_inc(s_wb, 16)
                sp.dma_start(wb[FEATS:FEATS + 1, :], a["L0_gnn_b1"].rearrange("(a n) -> a n", a=1)).then_inc(s_wb, 16)
                sp.dma_start(attr[:, :], a["edge_attr_T"].rearrange("f (q n) -> (f q) n", q=SPLIT)).then_inc(s_attr, 16)
                sp.dma_start(w2[:, :], a["L0_gnn_W2"].rearrange("p n -> n p").to_broadcast([P, HID])).then_inc(s_weights, 16)
                sp.dma_start(b2[:, :], a["L0_gnn_b2"].rearrange("(a n) -> a n", a=1).to_broadcast([P, 1])).then_inc(s_weights, 16)
                sp.dma_start(dst_q[:, :, :], a["dst"].rearrange("p f -> (p f)")[0:EDGES]
                             .rearrange("(h q c) -> q h c", q=HALF, c=P)).then_inc(s_dstq, 16)
                sp.wait_ge(s_ones, 1)
                ones = PARTS * PARTS * FEATS
                sp.dma_start(a["feat_parts"][ones:K, :].rearrange("f (q n) -> (f q) n", q=SPLIT), parts[:, PARTS, :]).then_inc(s_parts, 16)
                for i in range(PARTS):
                    sp.wait_ge(s_part, 2 * i + 1)
                    for j in range(PARTS):
                        row = (i * PARTS + j) * FEATS
                        sp.dma_start(a["feat_parts"][row:row + FEATS, :].rearrange("f (q n) -> (f q) n", q=SPLIT),
                                     parts[:, i, :]).then_inc(s_parts, 16)
                sp.wait_ge(s_parts, 16 * (PARTS * PARTS + 1))
                feat_load(sp, 0)
                feat_load(sp, 1)
                step = ROWS // 10
                for n in range(10):
                    if n >= 2:
                        sp.wait_ge(s_x[n % 2], 16 * (n // 2))
                    sp.dma_start(keep["x"][:, n * step * D:(n + 1) * step * D],
                                 a["x"][0:MAIN, :].rearrange("(p j) d -> p (j d)", p=P)[:, n * step * D:(n + 1) * step * D]
                                 ).then_inc(s_x[n % 2], 16)
                sp.wait_ge(s_xtail, 1)
                sp.dma_start(keep["x"][0:TAIL, ROWS * D:(ROWS + 1) * D], a["x"][MAIN:N, :]).then_inc(s_x[0], 16)
                sp.wait_ge(s_none, 1)
                for n in range(2):
                    for at in (0, SORT + 1):
                        sp.dma_start(a["targets"][n:n + 1, at:at + 1], none[0:1, 0:1]).then_inc(s_pad, 16)
                sp.wait_ge(s_zero, 1)
                zero_fill(sp, keep, a["agg0"])
                sp.wait_ge(s_tgt, 2)
                for n in range(2):
                    sp.dma_start(a["targets"][n, 1:SORT + 1].rearrange("(p f) -> p f", f=COLS),
                                 tgt[:, n, :]).then_inc(s_pad, 16)
                sp.wait_ge(s_pad, 16 * 6)
                for n in range(2):
                    sp.dma_start(nxt[:, n, :], a["targets"][n, 2:SORT + 2].rearrange("(p f) -> p f", f=COLS)).then_inc(s_near, 16)
                    sp.dma_start(prv[:, n, :], a["targets"][n, 0:SORT].rearrange("(p f) -> p f", f=COLS)).then_inc(s_near, 16)
                sp.wait_ge(s_same, 1)
                for n in range(2):
                    sp.dma_start(a["same"][n, :].rearrange("(p f) -> p f", f=COLS), same[:, n, :]).then_inc(s_store, 16)
                for s in range(2):
                    sp.wait_ge(s_x[s], 16 * (5 + (s == 0)))
                sp.wait_ge(s_store, 32)

            @block.gpsimd
            def _(pool):
                pool.iota(place[:, :], pattern=[[1, COLS]], base=0, channel_multiplier=COLS).then_inc(s_const, 1)
                pool.iota(part_i[:, :], pattern=[[0, 1]], base=0, channel_multiplier=1).then_inc(s_const, 1)
                pool.memset(parts[:, PARTS, :], 1.0).then_inc(s_ones, 1)
                for i in range(1, PARTS):
                    for n, (whole, left, part) in enumerate(((attr, rest, parts), (wb, wb_rest, wb_parts))):
                        pool.wait_ge(s_part, 2 * i - 1 + n)
                        pool.tensor_tensor(left, whole if i == 1 else left, part[:, i - 1, :], ALU.subtract).then_inc(s_left, 1)
                pool.memset(keep["ident"][:, :], 0.0).then_inc(s_ident, 1)
                pool.wait_ge(s_ident, 1)
                pool.affine_select(out=keep["ident"][:, :], in_=keep["ident"][:, :], compare_op=ALU.not_equal,
                                   fill=1.0, base=0, pattern=[[-1, P]], channel_multiplier=1).then_inc(s_ident, 1)
                pool.memset(keep["x"][:, ROWS * D:(ROWS + 1) * D], 0.0).then_inc(s_xtail, 1)
                pool.memset(keep["zeros"][:, :], 0.0).then_inc(s_zero, 1)
                pool.memset(none[:, :], -1).then_inc(s_none, 1)
                pool.wait_ge(s_dstq, 16)
                pool.tensor_copy(pay[:, :, :, 0], dst_q[:, :, :]).then_inc(s_pay, 1)
                pool.wait_ge(s_weights, 32)

                def unit(m, s):
                    pool.wait_ge(s_relu, m + 1)
                    v = hid[:, s, :].rearrange("p (q n) -> p q n", n=HID)
                    pool.tensor_tensor(v, v, w2[:, :].unsqueeze(1).to_broadcast([P, UT, HID]), ALU.mult).then_inc(s_mul, 1)
                unit(0, 0)
                over_pairs(pool, 1, UNITS // 2, unit)
                pool.wait_ge(s_pay, 2)
                pool.dma_start(a["payload"][:, :].rearrange("(h q c) two -> q h (c two)", q=HALF, c=P),
                               pay[:, :, :, :].rearrange("q h c two -> q h (c two)")).then_inc(s_payst, 16)
                pool.wait_ge(s_payst, 16)

            @block.tensor
            def _(pe):
                pe.wait_ge(s_ident, 2)

                def turns(cur, dst):
                    pe.wait_ge(s_key, cur)
                    for arr in range(2):
                        for h in range(2):
                            last = pe.transpose(turn[:, arr, h, :], dst[:, arr, h * P:(h + 1) * P], keep["ident"][:, :])
                    last.then_inc(s_turn, 1)

                def units(n, first, pairs, unit0=False):
                    pe.wait_ge(s_feat[n % 2], 16 * (n // 2 + 1))

                    def unit(m, s):
                        wait(pe, s_relu, m - 1)
                        for q in range(UT):
                            at = (m - first_unit(n)) * UNIT + q * P
                            last = pe.matmul(psh[s][:, q * HID:(q + 1) * HID], feat[:, n % 2, bass.ds(at, P)], w1[:, :],
                                             start=True, stop=True)
                        last.then_inc(s_hid, 1)
                    if unit0:
                        unit(0, 0)
                    over_pairs(pe, first, pairs, unit)

                pe.wait_ge(s_w1, 16 * (PARTS + 1))
                units(0, 1, LOAD // 2, unit0=True)
                for t, (cur, b) in enumerate(k.turn_points):
                    turns(cur, keys[b])
                    n = 1 + t // 2
                    if t % 2 == 0:
                        units(n, first_unit(n), 1)
                    else:
                        units(n, first_unit(n) + 2, LOAD // 2 - 1)
                pe.wait_ge(s_wcol, 1)
                for h in range(2):
                    last = pe.transpose(turn3[0:HALF, 0, h, :], wcol[:, h * HALF:(h + 1) * HALF], keep["ident"][:, :])
                last.then_inc(s_wturn, 1)
                for n in range(5):
                    pe.wait_ge(s_fidx, n + 1)
                    if n == 4:
                        pe.wait_ge(s_pay, 2)
                    for h in range(2):
                        bank = (turn, turn2, turn3)[n // 2]
                        last = pe.transpose(bank[:, n % 2, h, :], fidx[:, n, h * P:(h + 1) * P], keep["ident"][:, :])
                last.then_inc(s_turn, 1)

            @block.scalar
            def _(act):
                act.wait_ge(s_attr, 16)
                act.wait_ge(s_wb, 32)
                for i in range(PARTS):
                    for n, (whole, left, part) in enumerate(((attr, rest, parts), (wb, wb_rest, wb_parts))):
                        wait(act, s_left, 2 * i - 1 + n if i > 0 else 0)
                        act.activation(part[:, i, :], left if i > 0 else whole, ACT.Copy).then_inc(s_part, 1)
                act.wait_ge(s_part, 2 * PARTS)
                for j in range(PARTS):
                    act.dma_start(a["w1_parts"][j * FEATS:(j + 1) * FEATS, :], wb_parts[0:FEATS, j, :]).then_inc(s_wparts, 16)
                    act.dma_start(a["b1_parts"][j:j + 1, :], wb_parts[FEATS:FEATS + 1, j, :]).then_inc(s_wparts, 16)
                act.wait_ge(s_wparts, 16 * 2 * PARTS)
                rows = PARTS * FEATS
                for i in range(PARTS):
                    act.dma_start(w1[i * rows:(i + 1) * rows, :], a["w1_parts"]).then_inc(s_w1, 16)
                act.dma_start(w1[PARTS * rows:K, :], a["b1_parts"]).then_inc(s_w1, 16)

                def sums(m, s):
                    act.wait_ge(s_mul, m + 1)
                    for q in range(UT):
                        v = hid[:, s, q * HID:(q + 1) * HID]
                        act.activation(v, v, ACT.Copy, accum_out=wcol[:, bass.ds(m * UT + q, 1)]).then_inc(s_sum, 1)

                def unit(m, s):
                    if not isinstance(m, int) or m >= 2:
                        sums(m - 2, s)
                        act.wait_ge(s_sum, (m - 1) * UT)
                    act.wait_ge(s_hid, m + 1)
                    act.activation(hid[:, s, :], psh[s][:, :], ACT.Relu).then_inc(s_relu, 1)
                unit(0, 0)
                unit(1, 1)
                unit(2, 0)
                over_pairs(act, 3, LOAD // 2 - 1, unit)
                for n in range(1, LOADS):
                    if n < LOADS - 1:
                        act.wait_ge(s_hid, first_unit(n))
                        feat_load(act, n + 1)
                    over_pairs(act, first_unit(n), LOAD // 2, unit)
                sums(UNITS - 2, 1)
                sums(UNITS - 1, 0)
                act.wait_ge(s_sum, TILES)
                act.activation(wcol[:, :], wcol[:, :], ACT.Sigmoid, bias=b2[:, 0:1]).then_inc(s_wcol, 1)
                act.wait_ge(s_wturn, 1)
                act.activation(pay[:, :, :, 1].bitcast(F32), turn3[0:HALF, 0, :, :], ACT.Copy).then_inc(s_pay, 1)

            @block.vector
            def _(dve):
                ch = [0]

                def link(ins):
                    ch[0] += 1
                    ins.then_inc(s_key, 1)

                def settle():
                    dve.wait_ge(s_key, ch[0])

                dve.wait_ge(s_ends, 32)
                dve.wait_ge(s_const, 2)
                ki = [b[:, :, :].bitcast(I32) for b in keys]
                link(dve.tensor_scalar(tmp[:, :], ends[:, 0, :], float(SRC_OFF), None, ALU.add))
                link(dve.tensor_scalar(nxt[:, 1, :], ends[:, 1, :], float(DST_HALF), float(DST_HIGH - DST_LOW), ALU.is_ge, ALU.mult))
                link(dve.tensor_scalar(part_i[:, :], part_i[:, :], 1, None, ALU.bitwise_and))
                settle()
                link(dve.tensor_scalar(nxt[:, 0, :], tmp[:, :], 15, None, ALU.logical_shift_left))
                link(dve.scalar_tensor_tensor(prv[:, 1, :], ends[:, 1, :], float(DST_LOW), nxt[:, 1, :], ALU.add, ALU.add))
                link(dve.tensor_scalar(sign[:, :], part_i[:, :], -2.0, 1.0, ALU.mult, ALU.add))
                settle()
                link(dve.tensor_tensor(ki[0][:, 0, :], nxt[:, 0, :], place[:, :], ALU.bitwise_or))
                link(dve.tensor_scalar(prv[:, 0, :], prv[:, 1, :], 16, None, ALU.logical_shift_left))
                settle()
                link(dve.tensor_tensor(ki[0][:, 1, :], prv[:, 0, :], ends[:, 0, :], ALU.bitwise_or))
                settle()
                cur = 0

                def compare(cur, d):
                    x = keys[cur][:, :, :].rearrange("p a (b t k) -> p (a b) t k", t=2, k=d)
                    y = keys[1 - cur][:, :, :].rearrange("p a (b t k) -> p (a b) t k", t=2, k=d)
                    link(dve.tensor_tensor(y[:, :, 0, :], x[:, :, 0, :], x[:, :, 1, :], ALU.min))
                    link(dve.tensor_tensor(y[:, :, 1, :], x[:, :, 0, :], x[:, :, 1, :], ALU.max))
                    settle()
                    return 1 - cur

                def negate(cur, width, lo, hi):
                    v = keys[cur][:, :, :].rearrange("p a (b m) -> p (a b) m", m=width)[:, :, lo:hi]
                    link(dve.tensor_scalar(v, v, -1.0, None, ALU.mult))
                    settle()

                points = []

                def turn_over(cur):
                    points.append((ch[0], cur))
                    dve.wait_ge(s_turn, len(points))
                    link(dve.tensor_copy(keys[1 - cur][:, :, :], turn[:, :, :, :].rearrange("p a h m -> p a (h m)")))
                    settle()
                    return 1 - cur

                for m in range(1, LEVELS + 1):
                    if m == 1:
                        negate(cur, 4, 2, 4)
                    elif m <= 7:
                        negate(cur, 2 << m, 1 << (m - 1), 3 << (m - 1))
                    elif m == 8:
                        for f0, sg in ((0, 1.0), (P, -1.0)):
                            v = keys[cur][:, :, f0:f0 + P]
                            link(dve.tensor_scalar(v, v, sign[:, 0:1], sg, ALU.mult, ALU.mult))
                        settle()
                    if m <= 8:
                        for j in reversed(range(m)):
                            cur = compare(cur, 1 << j)
                        continue
                    cur = turn_over(cur)
                    if m < LEVELS:
                        negate(cur, 2 << (m - 8), 1 << (m - 9), 3 << (m - 9))
                    else:
                        negate(cur, P, P // 2, P)
                    for j in reversed(range(8, m)):
                        cur = compare(cur, 1 << (j - 8))
                    cur = turn_over(cur)
                    for j in reversed(range(8)):
                        cur = compare(cur, 1 << j)
                assert points == k.turn_points, points

                v = ki[cur]
                fr = ki[1 - cur]
                link(dve.tensor_scalar(tmp[:, :], v[:, 0, :], 15, None, ALU.logical_shift_right))
                link(dve.tensor_scalar(fr[:, 1, :], v[:, 1, :], 16, None, ALU.logical_shift_right))
                link(dve.tensor_scalar(fr[:, 0, :], v[:, 0, :], (1 << 15) - 1, None, ALU.bitwise_and))
                settle()
                dve.tensor_scalar(tgt[:, 0, :], tmp[:, :], float(-SRC_OFF), None, ALU.add).then_inc(s_tgt, 1)
                dve.wait_ge(s_sum, TILES)
                link(dve.tensor_scalar(nxt[:, 1, :], fr[:, 1, :], 32768.0, float(DST_HIGH - DST_LOW), ALU.is_ge, ALU.mult))
                dve.tensor_scalar(fidx[:, 0, :], fr[:, 0, :], float(E - 1), None, ALU.min).then_inc(s_fidx, 1)
                settle()
                dve.scalar_tensor_tensor(tgt[:, 1, :], fr[:, 1, :], float(-DST_HIGH), nxt[:, 1, :], ALU.add, ALU.add).then_inc(s_tgt, 1)
                dve.wait_ge(s_fidx, 1)
                link(dve.tensor_scalar(fr[:, 0, :], v[:, 1, :], (1 << 16) - 1, None, ALU.bitwise_and))
                settle()
                dve.wait_ge(s_tgt, 2)
                dve.tensor_scalar(fidx[:, 1, :], fr[:, 0, :], float(N - 1), None, ALU.min).then_inc(s_fidx, 1)
                dve.wait_ge(s_near, 64)
                dve.tensor_tensor(same[:, :, :], tgt[:, :, :], prv[:, :, :], ALU.is_equal).then_inc(s_same, 1)
                dve.wait_ge(s_same, 1)
                link(dve.tensor_tensor(prv[:, :, :], tgt[:, :, :], nxt[:, :, :], ALU.is_equal))
                settle()
                for n in range(2):
                    dve.scalar_tensor_tensor(fidx[:, 2 + n, :], prv[:, n, :], float(SKIP), tgt[:, n, :],
                                             ALU.mult, ALU.add).then_inc(s_fidx, 1)
                dve.tensor_copy(fidx[:, 4, :], tgt[:, 1, :]).then_inc(s_fidx, 1)
                dve.wait_ge(s_turn, len(points) + 1)
                half = TILES // 2
                for n in range(5):
                    bank = (turn, turn2, turn3)[n // 2]
                    out = keep["index"][:, n, :] if n < 4 else keep["dst"][:, :]
                    for h in range(2):
                        dve.tensor_copy(out[:, h:TILES:2], bank[:, n % 2, h, 0:half]).then_inc(s_fidx, 1)


def turn_points():
    out, ch, cur = [], 9, 0
    for m in range(1, 16):
        if m <= 7:
            ch += 1
        elif m == 8:
            ch += 2
        if m <= 8:
            ch += 2 * m
            cur ^= m & 1
            continue
        out.append((ch, cur))
        ch, cur = ch + 2 + 2 * (m - 8), cur ^ 1 ^ (m & 1)
        out.append((ch, cur))
        ch, cur = ch + 1 + 16, cur ^ 1
    return out


class Norm:

    SUM, DIFF, SQ, M2, VAR, STD, RSTD, SHIFT = range(8)
    STATS = G + 4
    SCALES = 1

    def __init__(self, sb, name):
        self.bn = [sb(f"{name}_bn{s}", [P, G, 6]) for s in range(2)]
        self.st = [sb(f"{name}_st{s}", [P, 8, G]) for s in range(2)]


def ln_stats(nc, ch, norm, g, tile):
    bn, st, w = norm.bn[g.slot], norm.st[g.slot], g.w
    for j in range(w):
        ch.note(nc.vector.bn_stats(bn[:, j, :], tile(j)))
    ch.settle()
    ch.note(nc.vector.tensor_tensor(st[:, norm.SUM, 0:w], bn[:, 0:w, 1], bn[:, 0:w, 4], ALU.add))
    ch.note(nc.vector.tensor_tensor(st[:, norm.DIFF, 0:w], bn[:, 0:w, 1], bn[:, 0:w, 4], ALU.subtract))
    ch.note(nc.vector.tensor_tensor(st[:, norm.M2, 0:w], bn[:, 0:w, 2], bn[:, 0:w, 5], ALU.add))
    ch.settle()
    ch.link(nc.vector.tensor_tensor(st[:, norm.SQ, 0:w], st[:, norm.DIFF, 0:w], st[:, norm.DIFF, 0:w], ALU.mult))
    return nc.vector.scalar_tensor_tensor(st[:, norm.VAR, 0:w], st[:, norm.SQ, 0:w], D / 4, st[:, norm.M2, 0:w],
                                          ALU.mult, ALU.add)


def ln_sqrt(nc, norm, g, eps):
    st, w = norm.st[g.slot], g.w
    return nc.scalar.activation(st[:, norm.STD, 0:w], st[:, norm.VAR, 0:w], ACT.Sqrt, bias=eps[:, 0:1], scale=1.0 / D)


def ln_scales(nc, ch, norm, g):
    st, w = norm.st[g.slot], g.w
    ch.link(nc.vector.reciprocal(st[:, norm.RSTD, 0:w], st[:, norm.STD, 0:w]))
    return nc.vector.scalar_tensor_tensor(st[:, norm.SHIFT, 0:w], st[:, norm.SUM, 0:w], -0.5, st[:, norm.RSTD, 0:w],
                                          ALU.mult, ALU.mult)


def ln_apply(nc, norm, g, func, out, tile, factors=None, tiles=None):
    st = norm.st[g.slot]
    by, add = (st[:, norm.RSTD, :], st[:, norm.SHIFT, :]) if factors is None else (factors[g.slot][:, 0, :], factors[g.slot][:, 1, :])
    for j in range(g.w) if tiles is None else tiles:
        last = nc.scalar.activation(out(j), tile(j), func, bias=add[:, j:j + 1], scale=by[:, j:j + 1])
    return last


def x_tile(keep, g, j):
    return keep["x"][:, bass.ds(g.num * (G * D) + j * D, D)]


def first_stage(k, a, keep):
    nc = k.nc
    k.stage = "first"
    with ExitStack() as mem:
        def sb(name, shape, dt=F32):
            return mem.enter_context(nc.sbuf_tensor(f"{k.stage}_{name}_sb", shape, dt))

        gidx = [sb(f"gidx{s}", [P, CT], I32) for s in range(2)]
        gbuf = [sb(f"gbuf{s}", [P, CT, 2], I32) for s in range(2)]
        iota_i = sb("iota_i", [P, ROWS + 1], I32)
        iota_f = sb("iota_f", [P, ROWS + 1])
        hi, lo, t0, t1 = (sb(n, [P, TILES]) for n in ("hi", "lo", "t0", "t1"))
        HOT = 4
        hot_lo = [sb(f"hot_lo{s}", [P, P], BF16) for s in range(HOT)]
        hot_hi = [sb(f"hot_hi{s}", [P, ROWS + 1], BF16) for s in range(HOT)]
        c1 = sb("c1", [P, ROWS + 1])
        norm = Norm(sb, "norm")
        hout = [sb(f"hout{s}", [P, G, D]) for s in range(2)]
        count = mem.enter_context(nc.psum_tensor("first_count_ps", [P, 512], F32))

        s_idx, s_out, s_alone = k.sem("idx"), k.sem("out"), k.sem("alone")
        s_gath = k.dmas("gath")
        s_iota, s_hot, s_used = k.sem("iota"), k.sem("hot"), k.sem("used")
        s_dve, s_c1, s_sq, s_eps = k.sem("dve"), k.sem("c1"), k.sem("sq"), k.sem("eps")
        s_var, s_std, s_scale, s_norm = k.sem("var"), k.sem("std"), k.sem("scale"), k.sem("norm")
        s_store = k.dmas("store")

        with nc.Block() as block:
            @block.gpsimd
            def _(pool):
                pool.iota(iota_i[:, :], pattern=[[1, ROWS + 1]], base=0, channel_multiplier=0).then_inc(s_iota, 1)
                pool.memset(keep["eps"][:, 0:1], LN_EPS).then_inc(s_eps, 1)
                pool.memset(keep["eps"][:, 1:2], MSG_EPS)

                def gather(i, s):
                    pool.tensor_copy(gidx[s][:, :], keep["index"][:, 0, bass.ds((2 * i + s) * CT, CT)]).then_inc(s_idx, 1)
                    pool.wait_ge(s_idx, 2 * i + s + 1)
                    alone(pool, s_alone)
                    for j in range(CT):
                        pool.indirect_dma_start(gbuf[s][:, j, :], None, a["payload"],
                                                bass.IndirectOffsetOnAxis(gidx[s][:, j:j + 1], 0)).then_inc(s_gath[s], 16)

                def keep_it(i, s):
                    pool.wait_ge(s_gath[s], (i + 1) * (16 * CT))
                    pool.tensor_copy(keep["payload"][:, bass.ds((2 * i + s) * CT, CT), :], gbuf[s][:, :, :]).then_inc(s_out, 1)
                    pool.wait_ge(s_out, 2 * i + s + 1)
                gather(0, 0)
                with pool.Fori(0, CHUNKS // 2 - 1) as i:
                    gather(i, 1)
                    keep_it(i, 0)
                    gather(i + 1, 0)
                    keep_it(i, 1)
                gather(CHUNKS // 2 - 1, 1)
                keep_it(CHUNKS // 2 - 1, 0)
                keep_it(CHUNKS // 2 - 1, 1)

            @block.tensor
            def _(pe):
                def add(i, s, start, stop):
                    pe.wait_ge(s_hot, (i * HOT + s + 1) * 2)
                    pe.matmul(count[:, 0:ROWS + 1], hot_lo[s][:, :], hot_hi[s][:, :], start=start, stop=stop).then_inc(s_used, 1)
                for s in range(HOT):
                    add(0, s, s == 0, False)
                with pe.Fori(1, TILES // HOT - 1) as i:
                    for s in range(HOT):
                        add(i, s, False, False)
                for s in range(HOT):
                    add(TILES // HOT - 1, s, False, s == HOT - 1)

            @block.vector
            def _(dve):
                ch = Chain(dve, s_dve)
                dve.wait_ge(s_iota, 1)
                magic = 1.5 * 2 ** 23
                n = keep["dst"]
                ch.note(dve.tensor_copy(iota_f[:, :], iota_i[:, :]))
                ch.note(dve.tensor_scalar(t0[:, :], n[:, :], -(ROWS - 1) / 2, 1.0 / ROWS, ALU.add, ALU.mult))
                ch.settle()
                ch.link(dve.tensor_scalar(t1[:, :], t0[:, :], magic, None, ALU.add))
                ch.link(dve.tensor_scalar(lo[:, :], t1[:, :], -magic, None, ALU.add))
                ch.link(dve.scalar_tensor_tensor(hi[:, :], lo[:, :], float(-ROWS), n[:, :], ALU.mult, ALU.add))
                ch.note(dve.tensor_tensor(t0[:, :], hi[:, :], lo[:, :], ALU.subtract))
                ch.note(dve.tensor_scalar(t1[:, :], n[:, :], float(MAIN), None, ALU.is_ge))
                ch.settle()
                ch.link(dve.tensor_tensor(t0[:, :], t0[:, :], t1[:, :], ALU.mult))
                ch.link(dve.tensor_tensor(lo[:, :], lo[:, :], t0[:, :], ALU.add))
                ch.link(dve.tensor_scalar(t0[:, :], hi[:, :], -1.0, float(ROWS), ALU.mult, ALU.add))
                ch.link(dve.tensor_tensor(t0[:, :], t0[:, :], t1[:, :], ALU.mult))
                ch.link(dve.tensor_tensor(hi[:, :], hi[:, :], t0[:, :], ALU.add))
                ch.link(dve.tensor_scalar(t0[:, :], n[:, :], float(N), 1000.0, ALU.is_ge, ALU.mult))
                ch.link(dve.tensor_tensor(lo[:, :], lo[:, :], t0[:, :], ALU.add))
                ch.link(dve.tensor_scalar(t0[:, :], n[:, :], float(N), 1000.0, ALU.is_ge, ALU.mult))

                def hot(i, s, first):
                    if not first:
                        dve.wait_ge(s_used, (i - 1) * HOT + s + 1)
                    t = i * HOT + s
                    dve.tensor_scalar(hot_lo[s][:, :], iota_f[:, 0:P], lo[:, bass.ds(t, 1)], None, ALU.is_equal).then_inc(s_hot, 1)
                    dve.tensor_scalar(hot_hi[s][:, :], iota_f[:, :], hi[:, bass.ds(t, 1)], None, ALU.is_equal).then_inc(s_hot, 1)
                for s in range(HOT):
                    hot(0, s, True)
                with dve.Fori(1, TILES // HOT) as i:
                    for s in range(HOT):
                        hot(i, s, False)
                dve.wait_ge(s_used, TILES)
                ch.link(dve.tensor_copy(keep["cnt"][:, :], count[:, 0:ROWS + 1]))
                dve.tensor_scalar(c1[:, :], keep["cnt"][:, :], 1.0, None, ALU.add).then_inc(s_c1, 1)
                ch.link(dve.tensor_scalar(keep["deg"][:, :], keep["cnt"][:, :], 1.0, None, ALU.max))
                ch.link(dve.reciprocal(keep["inv_deg"][:, :], keep["deg"][:, :]))
                dve.wait_ge(s_sq, 1)
                ch.link(dve.reciprocal(keep["dinv"][:, :], keep["sqrt_c1"][:, :]))
                base = ch.k
                per = Norm.STATS + Norm.SCALES

                def step(g):
                    c = Chain(dve, s_dve, base + g.num * per)
                    if g.live:
                        wait(dve, s_norm, g.num - 1)
                        ln_stats(nc, c, norm, g, lambda j: x_tile(keep, g, j)).then_inc(s_var, 1)
                        dve.wait_ge(s_std, g.num + 1)
                        ln_scales(nc, c, norm, g).then_inc(s_scale, 1)
                over_groups(dve, step)

            @block.scalar
            def _(act):
                act.wait_ge(s_c1, 1)
                act.activation(keep["sqrt_c1"][:, :], c1[:, :], ACT.Sqrt).then_inc(s_sq, 1)
                act.wait_ge(s_eps, 1)

                def step(g):
                    if g.live:
                        act.wait_ge(s_var, g.num + 1)
                        ln_sqrt(nc, norm, g, keep["eps"]).then_inc(s_std, 1)
                        act.wait_ge(s_scale, g.num + 1)
                        wait(act, s_store[g.slot], g.uses * 16)
                        ln_apply(nc, norm, g, ACT.Relu, lambda j: hout[g.slot][:, j, :],
                                 lambda j: x_tile(keep, g, j)).then_inc(s_norm, 1)
                over_groups(act, step)

            @block.sync
            def _(sp):
                zero_fill(sp, keep, a["agg"])
                for s in range(2):
                    sp.wait_ge(keep["zfill"][s], 16 * FILLS)
                sp.wait_ge(keep["zfill_tail"], 32)

                def step(g):
                    if g.live:
                        sp.wait_ge(s_norm, g.num + 1)
                        sp.dma_start(group_rows(a["table"], g), group_buf(hout[g.slot], g)).then_inc(s_store[g.slot], 16)
                over_groups(sp, step)
                for s in range(2):
                    sp.wait_ge(s_store[s], 16 * ((GROUPS + 1) // 2))


def over_chunks(eng, step):
    for c in range(4):
        step(Chunk(0, c))
    with eng.Fori(0, (CHUNKS - 4) // 2) as i:
        step(Chunk(i, 4))
        step(Chunk(i, 5))
    for c in range(CHUNKS, CHUNKS + 2):
        step(Chunk(0, c))


def alone(eng, sem):
    eng.sem_inc(sem, 1)


def edge_stage(k, a, keep, layer):
    nc = k.nc
    k.stage = f"edges{layer}"
    by = 0 if layer == 0 else 1
    soft = layer == 3
    agg = a["agg0"] if layer == 0 else a["agg"]
    with ExitStack() as mem:
        def sb(name, shape, dt=F32):
            return mem.enter_context(nc.sbuf_tensor(f"{k.stage}_{name}_sb", shape, dt))

        def two(name, shape, dt=F32):
            return [sb(f"{name}{s}", shape, dt) for s in range(2)]

        gidx, sidx = two("gidx", [P, CT], I32), two("sidx", [P, CT], I32)
        rows = two("rows", [P, CT, D])
        same = two("same", [D, CW], BF16)
        sums = two("sums", [D, CW])
        back = two("back", [P, CT, D])
        turned = [mem.enter_context(nc.psum_tensor(f"{k.stage}_turned{s}_ps", [D, 1024], F32)) for s in range(2)]
        again = [mem.enter_context(nc.psum_tensor(f"{k.stage}_again{s}_ps", [P, 2, 512], F32)) for s in range(2)]
        BANK = 4
        if soft:
            most = sb("most", [D, CW + 1])
            logit = sb("logit", [D, CW])
            decay = sb("decay", [D, CW])
            ex = sb("ex", [D, CW])
            den, num = sb("den", [D, CW]), sb("num", [D, CW])
            carry = sb("carry", [D, 2])

        s_gidx, s_sidx, s_alone = k.sem("gidx"), k.sem("sidx"), k.sem("alone")
        s_gath, s_scat, s_same = k.dmas("gath"), k.dmas("scat"), k.dmas("same")
        s_rows, s_turned, s_sums, s_again, s_back = k.sem("rows"), k.sem("turned"), k.sem("sums"), k.sem("again"), k.sem("back")
        if soft:
            s_logit, s_arg, s_exp, s_dve, s_read = k.sem("logit"), k.sem("arg"), k.sem("exp"), k.sem("dve"), k.sem("read")

        with nc.Block() as block:
            @block.gpsimd
            def _(pool):
                def step(c):
                    if c.live:
                        s = c.slot
                        if layer == 0:
                            src = keep["payload"][:, c.tiles(), 0]
                        else:
                            src = keep["index"][:, 1, c.tiles()]
                        wait(pool, s_turned, c.num - 1)
                        pool.tensor_copy(gidx[s][:, :], src).then_inc(s_gidx, 1)
                        pool.wait_ge(s_gidx, c.num + 1)
                        alone(pool, s_alone)
                        for j in range(CT):
                            pool.indirect_dma_start(rows[s][:, j, :], None, a["table"],
                                                    bass.IndirectOffsetOnAxis(gidx[s][:, j:j + 1], 0)).then_inc(s_gath[s], 16)
                    c = c + -2
                    if c.live:
                        s = c.slot
                        wait(pool, s_scat[s], c.uses * (16 * CT))
                        pool.tensor_copy(sidx[s][:, :], keep["index"][:, 2 + by, c.tiles()]).then_inc(s_sidx, 1)
                        pool.wait_ge(s_sidx, c.num + 1)
                        pool.wait_ge(s_back, c.num + 1)
                        alone(pool, s_alone)
                        for j in range(CT):
                            pool.indirect_dma_start(agg, bass.IndirectOffsetOnAxis(sidx[s][:, j:j + 1], 0),
                                                    back[s][:, j, :], None, bounds_check=N - 1,
                                                    oob_is_err=False).then_inc(s_scat[s], 16)
                over_chunks(pool, step)
                for s in range(2):
                    pool.wait_ge(s_scat[s], 16 * CT * CHUNKS // 2)

            @block.sync
            def _(sp):
                def step(c):
                    if c.live:
                        wait(sp, s_sums, c.num - 1)
                        sp.dma_start(same[c.slot][:, :], a["same"][by:by + 1, bass.ds(c.num * CW, CW)].to_broadcast([D, CW])
                                     ).then_inc(s_same[c.slot], 16)
                over_chunks(sp, step)

            @block.tensor
            def _(pe):
                def step(c):
                    if c.live:
                        if layer == 0:
                            pe.wait_ge(s_rows, c.num + 1)
                        else:
                            pe.wait_ge(s_gath[c.slot], (c.uses + 1) * (16 * CT))
                        wait(pe, s_logit if soft else s_sums, c.num - 1)
                        for j in range(CT):
                            last = pe.transpose(turned[c.slot][:, j * P:(j + 1) * P], rows[c.slot][:, j, :], keep["ident"][:, :])
                        last.then_inc(s_turned, 1)
                    c = c + -1
                    if c.live:
                        pe.wait_ge(s_sums, c.num + 1)
                        wait(pe, s_back, c.num - 1)
                        for j in range(CT):
                            last = pe.transpose(again[c.slot][:, j // BANK, (j % BANK) * D:(j % BANK + 1) * D],
                                                sums[c.slot][:, j * P:(j + 1) * P], keep["ident"][0:D, 0:D])
                        last.then_inc(s_again, 1)
                over_chunks(pe, step)

            @block.scalar
            def _(act):
                def step(c):
                    if c.live and soft:
                        act.wait_ge(s_turned, c.num + 1)
                        wait(act, s_read, c.num)
                        act.activation(logit[:, :], turned[c.slot][:, 0:CW], ACT.Identity,
                                       bias=keep["eps"][0:D, 1:2]).then_inc(s_logit, 1)
                        act.wait_ge(s_arg, c.num * 2 + 1)
                        act.activation(ex[:, :], ex[:, :], ACT.Exp).then_inc(s_exp, 1)
                        act.wait_ge(s_arg, c.num * 2 + 2)
                        act.activation(decay[:, :], decay[:, :], ACT.Exp).then_inc(s_exp, 1)
                    c = c + -1
                    if c.live:
                        act.wait_ge(s_again, c.num + 1)
                        wait(act, s_scat[c.slot], c.uses * (16 * CT))
                        act.activation(back[c.slot][:, 0:BANK, :].rearrange("p j d -> p (j d)"),
                                       again[c.slot][:, 0, 0:BANK * D], ACT.Copy)
                        act.activation(back[c.slot][:, BANK:CT, :].rearrange("p j d -> p (j d)"),
                                       again[c.slot][:, 1, 0:(CT - BANK) * D], ACT.Copy).then_inc(s_back, 1)
                over_chunks(act, step)

            @block.vector
            def _(dve):
                if soft:
                    dve.memset(most[:, CW:CW + 1], 0.0).then_inc(s_dve, 1)
                    dve.memset(carry[:, :], 0.0).then_inc(s_dve, 1)

                def step(c):
                    if not c.live:
                        return
                    s = c.slot
                    if layer == 0:
                        dve.wait_ge(s_gath[s], (c.uses + 1) * (16 * CT))
                        weight = keep["payload"][:, c.tiles(), 1:2].bitcast(F32).to_broadcast([P, CT, D])
                        dve.tensor_tensor(rows[s][:, :, :], rows[s][:, :, :], weight, ALU.mult).then_inc(s_rows, 1)
                    dve.wait_ge(s_same[s], (c.uses + 1) * 16)
                    if not soft:
                        dve.wait_ge(s_turned, c.num + 1)
                        wait(dve, s_again, c.num - 1)
                        before = sums[1 - s][:, CW - 1:CW]
                        if c.known and c.num == 0:
                            before = 0.0
                        else:
                            dve.wait_ge(s_sums, c.num)
                        dve.tensor_tensor_scan(sums[s][:, :], same[s][:, :], turned[s][:, 0:CW], before,
                                               ALU.mult, ALU.add).then_inc(s_sums, 1)
                        return
                    per = 9
                    ch = Chain(dve, s_dve, c.num * per + 2)
                    ch.settle()
                    ch.link(dve.tensor_copy(most[:, 0:1], most[:, CW:CW + 1]))
                    dve.wait_ge(s_logit, c.num + 1)
                    ch.link(dve.tensor_tensor_scan(most[:, 1:CW + 1], same[s][:, :], logit[:, :], most[:, 0:1], ALU.mult, ALU.max))
                    dve.tensor_tensor(ex[:, :], logit[:, :], most[:, 1:CW + 1], ALU.subtract).then_inc(s_arg, 1)
                    ch.link(dve.tensor_tensor(decay[:, :], most[:, 0:CW], same[s][:, :], ALU.mult))
                    dve.tensor_tensor(decay[:, :], decay[:, :], most[:, 1:CW + 1], ALU.subtract).then_inc(s_arg, 1)
                    dve.wait_ge(s_exp, c.num * 2 + 1)
                    ch.note(dve.tensor_tensor(logit[:, :], logit[:, :], ex[:, :], ALU.mult))
                    dve.wait_ge(s_exp, c.num * 2 + 2)
                    ch.link(dve.tensor_tensor(decay[:, :], decay[:, :], same[s][:, :], ALU.mult))
                    ch.note(dve.tensor_tensor_scan(den[:, :], decay[:, :], ex[:, :], carry[:, 0:1], ALU.mult, ALU.add))
                    dve.tensor_tensor_scan(num[:, :], decay[:, :], logit[:, :], carry[:, 1:2], ALU.mult, ALU.add).then_inc(s_read, 1)
                    ch.settle()
                    ch.note(dve.tensor_copy(carry[:, 0:1], den[:, CW - 1:CW]))
                    dve.wait_ge(s_read, c.num + 1)
                    ch.note(dve.tensor_copy(carry[:, 1:2], num[:, CW - 1:CW]))
                    ch.settle()
                    ch.link(dve.reciprocal(den[:, :], den[:, :]))
                    wait(dve, s_again, c.num - 1)
                    dve.tensor_tensor(sums[s][:, :], num[:, :], den[:, :], ALU.mult).then_inc(s_sums, 1)
                    dve.wait_ge(s_sums, c.num + 1)
                    assert ch.k == per, ch.k
                over_chunks(dve, step)


def bcast(column, w):
    return column.unsqueeze(2).to_broadcast([P, w, D])


def node_cols(keep, name, g):
    return keep[name][:, g.tiles()]


def node_stage(k, a, keep, layer):
    nc = k.nc
    k.stage = f"nodes{layer}"
    final = layer == 3
    with ExitStack() as mem:
        def sb(name, shape, dt=F32):
            return mem.enter_context(nc.sbuf_tensor(f"{k.stage}_{name}_sb", shape, dt))

        def two(name, shape, dt=F32):
            return [sb(f"{name}{s}", shape, dt) for s in range(2)]

        K = D + 1
        weight = sb("weight", [K, D])
        slope = sb("slope", [P, 1])
        agg = two("agg", [P, G, K])
        own = two("own", [P, G, D]) if layer > 1 else None
        aggT = two("aggT", [K, 2, SUB * P])
        y = two("y", [P, G, D])
        neg = sb("neg", [P, G, D]) if layer == 2 else None
        hout = two("hout", [P, G, D]) if not final else y
        norm = Norm(sb, "norm")
        scale = two("scale", [P, 2, G]) if layer == 1 else None
        turned = [mem.enter_context(nc.psum_tensor(f"{k.stage}_turned{s}_ps", [P, 2, 512], F32)) for s in range(2)]
        prod = [mem.enter_context(nc.psum_tensor(f"{k.stage}_prod{s}_ps", [P, 2, 512], F32)) for s in range(2)]

        s_weight, s_ones, s_sum = k.dma("weight"), k.sem("ones"), k.sem("sum")
        s_agg, s_own, s_store = k.dmas("agg"), k.dmas("own"), k.dmas("store")
        s_turned, s_aggT, s_prod, s_y, s_x = k.sem("turned"), k.sem("aggT"), k.sem("prod"), k.sem("y"), k.sem("x")
        s_dve, s_var, s_std, s_scale, s_norm = k.sem("dve"), k.sem("var"), k.sem("std"), k.sem("scale"), k.sem("norm")
        s_in, s_act = k.sem("in"), k.sem("act")

        def halves(g):
            return [(u, u * SUB, min(SUB, g.w - u * SUB)) for u in range(2) if g.w > u * SUB]

        with nc.Block() as block:
            @block.sync
            def _(sp):
                sp.dma_start(weight[0:D, :], a[f"L{layer}_gnn_W"]).then_inc(s_weight, 16)
                sp.dma_start(weight[D:K, :], a[f"L{layer}_gnn_b"].rearrange("(a n) -> a n", a=1)).then_inc(s_weight, 16)
                if layer == 2:
                    sp.dma_start(slope[:, :], a["L2_gnn_prelu_a"].rearrange("(a n) -> a n", a=1).to_broadcast([P, 1])).then_inc(s_weight, 16)

                def load(g):
                    wait(sp, s_turned, g.num - 1)
                    rows = TAIL if g.tail else P
                    src = group_rows(a["agg"], g).rearrange("p (j d) -> p j d", d=D)
                    sp.dma_start(agg[g.slot][0:rows, 0:g.w, 0:D], src).then_inc(s_agg[g.slot], 16)
                    if own:
                        sp.dma_start(group_buf(own[g.slot], g), group_rows(a["table"], g)).then_inc(s_own[g.slot], 16)

                def step(g):
                    if (g + 3).live:
                        load(g + 3)
                    g = g + (-1 if final else -3)
                    if g.live:
                        sp.wait_ge(s_y if final else s_norm, g.num + 1)
                        sp.dma_start(group_rows(a["out"] if final else a["table"], g), group_buf(hout[g.slot], g)
                                     ).then_inc(s_store[g.slot], 16)
                over_groups(sp, step)
                for s in range(2):
                    sp.wait_ge(s_store[s], 16 * ((GROUPS + 1) // 2))

            @block.gpsimd
            def _(pool):
                if layer == 3:
                    for s in range(2):
                        pool.memset(agg[s][:, :, D:K], 1.0).then_inc(s_ones, 1)

                def factor(g):
                    if not g.live:
                        return
                    s, w = g.slot, g.w
                    if layer < 3:
                        wait(pool, s_turned, g.num - 1)
                        pool.tensor_copy(agg[s][:, 0:w, D], node_cols(keep, "cnt" if layer == 1 else "sqrt_c1", g)).then_inc(s_in, 1)
                    if own:
                        pool.wait_ge(s_agg[s], (g.uses + 1) * 16)
                        pool.wait_ge(s_own[s], (g.uses + 1) * 16)
                        pool.tensor_tensor(agg[s][:, 0:w, 0:D], agg[s][:, 0:w, 0:D], own[s][:, 0:w, :], ALU.add).then_inc(s_sum, 1)

                def step(g):
                    factor(g + 3)
                    g = g + -1
                    if g.live and not final:
                        pool.wait_ge(s_y, g.num + 1)
                        xs = keep["x"][:, g.cols()]
                        pool.tensor_tensor(xs, xs, y[g.slot][:, 0:g.w, :].rearrange("p j d -> p (j d)"), ALU.add).then_inc(s_x, 1)
                over_groups(pool, step)

            @block.tensor
            def _(pe):
                pe.wait_ge(s_weight, 48 if layer == 2 else 32)
                if layer == 3:
                    pe.wait_ge(s_ones, 2)

                def step(g):
                    n = g + 2
                    if n.live:
                        if layer < 3:
                            pe.wait_ge(s_in, n.num + 1)
                        if own:
                            pe.wait_ge(s_sum, n.num + 1)
                        else:
                            pe.wait_ge(s_agg[n.slot], (n.uses + 1) * 16)
                        wait(pe, s_aggT, n.num - 1)
                        for u, j0, m in halves(n):
                            for j in range(m):
                                last = pe.transpose(turned[n.slot][0:K, u, j * P:(j + 1) * P], agg[n.slot][:, j0 + j, :], keep["ident"][:, :])
                        last.then_inc(s_turned, 1)
                    if g.live:
                        pe.wait_ge(s_aggT, g.num + 1)
                        wait(pe, s_y, g.num - 1)
                        for u, j0, m in halves(g):
                            for j in range(m):
                                last = pe.matmul(prod[g.slot][:, u, j * D:(j + 1) * D], aggT[g.slot][:, u, j * P:(j + 1) * P],
                                                 weight[:, :], start=True, stop=True)
                        last.then_inc(s_prod, 1)
                over_groups(pe, step)

            @block.scalar
            def _(act):
                def step(g):
                    p = g + -3
                    if p.live and not final:
                        act.wait_ge(s_var, p.num + 1)
                        ln_sqrt(nc, norm, p, keep["eps"]).then_inc(s_std, 1)
                    n = g + 1
                    if n.live:
                        act.wait_ge(s_turned, n.num + 1)
                        wait(act, s_prod, n.num - 1)
                        if n.tail:
                            act.activation(aggT[n.slot][:, 0, 0:P], turned[n.slot][0:K, 0, 0:P], ACT.Copy).then_inc(s_aggT, 1)
                        else:
                            act.activation(aggT[n.slot][:, :, :], turned[n.slot][0:K, :, 0:SUB * P], ACT.Copy).then_inc(s_aggT, 1)
                    if p.live and not final:
                        act.wait_ge(s_scale, p.num + 1)
                        wait(act, s_store[p.slot], p.uses * 16)
                        ln_apply(nc, norm, p, ACT.Relu, lambda j: hout[p.slot][:, j, :], lambda j: x_tile(keep, p, j),
                                 factors=scale).then_inc(s_norm, 1)
                over_groups(act, step)

            @block.vector
            def _(dve):
                per = Norm.STATS + Norm.SCALES + (2 if layer == 1 else 0)

                def product(g):
                    c = Chain(dve, s_act, g.num * 3)
                    s, w = g.slot, g.w
                    dve.wait_ge(s_prod, g.num + 1)
                    if final:
                        wait(dve, s_store[s], g.uses * 16)
                    else:
                        wait(dve, s_x, g.num - 1)
                    xs = keep["x"][:, g.cols()].rearrange("p (j d) -> p j d", d=D)
                    cols = {1: "inv_deg", 2: "dinv"}.get(layer)
                    parts = halves(g)
                    for u, j0, m in parts:
                        pr = prod[s][:, u, 0:m * D].rearrange("p (j d) -> p j d", d=D)
                        out = y[s][:, j0:j0 + m, :]
                        if final:
                            ins = dve.tensor_tensor(out, pr, xs[:, j0:j0 + m, :], ALU.add)
                        else:
                            col = keep[cols][:, bass.ds(g.num * G + j0, m)]
                            ins = dve.tensor_tensor(out, pr, bcast(col, m), ALU.mult)
                        if layer == 2:
                            c.note(ins)
                    if layer == 2:
                        c.settle()
                        flat = y[s][:, 0:w, :].rearrange("p j d -> p (j d)")
                        below = neg[:, 0:w, :].rearrange("p j d -> p (j d)")
                        c.link(dve.tensor_scalar(below, flat, 0.0, slope[:, 0:1], ALU.min, ALU.mult))
                        ins = dve.scalar_tensor_tensor(flat, flat, 0.0, below, ALU.max, ALU.add)
                    ins.then_inc(s_y, 1)

                def step(g):
                    q = g + -3
                    if q.live and not final:
                        dve.wait_ge(s_std, q.num + 1)
                        c = Chain(dve, s_dve, q.num * per + Norm.STATS - (G - q.w))
                        ins = ln_scales(nc, c, norm, q)
                        if layer == 1:
                            c.link(ins)
                            dinv = node_cols(keep, "dinv", q)
                            st = norm.st[q.slot]
                            c.note(dve.tensor_tensor(scale[q.slot][:, 0, 0:q.w], st[:, Norm.RSTD, 0:q.w], dinv, ALU.mult))
                            c.settle()
                            ins = dve.tensor_tensor(scale[q.slot][:, 1, 0:q.w], st[:, Norm.SHIFT, 0:q.w], dinv, ALU.mult)
                        ins.then_inc(s_scale, 1)
                    if (g + -1).live:
                        product(g + -1)
                    p = g + -2
                    if p.live and not final:
                        dve.wait_ge(s_x, p.num + 1)
                        wait(dve, s_norm, p.num - 1)
                        c = Chain(dve, s_dve, p.num * per)
                        ln_stats(nc, c, norm, p, lambda j: x_tile(keep, p, j)).then_inc(s_var, 1)
                over_groups(dve, step)


def mlp_stage(k, a, keep):
    nc = k.nc
    k.stage = "mlp"
    with ExitStack() as mem:
        def sb(name, shape, dt=F32):
            return mem.enter_context(nc.sbuf_tensor(f"{k.stage}_{name}_sb", shape, dt))

        def two(name, shape, dt=F32):
            return [sb(f"{name}{s}", shape, dt) for s in range(2)]

        def ps(name, shape):
            return mem.enter_context(nc.psum_tensor(f"{k.stage}_{name}_ps", shape, F32))

        K = D + 2
        wh = sb("wh", [D, HID])
        wa = sb("wa", [K, HID])
        wo = sb("wo", [P, 2, D])
        rows = {n: sb(n, [P, D]) for n in ("bias", "gamma", "beta")}
        agg = two("agg", [P, G, K])
        h = two("h", [P, G, D])
        hb = two("hb", [P, G, D])
        aggT, hT = two("aggT", [K, SUB * P]), two("hT", [D, SUB * P])
        hid = two("hid", [P, 2, SUB * P])
        y = two("y", [P, G, D])
        hout = two("hout", [P, G, D])
        norm1, norm2 = Norm(sb, "norm1"), Norm(sb, "norm2")
        turned_a, turned_h, prod = ([ps(f"{n}{u}", [P, 512]) for u in range(2)] for n in ("ta", "th", "prod"))
        hidp = [ps(f"hidp{v}", [P, 512]) for v in range(2)]

        s_weight, s_rows, s_ones = k.dma("weight"), k.dma("rows"), k.sem("ones")
        s_agg, s_h, s_store = k.dmas("agg"), k.dmas("h"), k.dmas("store")
        s_div, s_deg, s_hb, s_turned, s_copied = k.sem("div"), k.sem("deg"), k.sem("hb"), k.sem("turned"), k.sem("copied")
        s_hidp, s_hid, s_prod, s_y, s_z, s_xb, s_x = (k.sem(n) for n in ("hidp", "hid", "prod", "y", "z", "xb", "x"))
        s_dve, s_var1, s_std1, s_scale1 = k.sem("dve"), k.sem("var1"), k.sem("std1"), k.sem("scale1")
        s_dve2, s_gamma, s_var2, s_std2, s_scale2, s_norm = k.sem("dve2"), k.sem("gamma"), k.sem("var2"), k.sem("std2"), k.sem("scale2"), k.sem("norm")

        def halves(g):
            return [(u, u * SUB, min(SUB, g.w - u * SUB)) for u in range(2) if g.w > u * SUB]

        def upto(g, u):
            return g.num * 2 + u + 1

        def last(g):
            return g.num * 2 + len(halves(g))

        with nc.Block() as block:
            @block.sync
            def _(sp):
                wm = a["L0_gnn_Wm1"]
                sp.dma_start(wh[:, :], wm[0:D, :]).then_inc(s_weight, 16)
                sp.dma_start(wa[0:D, :], wm[D:2 * D, :]).then_inc(s_weight, 16)
                sp.dma_start(wa[D:D + 1, :], a["L0_gnn_bm1"].rearrange("(a n) -> a n", a=1)).then_inc(s_weight, 16)
                sp.dma_start(wa[D + 1:K, :], wm[2 * D:2 * D + 1, :]).then_inc(s_weight, 16)
                sp.dma_start(wo[:, :, :], a["L0_gnn_Wm2"].rearrange("(v p) d -> p v d", p=P)).then_inc(s_weight, 16)
                for n, name in (("bias", "bm2"), ("gamma", "gamma"), ("beta", "beta")):
                    sp.dma_start(rows[n][:, :], a[f"L0_gnn_{name}"].rearrange("(a n) -> a n", a=1).to_broadcast([P, D])).then_inc(s_rows, 16)

                def load(g):
                    wait(sp, s_turned, (g.num - 1) * 2)
                    wait(sp, s_hb, g.num - 1)
                    part = TAIL if g.tail else P
                    src = group_rows(a["agg0"], g).rearrange("p (j d) -> p j d", d=D)
                    sp.dma_start(agg[g.slot][0:part, 0:g.w, 0:D], src).then_inc(s_agg[g.slot], 16)
                    sp.dma_start(group_buf(h[g.slot], g), group_rows(a["table"], g)).then_inc(s_h[g.slot], 16)

                def step(g):
                    if (g + 2).live:
                        load(g + 2)
                    n = g + -4
                    if n.live:
                        sp.wait_ge(s_norm, last(n))
                        sp.dma_start(group_rows(a["table"], n), group_buf(hout[n.slot], n)).then_inc(s_store[n.slot], 16)
                over_groups(sp, step)
                for s in range(2):
                    sp.wait_ge(s_store[s], 16 * ((GROUPS + 1) // 2))

            @block.gpsimd
            def _(pool):
                for s in range(2):
                    pool.memset(agg[s][:, :, D:D + 1], 1.0).then_inc(s_ones, 1)
                pool.wait_ge(s_rows, 48)

                def step(g):
                    if g.live:
                        s, w = g.slot, g.w
                        pool.wait_ge(s_h[s], (g.uses + 1) * 16)
                        wait(pool, s_y, (g.num - 1) * 2)
                        pool.tensor_tensor(hb[s][:, 0:w, :], h[s][:, 0:w, :], rows["bias"][:, :].unsqueeze(1).to_broadcast([P, w, D]),
                                           ALU.add).then_inc(s_hb, 1)
                    n = g + 2
                    if n.live:
                        wait(pool, s_turned, (n.num - 1) * 2)
                        pool.tensor_copy(agg[n.slot][:, 0:n.w, D + 1], node_cols(keep, "deg", n)).then_inc(s_deg, 1)
                    n = g + -2
                    if n.live:
                        xs = keep["x"][:, n.cols()].rearrange("p (j d) -> p j d", d=D)
                        pool.tensor_tensor(xs, xs, rows["beta"][:, :].unsqueeze(1).to_broadcast([P, n.w, D]), ALU.add).then_inc(s_xb, 1)
                over_groups(pool, step)

            @block.tensor
            def _(pe):
                pe.wait_ge(s_weight, 16 * 5)
                pe.wait_ge(s_ones, 2)

                def turn(n, u):
                    if u == 0:
                        pe.wait_ge(s_div, n.num + 1)
                        pe.wait_ge(s_deg, n.num + 1)
                        pe.wait_ge(s_h[n.slot], (n.uses + 1) * 16)
                    _, j0, m = halves(n)[u]
                    wait(pe, s_copied, (n.num - 1) * 2 + u + 1)
                    for j in range(m):
                        pe.transpose(turned_a[u][0:K, j * P:(j + 1) * P], agg[n.slot][:, j0 + j, :], keep["ident"][:, :])
                    for j in range(m):
                        ins = pe.transpose(turned_h[u][0:D, j * P:(j + 1) * P], h[n.slot][:, j0 + j, :], keep["ident"][:, :])
                    ins.then_inc(s_turned, 1)

                def step(g):
                    n = g + 1
                    for u in range(2):
                        mine = g.live and u < len(halves(g))
                        if mine:
                            _, j0, m = halves(g)[u]
                            pe.wait_ge(s_copied, upto(g, u))
                            for v in range(2):
                                wait(pe, s_hid, g.num * 4 + u * 2 + v - 1)
                                pe.matmul(hidp[v][:, 0:m * P], wh[:, v * P:(v + 1) * P], hT[u][:, 0:m * P], start=True, stop=False)
                                pe.matmul(hidp[v][:, 0:m * P], wa[:, v * P:(v + 1) * P], aggT[u][:, 0:m * P],
                                          start=False, stop=True).then_inc(s_hidp, 1)
                        if n.live and u < len(halves(n)):
                            turn(n, u)
                        if mine:
                            wait(pe, s_y, (g.num - 1) * 2 + u + 1)
                            pe.wait_ge(s_hid, g.num * 4 + u * 2 + 2)
                            for j in range(m):
                                for v in range(2):
                                    ins = pe.matmul(prod[u][:, j * D:(j + 1) * D], hid[u][:, v, j * P:(j + 1) * P],
                                                    wo[:, v, :], start=(v == 0), stop=(v == 1))
                            ins.then_inc(s_prod, 1)
                over_groups(pe, step)

            @block.scalar
            def _(act):
                def normed1(n, u):
                    if n.live and u < len(halves(n)):
                        _, j0, m = halves(n)[u]
                        act.wait_ge(s_scale1, n.num + 1)
                        ys = y[n.slot]
                        ln_apply(nc, norm1, n, ACT.Identity, lambda j: ys[:, j, :], lambda j: ys[:, j, :],
                                 tiles=range(j0, j0 + m)).then_inc(s_z, 1)

                def normed2(n, u):
                    if n.live and u < len(halves(n)):
                        _, j0, m = halves(n)[u]
                        act.wait_ge(s_scale2, n.num + 1)
                        wait(act, s_store[n.slot], n.uses * 16)
                        ln_apply(nc, norm2, n, ACT.Relu, lambda j: hout[n.slot][:, j, :], lambda j: x_tile(keep, n, j),
                                 tiles=range(j0, j0 + m)).then_inc(s_norm, 1)

                def step(g):
                    z, q = g + -2, g + -4
                    if z.live:
                        act.wait_ge(s_var1, z.num + 1)
                        ln_sqrt(nc, norm1, z, keep["eps"]).then_inc(s_std1, 1)
                    if q.live:
                        act.wait_ge(s_var2, q.num + 1)
                        ln_sqrt(nc, norm2, q, keep["eps"]).then_inc(s_std2, 1)
                    n = g + 1
                    for u in range(2):
                        if g.live and u < len(halves(g)):
                            m = halves(g)[u][2]
                            wait(act, s_prod, (g.num - 1) * 2 + u + 1)
                            for v in range(2):
                                act.wait_ge(s_hidp, g.num * 4 + u * 2 + v + 1)
                                act.activation(hid[u][:, v, 0:m * P], hidp[v][:, 0:m * P], ACT.Relu).then_inc(s_hid, 1)
                        normed1(z, u)
                        if n.live and u < len(halves(n)):
                            m = halves(n)[u][2]
                            act.wait_ge(s_turned, upto(n, u))
                            wait(act, s_hidp, (n.num - 1) * 4 + u * 2 + 2)
                            act.activation(aggT[u][:, 0:m * P], turned_a[u][0:K, 0:m * P], ACT.Copy)
                            act.activation(hT[u][:, 0:m * P], turned_h[u][0:D, 0:m * P], ACT.Copy).then_inc(s_copied, 1)
                        normed2(q, u)
                over_groups(act, step)

            @block.vector
            def _(dve):
                per = Norm.STATS + Norm.SCALES

                def step(g):
                    n = g + -3
                    if n.live:
                        s = n.slot
                        dve.wait_ge(s_z, last(n))
                        dve.wait_ge(s_xb, n.num + 1)
                        ys = y[s][:, 0:n.w, :]
                        dve.tensor_tensor(ys, ys, rows["gamma"][:, :].unsqueeze(1).to_broadcast([P, n.w, D]), ALU.mult).then_inc(s_gamma, 1)
                        dve.wait_ge(s_gamma, n.num + 1)
                        xs = keep["x"][:, n.cols()]
                        dve.tensor_tensor(xs, xs, ys.rearrange("p j d -> p (j d)"), ALU.add).then_inc(s_x, 1)
                    n = g + -1
                    if n.live:
                        s = n.slot
                        dve.wait_ge(s_prod, last(n))
                        dve.wait_ge(s_hb, n.num + 1)
                        wait(dve, s_x, n.num - 1)
                        for u, j0, m in halves(n):
                            dve.tensor_tensor(y[s][:, j0:j0 + m, :], prod[u][:, 0:m * D].rearrange("p (j d) -> p j d", d=D),
                                              hb[s][:, j0:j0 + m, :], ALU.add).then_inc(s_y, 1)
                    n = g + -2
                    if n.live:
                        dve.wait_ge(s_std1, n.num + 1)
                        c = Chain(dve, s_dve, n.num * per + Norm.STATS - (G - n.w))
                        ln_scales(nc, c, norm1, n).then_inc(s_scale1, 1)
                    n = g + -4
                    if n.live:
                        dve.wait_ge(s_std2, n.num + 1)
                        c = Chain(dve, s_dve2, n.num * per + Norm.STATS - (G - n.w))
                        ln_scales(nc, c, norm2, n).then_inc(s_scale2, 1)
                    n = g + -3
                    if n.live:
                        dve.wait_ge(s_x, n.num + 1)
                        wait(dve, s_norm, (n.num - 1) * 2)
                        c = Chain(dve, s_dve2, n.num * per)
                        ln_stats(nc, c, norm2, n, lambda j: x_tile(keep, n, j)).then_inc(s_var2, 1)
                    n = g + -1
                    if n.live:
                        dve.wait_ge(s_y, last(n))
                        c = Chain(dve, s_dve, n.num * per)
                        ln_stats(nc, c, norm1, n, lambda j: y[n.slot][:, j, :]).then_inc(s_var1, 1)
                    n = g + 2
                    if n.live:
                        dve.wait_ge(s_agg[n.slot], (n.uses + 1) * 16)
                        v = agg[n.slot][:, 0:n.w, 0:D]
                        dve.tensor_tensor(v, v, bcast(node_cols(keep, "inv_deg", n), n.w), ALU.mult).then_inc(s_div, 1)
                over_groups(dve, step)


class Chunk:

    def __init__(self, i, c):
        self.i, self.c = i, c
        self.known = isinstance(i, int)
        self.slot = c % 2
        self.num = 2 * i + c
        self.uses = i + c // 2
        self.live = not self.known or 0 <= self.num < CHUNKS

    def __add__(self, d):
        return Chunk(self.i, self.c + d)

    def tiles(self):
        return bass.ds(self.num * CT, CT)


_WEIGHTS = ["L0_gnn_W1", "L0_gnn_b1", "L0_gnn_W2", "L0_gnn_b2", "L0_gnn_Wm1", "L0_gnn_bm1", "L0_gnn_Wm2", "L0_gnn_bm2",
            "L0_gnn_gamma", "L0_gnn_beta", "L1_gnn_W", "L1_gnn_b", "L2_gnn_W", "L2_gnn_b", "L2_gnn_prelu_a",
            "L3_gnn_W", "L3_gnn_b"]


def build(nc, a):
    a = dict(a)
    for name, shape, dt in (("table", (N, D), F32), ("agg0", (N, D), F32), ("agg", (N, D), F32),
                            ("targets", (2, SORT + 2), I32), ("same", (2, SORT), BF16),
                            ("payload", (EDGES, 2), I32), ("feat_parts", ((PARTS * PARTS + 1) * FEATS, EDGES), BF16),
                            ("w1_parts", (PARTS * FEATS, HID), BF16), ("b1_parts", (PARTS, HID), BF16)):
        a[name] = nc.dram_tensor(name, shape, dt).ap()
    with ExitStack() as ctx:
        k = Kernel(nc)
        k.stage = "keep"
        k.turn_points = turn_points()

        def sb(name, shape, dt=F32):
            return ctx.enter_context(nc.sbuf_tensor(f"{name}_keep", shape, dt))

        keep = {
            "x": sb("x_all", [P, (ROWS + 1) * D]),
            "ident": sb("ident", [P, P]),
            "index": sb("index", [P, 4, TILES], I32),
            "dst": sb("dst_sorted", [P, TILES]),
            "payload": sb("payload", [P, TILES, 2], I32),
            "eps": sb("eps", [P, 2]),
        }
        names = ("cnt", "deg", "inv_deg", "sqrt_c1", "dinv")
        keep["node"] = sb("node", [P, len(names), ROWS + 1])
        for n, name in enumerate(names):
            keep[name] = keep["node"][:, n, :]
        keep["zeros"] = sb("zeros", [P, ROWS * D // FILLS])
        keep["zfill"], keep["zfill_tail"], keep["zfills"] = k.dmas("zfill"), k.dma("zfill_tail"), 0
        for stage in STAGES:
            stage(k, a, keep)
            k.end()


def edges(layer):
    return lambda k, a, keep: edge_stage(k, a, keep, layer)


def nodes(layer):
    return lambda k, a, keep: node_stage(k, a, keep, layer)


STAGES = [sort_stage, first_stage, edges(0), mlp_stage, edges(1), nodes(1), edges(2), nodes(2), edges(3), nodes(3)]


def kernel(**inputs):
    import numpy as _np
    import concourse.bacc as _bacc
    from concourse import mybir as _mybir
    from concourse.bass_utils import run_bass_kernel_spmd as _run

    nc = _bacc.Bacc("TRN2", target_bir_lowering=False, num_devices=1)
    pad = SORT - E
    laid = {
        "x": inputs["x"],
        "src": _np.concatenate([inputs["src"], _np.full(pad, SRC_PAD, _np.int32)]).reshape(P, COLS),
        "dst": _np.concatenate([inputs["dst"], _np.full(pad, DST_PAD, _np.int32)]).reshape(P, COLS),
        "edge_attr_T": _np.concatenate([inputs["edge_attr_3"], _np.zeros((EDGES - E, FEATS), _np.float32)]).T,
    }
    laid.update({name: inputs[name] for name in _WEIGHTS})
    arrays, args = {}, {}
    for name, value in laid.items():
        value = _np.ascontiguousarray(value)
        arrays[f"in_{name}"] = value
        args[name] = nc.dram_tensor(f"in_{name}", value.shape, _mybir.dt.from_np(value.dtype), kind="ExternalInput").ap()
    args["out"] = nc.dram_tensor("out_0", (N, D), F32, kind="ExternalOutput").ap()
    build(nc, args)
    r = _run(nc, [arrays], core_ids=[0])
    return r.results[0]["out_0"]
```

```python
import concourse.bass as bass
from concourse import mybir
from contextlib import ExitStack

F32 = mybir.dt.float32
I32 = mybir.dt.int32
BF16 = mybir.dt.bfloat16
ALU = mybir.AluOpType
ACT = mybir.ActivationFunctionType

P = 128
N, D, E = 50000, 96, 25000
HID = 256
LN_EPS, MSG_EPS = 1e-5, 1e-7

ROWS = N // P
MAIN = P * ROWS
TAIL = N - MAIN
G = 6
STEPS = 4
SUB = 3
GROUPS = ROWS // G
assert ROWS % G == 0 and GROUPS % 2 == 1

SORT, COLS = 32768, 256
TILES = -(-E // P)
CT = 7
CHUNKS = TILES // CT
CW = CT * P
assert TILES % CT == 0 and CHUNKS % 2 == 0

SRC_OFF = 256
SRC_PAD = 65024 - SRC_OFF
DST_LOW = 32768 + 128
DST_HALF = 25000
DST_HIGH = 128 - DST_HALF
DST_PAD = 32512 - DST_HIGH
WARM = 64
FILLS = 36
SKIP = 100000

UNIT, LOAD = 512, 6
UT = UNIT // P
UNITS = TILES // UT
LOADS = UNITS // LOAD
EDGES = UNITS * UNIT
assert LOADS * LOAD + 1 == UNITS and UT * UNITS == TILES and LOAD % 2 == 0
FEATS, PARTS = 3, 3
SPLIT = 32


class Group:

    def __init__(self, i, c):
        self.i, self.c = i, c
        self.known = isinstance(i, int)
        self.slot = c % 2
        self.num = STEPS * i + c
        self.uses = STEPS // 2 * i + c // 2
        self.live = not self.known or 0 <= self.num <= GROUPS
        self.tail = self.known and self.num == GROUPS
        self.w = 1 if self.tail else G

    def __add__(self, d):
        return Group(self.i, self.c + d)

    def tiles(self):
        return bass.ds(self.num * G, self.w)

    def cols(self):
        return bass.ds(self.num * G * D, self.w * D)


def wait(eng, sem, value):
    if not isinstance(value, int) or value > 0:
        eng.wait_ge(sem, value)


def over_groups(eng, step):
    first, loops = 8, (GROUPS - 12) // STEPS
    for c in range(-3, first):
        step(Group(0, c))
    with eng.Fori(0, loops) as i:
        for c in range(first, first + STEPS):
            step(Group(i, c))
    for c in range(first + loops * STEPS, GROUPS + 7):
        step(Group(0, c))


class Chain:

    def __init__(self, eng, sem, base=0):
        self.eng, self.sem, self.base, self.k = eng, sem, base, 0

    def note(self, ins):
        ins.then_inc(self.sem, 1)
        self.k += 1

    def settle(self):
        self.eng.wait_ge(self.sem, self.base + self.k)

    def link(self, ins):
        self.note(ins)
        self.settle()


class Kernel:

    def __init__(self, nc):
        self.nc, self.stage, self.steps = nc, "", []

    def sem(self, name):
        self.steps.append(self.nc.alloc_semaphore(f"{self.stage}_{name}"))
        return self.steps[-1]

    def dma(self, name):
        return self.nc.alloc_semaphore(f"{self.stage}_{name}")

    def dmas(self, name):
        return [self.dma(f"{name}{s}") for s in range(2)]

    def end(self):
        self.nc.clear_and_free_semaphores(self.steps)
        self.nc.all_engine_barrier()
        self.steps = []


def group_rows(dram, g):
    if g.tail:
        return dram[MAIN:N, :]
    return dram[0:MAIN, :].rearrange("(p j) d -> p (j d)", p=P)[:, g.cols()]


def group_buf(buf, g):
    rows = TAIL if g.tail else P
    return buf[0:rows, 0:g.w, :].rearrange("p j d -> p (j d)")


def sort_stage(k, a, keep):
    nc = k.nc
    k.stage = "sort"
    with ExitStack() as mem:
        def sb(name, shape, dt=F32):
            return mem.enter_context(nc.sbuf_tensor(f"{k.stage}_{name}_sb", shape, dt))

        def ps(name, shape):
            return mem.enter_context(nc.psum_tensor(f"{k.stage}_{name}_ps", shape, F32))

        ends = sb("ends", [P, 2, COLS], I32)
        keys = [sb(f"keys{b}", [P, 2, COLS]) for b in range(2)]
        place = sb("place", [P, COLS], I32)
        part_i = sb("part_i", [P, 1], I32)
        sign = sb("sign", [P, 1])
        tmp = sb("tmp", [P, COLS], I32)
        tgt = sb("tgt", [P, 2, COLS], I32)
        nxt = sb("nxt", [P, 2, COLS], I32)
        prv = sb("prv", [P, 2, COLS], I32)
        same = sb("same", [P, 2, COLS], BF16)
        none = sb("none", [2, 2], I32)
        K = PARTS * PARTS * FEATS + PARTS
        assert FEATS == PARTS
        hid = sb("hid", [P, 2, UT * HID])
        cut = EDGES // SPLIT
        early = {n: keep[n][:, :, :].rearrange("p a b -> p (a b)") for n in ("node", "index", "payload")}
        attr, rest = (hid[0:FEATS * SPLIT, s, 0:cut] for s in range(2))
        words = (PARTS + 1) * cut // 2
        parts = early["node"][0:FEATS * SPLIT, 0:words].bitcast(BF16).rearrange("p (i n) -> p i n", i=PARTS + 1)
        wb = early["node"][0:FEATS + 1, words:words + HID]
        wb_rest = early["index"][0:FEATS + 1, 0:HID].bitcast(F32)
        wb_parts = early["payload"][0:FEATS + 1, 0:PARTS * HID // 2].bitcast(BF16).rearrange("p (i n) -> p i n", i=PARTS)
        feat = sb("feat", [K, 2, (LOAD + 1) * UNIT], BF16)
        w1 = sb("w1", [K, HID], BF16)
        w2 = sb("w2", [P, HID])
        b2 = sb("b2", [P, 1])
        wcol = sb("wcol", [P, TILES])
        fidx = hid[:, :, :].rearrange("p s n -> p (s n)")[:, 0:5 * COLS].rearrange("p (n f) -> p n f", f=COLS)
        HALF = TILES // 2
        dst_q = sb("dst_q", [HALF, 2, P], I32)
        pay = sb("pay", [HALF, 2, P, 2], I32)
        turn = ps("turn", [P, 2, 2, P])
        turn2 = ps("turn2", [P, 2, 2, P])
        turn3 = ps("turn3", [P, 2, 2, P])
        psh = [ps(f"psh{s}", [P, UT * HID]) for s in range(2)]

        s_ends, s_x, s_zero, s_xtail = k.dma("ends"), k.dmas("x"), k.sem("zero"), k.sem("xtail")
        s_const, s_key, s_ident, s_turn = k.sem("const"), k.sem("key"), k.sem("ident"), k.sem("turned")
        s_tgt, s_near, s_same, s_none, s_pad = k.sem("tgt"), k.dma("near"), k.sem("same"), k.sem("none"), k.dma("pad")
        s_fidx, s_store, s_ones = k.sem("fidx"), k.dma("store"), k.sem("ones")
        s_attr, s_wb, s_weights, s_dstq = k.dma("attr"), k.dma("wb"), k.dma("weights"), k.dma("dstq")
        s_part, s_left = k.sem("part"), k.sem("left")
        s_wparts, s_w1, s_parts, s_feat = k.dma("wparts"), k.dma("w1"), k.dma("parts"), k.dmas("feat")
        s_hid, s_relu, s_mul, s_sum, s_wcol, s_wturn = (k.sem(n) for n in ("hid", "relu", "mul", "sum", "wcol", "wturn"))
        s_pay, s_payst, s_zfill = k.sem("pay"), k.dma("payst"), k.dmas("zfill")

        LEVELS = 15

        def first_unit(n):
            return n * LOAD + (n > 0)

        def feat_load(eng, n):
            cols = slice(first_unit(n) * UNIT, first_unit(n + 1) * UNIT)
            eng.dma_start(feat[:, n % 2, 0:cols.stop - cols.start], a["feat_parts"][:, cols]).then_inc(s_feat[n % 2], 16)

        def over_pairs(eng, first, pairs, unit):
            if pairs == 1:
                unit(first, 1)
                unit(first + 1, 0)
            else:
                with eng.Fori(0, pairs) as i:
                    unit(2 * i + first, 1)
                    unit(2 * i + (first + 1), 0)

        with nc.Block() as block:
            @block.sync
            def _(sp):
                sp.dma_start(ends[:, 0, :], a["src"]).then_inc(s_ends, 16)
                sp.dma_start(ends[:, 1, :], a["dst"]).then_inc(s_ends, 16)
                sp.dma_start(wb[0:FEATS, :], a["L0_gnn_W1"]).then_inc(s_wb, 16)
                sp.dma_start(wb[FEATS:FEATS + 1, :], a["L0_gnn_b1"].rearrange("(a n) -> a n", a=1)).then_inc(s_wb, 16)
                sp.dma_start(attr[:, :], a["edge_attr_T"].rearrange("f (q n) -> (f q) n", q=SPLIT)).then_inc(s_attr, 16)
                sp.dma_start(w2[:, :], a["L0_gnn_W2"].rearrange("p n -> n p").to_broadcast([P, HID])).then_inc(s_weights, 16)
                sp.dma_start(b2[:, :], a["L0_gnn_b2"].rearrange("(a n) -> a n", a=1).to_broadcast([P, 1])).then_inc(s_weights, 16)
                sp.dma_start(dst_q[:, :, :], a["dst"].rearrange("p f -> (p f)")[0:EDGES]
                             .rearrange("(h q c) -> q h c", q=HALF, c=P)).then_inc(s_dstq, 16)
                sp.wait_ge(s_ones, 1)
                ones = PARTS * PARTS * FEATS
                sp.dma_start(a["feat_parts"][ones:K, :].rearrange("f (q n) -> (f q) n", q=SPLIT), parts[:, PARTS, :]).then_inc(s_parts, 16)
                for i in range(PARTS):
                    sp.wait_ge(s_part, 2 * i + 1)
                    for j in range(PARTS):
                        row = (i * PARTS + j) * FEATS
                        sp.dma_start(a["feat_parts"][row:row + FEATS, :].rearrange("f (q n) -> (f q) n", q=SPLIT),
                                     parts[:, i, :]).then_inc(s_parts, 16)
                sp.wait_ge(s_parts, 16 * (PARTS * PARTS + 1))
                feat_load(sp, 0)
                feat_load(sp, 1)
                step = ROWS // 10
                for n in range(10):
                    if n >= 2:
                        sp.wait_ge(s_x[n % 2], 16 * (n // 2))
                    sp.dma_start(keep["x"][:, n * step * D:(n + 1) * step * D],
                                 a["x"][0:MAIN, :].rearrange("(p j) d -> p (j d)", p=P)[:, n * step * D:(n + 1) * step * D]
                                 ).then_inc(s_x[n % 2], 16)
                sp.wait_ge(s_xtail, 1)
                sp.dma_start(keep["x"][0:TAIL, ROWS * D:(ROWS + 1) * D], a["x"][MAIN:N, :]).then_inc(s_x[0], 16)
                sp.wait_ge(s_none, 1)
                for n in range(2):
                    for at in (0, SORT + 1):
                        sp.dma_start(a["targets"][n:n + 1, at:at + 1], none[0:1, 0:1]).then_inc(s_pad, 16)
                sp.wait_ge(s_zero, 1)
                w = ROWS * D // FILLS
                flat = a["agg0"][0:MAIN, :].rearrange("(p j) d -> p (j d)", p=P)
                for n in range(FILLS):
                    if n >= 2:
                        sp.wait_ge(s_zfill[n % 2], 16 * (n // 2))
                    sp.dma_start(flat[:, n * w:(n + 1) * w], keep["zeros"][:, :]).then_inc(s_zfill[n % 2], 16)
                sp.dma_start(a["agg0"][MAIN:N, :], keep["zeros"][0:TAIL, 0:D]).then_inc(s_zfill[0], 16)
                sp.wait_ge(s_tgt, 2)
                for n in range(2):
                    sp.dma_start(a["targets"][n, 1:SORT + 1].rearrange("(p f) -> p f", f=COLS),
                                 tgt[:, n, :]).then_inc(s_pad, 16)
                sp.wait_ge(s_pad, 16 * 6)
                for n in range(2):
                    sp.dma_start(nxt[:, n, :], a["targets"][n, 2:SORT + 2].rearrange("(p f) -> p f", f=COLS)).then_inc(s_near, 16)
                    sp.dma_start(prv[:, n, :], a["targets"][n, 0:SORT].rearrange("(p f) -> p f", f=COLS)).then_inc(s_near, 16)
                sp.wait_ge(s_same, 1)
                for n in range(2):
                    sp.dma_start(a["same"][n, :].rearrange("(p f) -> p f", f=COLS), same[:, n, :]).then_inc(s_store, 16)
                for s in range(2):
                    sp.wait_ge(s_x[s], 16 * (5 + (s == 0)))
                    sp.wait_ge(s_zfill[s], 16 * (FILLS // 2 + (s == 0)))
                sp.wait_ge(s_store, 32)

            @block.gpsimd
            def _(pool):
                pool.iota(place[:, :], pattern=[[1, COLS]], base=0, channel_multiplier=COLS).then_inc(s_const, 1)
                pool.iota(part_i[:, :], pattern=[[0, 1]], base=0, channel_multiplier=1).then_inc(s_const, 1)
                pool.memset(parts[:, PARTS, :], 1.0).then_inc(s_ones, 1)
                for i in range(1, PARTS):
                    for n, (whole, left, part) in enumerate(((attr, rest, parts), (wb, wb_rest, wb_parts))):
                        pool.wait_ge(s_part, 2 * i - 1 + n)
                        pool.tensor_tensor(left, whole if i == 1 else left, part[:, i - 1, :], ALU.subtract).then_inc(s_left, 1)
                pool.memset(keep["ident"][:, :], 0.0).then_inc(s_ident, 1)
                pool.wait_ge(s_ident, 1)
                pool.affine_select(out=keep["ident"][:, :], in_=keep["ident"][:, :], compare_op=ALU.not_equal,
                                   fill=1.0, base=0, pattern=[[-1, P]], channel_multiplier=1).then_inc(s_ident, 1)
                pool.memset(keep["x"][:, ROWS * D:(ROWS + 1) * D], 0.0).then_inc(s_xtail, 1)
                pool.memset(keep["zeros"][:, :], 0.0).then_inc(s_zero, 1)
                pool.memset(none[:, :], -1).then_inc(s_none, 1)
                pool.wait_ge(s_dstq, 16)
                pool.tensor_copy(pay[:, :, :, 0], dst_q[:, :, :]).then_inc(s_pay, 1)
                pool.wait_ge(s_weights, 32)

                def unit(m, s):
                    pool.wait_ge(s_relu, m + 1)
                    v = hid[:, s, :].rearrange("p (q n) -> p q n", n=HID)
                    pool.tensor_tensor(v, v, w2[:, :].unsqueeze(1).to_broadcast([P, UT, HID]), ALU.mult).then_inc(s_mul, 1)
                unit(0, 0)
                over_pairs(pool, 1, UNITS // 2, unit)
                pool.wait_ge(s_pay, 2)
                pool.dma_start(a["payload"][:, :].rearrange("(h q c) two -> q h (c two)", q=HALF, c=P),
                               pay[:, :, :, :].rearrange("q h c two -> q h (c two)")).then_inc(s_payst, 16)
                pool.wait_ge(s_payst, 16)

            @block.tensor
            def _(pe):
                pe.wait_ge(s_ident, 2)

                def turns(cur, dst):
                    pe.wait_ge(s_key, cur)
                    for arr in range(2):
                        for h in range(2):
                            last = pe.transpose(turn[:, arr, h, :], dst[:, arr, h * P:(h + 1) * P], keep["ident"][:, :])
                    last.then_inc(s_turn, 1)

                def unit_of(n):
                    def unit(m, s):
                        wait(pe, s_relu, m - 1)
                        for q in range(UT):
                            at = (m - first_unit(n)) * UNIT + q * P
                            last = pe.matmul(psh[s][:, q * HID:(q + 1) * HID], feat[:, n % 2, bass.ds(at, P)], w1[:, :],
                                             start=True, stop=True)
                        last.then_inc(s_hid, 1)
                    return unit

                pe.wait_ge(s_w1, 16 * (PARTS + 1))
                pe.wait_ge(s_feat[0], 16)
                for m in range(3):
                    unit_of(0)(m, m % 2)
                over_pairs(pe, 3, LOAD // 2 - 1, unit_of(0))
                for t, (cur, b) in enumerate(k.turn_points):
                    turns(cur, keys[b])
                    n = 1 + t // 2
                    if t % 2 == 0:
                        pe.wait_ge(s_feat[n % 2], 16 * (n // 2 + 1))
                        over_pairs(pe, first_unit(n), 1, unit_of(n))
                    else:
                        over_pairs(pe, first_unit(n) + 2, LOAD // 2 - 1, unit_of(n))
                pe.wait_ge(s_wcol, 1)
                for h in range(2):
                    last = pe.transpose(turn3[0:HALF, 0, h, :], wcol[:, h * HALF:(h + 1) * HALF], keep["ident"][:, :])
                last.then_inc(s_wturn, 1)
                for n in range(5):
                    pe.wait_ge(s_fidx, n + 1)
                    if n == 4:
                        pe.wait_ge(s_pay, 2)
                    for h in range(2):
                        bank = (turn, turn2, turn3)[n // 2]
                        last = pe.transpose(bank[:, n % 2, h, :], fidx[:, n, h * P:(h + 1) * P], keep["ident"][:, :])
                last.then_inc(s_turn, 1)

            @block.scalar
            def _(act):
                act.wait_ge(s_attr, 16)
                act.wait_ge(s_wb, 32)
                for i in range(PARTS):
                    for n, (whole, left, part) in enumerate(((attr, rest, parts), (wb, wb_rest, wb_parts))):
                        wait(act, s_left, 2 * i - 1 + n if i > 0 else 0)
                        act.activation(part[:, i, :], left if i > 0 else whole, ACT.Copy).then_inc(s_part, 1)
                act.wait_ge(s_part, 2 * PARTS)
                for j in range(PARTS):
                    act.dma_start(a["w1_parts"][j * FEATS:(j + 1) * FEATS, :], wb_parts[0:FEATS, j, :]).then_inc(s_wparts, 16)
                    act.dma_start(a["b1_parts"][j:j + 1, :], wb_parts[FEATS:FEATS + 1, j, :]).then_inc(s_wparts, 16)
                act.wait_ge(s_wparts, 16 * 2 * PARTS)
                rows = PARTS * FEATS
                for i in range(PARTS):
                    act.dma_start(w1[i * rows:(i + 1) * rows, :], a["w1_parts"]).then_inc(s_w1, 16)
                act.dma_start(w1[PARTS * rows:K, :], a["b1_parts"]).then_inc(s_w1, 16)

                def sums(m, s):
                    act.wait_ge(s_mul, m + 1)
                    for q in range(UT):
                        v = hid[:, s, q * HID:(q + 1) * HID]
                        act.activation(v, v, ACT.Copy, accum_out=wcol[:, bass.ds(m * UT + q, 1)]).then_inc(s_sum, 1)

                def unit(m, s):
                    if not isinstance(m, int) or m >= 2:
                        sums(m - 2, s)
                        act.wait_ge(s_sum, (m - 1) * UT)
                    act.wait_ge(s_hid, m + 1)
                    act.activation(hid[:, s, :], psh[s][:, :], ACT.Relu).then_inc(s_relu, 1)
                unit(0, 0)
                unit(1, 1)
                unit(2, 0)
                over_pairs(act, 3, LOAD // 2 - 1, unit)
                for n in range(1, LOADS):
                    if n < LOADS - 1:
                        act.wait_ge(s_hid, first_unit(n))
                        feat_load(act, n + 1)
                    over_pairs(act, first_unit(n), LOAD // 2, unit)
                sums(UNITS - 2, 1)
                sums(UNITS - 1, 0)
                act.wait_ge(s_sum, TILES)
                act.activation(wcol[:, :], wcol[:, :], ACT.Sigmoid, bias=b2[:, 0:1]).then_inc(s_wcol, 1)
                act.wait_ge(s_wturn, 1)
                act.activation(pay[:, :, :, 1].bitcast(F32), turn3[0:HALF, 0, :, :], ACT.Copy).then_inc(s_pay, 1)

            @block.vector
            def _(dve):
                ch = [0]

                def link(ins):
                    ch[0] += 1
                    ins.then_inc(s_key, 1)

                def settle():
                    dve.wait_ge(s_key, ch[0])

                dve.wait_ge(s_ends, 32)
                dve.wait_ge(s_const, 2)
                ki = [b[:, :, :].bitcast(I32) for b in keys]
                link(dve.tensor_scalar(tmp[:, :], ends[:, 0, :], float(SRC_OFF), None, ALU.add))
                link(dve.tensor_scalar(nxt[:, 1, :], ends[:, 1, :], float(DST_HALF), float(DST_HIGH - DST_LOW), ALU.is_ge, ALU.mult))
                link(dve.tensor_scalar(part_i[:, :], part_i[:, :], 1, None, ALU.bitwise_and))
                settle()
                link(dve.tensor_scalar(nxt[:, 0, :], tmp[:, :], 15, None, ALU.logical_shift_left))
                link(dve.scalar_tensor_tensor(prv[:, 1, :], ends[:, 1, :], float(DST_LOW), nxt[:, 1, :], ALU.add, ALU.add))
                link(dve.tensor_scalar(sign[:, :], part_i[:, :], -2.0, 1.0, ALU.mult, ALU.add))
                settle()
                link(dve.tensor_tensor(ki[0][:, 0, :], nxt[:, 0, :], place[:, :], ALU.bitwise_or))
                link(dve.tensor_scalar(prv[:, 0, :], prv[:, 1, :], 16, None, ALU.logical_shift_left))
                settle()
                link(dve.tensor_tensor(ki[0][:, 1, :], prv[:, 0, :], ends[:, 0, :], ALU.bitwise_or))
                settle()
                cur = 0

                def compare(cur, d):
                    x = keys[cur][:, :, :].rearrange("p a (b t k) -> p (a b) t k", t=2, k=d)
                    y = keys[1 - cur][:, :, :].rearrange("p a (b t k) -> p (a b) t k", t=2, k=d)
                    link(dve.tensor_tensor(y[:, :, 0, :], x[:, :, 0, :], x[:, :, 1, :], ALU.min))
                    link(dve.tensor_tensor(y[:, :, 1, :], x[:, :, 0, :], x[:, :, 1, :], ALU.max))
                    settle()
                    return 1 - cur

                def negate(cur, width, lo, hi):
                    v = keys[cur][:, :, :].rearrange("p a (b m) -> p (a b) m", m=width)[:, :, lo:hi]
                    link(dve.tensor_scalar(v, v, -1.0, None, ALU.mult))
                    settle()

                points = []

                def turn_over(cur):
                    points.append((ch[0], cur))
                    dve.wait_ge(s_turn, len(points))
                    link(dve.tensor_copy(keys[1 - cur][:, :, :], turn[:, :, :, :].rearrange("p a h m -> p a (h m)")))
                    settle()
                    return 1 - cur

                for m in range(1, LEVELS + 1):
                    if m == 1:
                        negate(cur, 4, 2, 4)
                    elif m <= 7:
                        negate(cur, 2 << m, 1 << (m - 1), 3 << (m - 1))
                    elif m == 8:
                        for f0, sg in ((0, 1.0), (P, -1.0)):
                            v = keys[cur][:, :, f0:f0 + P]
                            link(dve.tensor_scalar(v, v, sign[:, 0:1], sg, ALU.mult, ALU.mult))
                        settle()
                    if m <= 8:
                        for j in reversed(range(m)):
                            cur = compare(cur, 1 << j)
                        continue
                    cur = turn_over(cur)
                    if m < LEVELS:
                        negate(cur, 2 << (m - 8), 1 << (m - 9), 3 << (m - 9))
                    else:
                        negate(cur, P, P // 2, P)
                    for j in reversed(range(8, m)):
                        cur = compare(cur, 1 << (j - 8))
                    cur = turn_over(cur)
                    for j in reversed(range(8)):
                        cur = compare(cur, 1 << j)
                assert points == k.turn_points, points

                v = ki[cur]
                fr = ki[1 - cur]
                link(dve.tensor_scalar(tmp[:, :], v[:, 0, :], 15, None, ALU.logical_shift_right))
                link(dve.tensor_scalar(fr[:, 1, :], v[:, 1, :], 16, None, ALU.logical_shift_right))
                link(dve.tensor_scalar(fr[:, 0, :], v[:, 0, :], (1 << 15) - 1, None, ALU.bitwise_and))
                settle()
                dve.tensor_scalar(tgt[:, 0, :], tmp[:, :], float(-SRC_OFF), None, ALU.add).then_inc(s_tgt, 1)
                dve.wait_ge(s_sum, TILES)
                link(dve.tensor_scalar(nxt[:, 1, :], fr[:, 1, :], 32768.0, float(DST_HIGH - DST_LOW), ALU.is_ge, ALU.mult))
                dve.tensor_scalar(fidx[:, 0, :], fr[:, 0, :], float(E - 1), None, ALU.min).then_inc(s_fidx, 1)
                settle()
                dve.scalar_tensor_tensor(tgt[:, 1, :], fr[:, 1, :], float(-DST_HIGH), nxt[:, 1, :], ALU.add, ALU.add).then_inc(s_tgt, 1)
                dve.wait_ge(s_fidx, 1)
                link(dve.tensor_scalar(fr[:, 0, :], v[:, 1, :], (1 << 16) - 1, None, ALU.bitwise_and))
                settle()
                dve.wait_ge(s_tgt, 2)
                dve.tensor_scalar(fidx[:, 1, :], fr[:, 0, :], float(N - 1), None, ALU.min).then_inc(s_fidx, 1)
                dve.wait_ge(s_near, 64)
                dve.tensor_tensor(same[:, :, :], tgt[:, :, :], prv[:, :, :], ALU.is_equal).then_inc(s_same, 1)
                dve.wait_ge(s_same, 1)
                link(dve.tensor_tensor(prv[:, :, :], tgt[:, :, :], nxt[:, :, :], ALU.is_equal))
                settle()
                for n in range(2):
                    dve.scalar_tensor_tensor(fidx[:, 2 + n, :], prv[:, n, :], float(SKIP), tgt[:, n, :],
                                             ALU.mult, ALU.add).then_inc(s_fidx, 1)
                dve.tensor_copy(fidx[:, 4, :], tgt[:, 1, :]).then_inc(s_fidx, 1)
                dve.wait_ge(s_turn, len(points) + 1)
                half = TILES // 2
                for n in range(5):
                    bank = (turn, turn2, turn3)[n // 2]
                    out = keep["index"][:, n, :] if n < 4 else keep["dst"][:, :]
                    for h in range(2):
                        dve.tensor_copy(out[:, h:TILES:2], bank[:, n % 2, h, 0:half]).then_inc(s_fidx, 1)


def turn_points():
    out, ch, cur = [], 9, 0
    for m in range(1, 16):
        if m <= 7:
            ch += 1
        elif m == 8:
            ch += 2
        if m <= 8:
            ch += 2 * m
            cur ^= m & 1
            continue
        out.append((ch, cur))
        ch, cur = ch + 2 + 2 * (m - 8), cur ^ 1 ^ (m & 1)
        out.append((ch, cur))
        ch, cur = ch + 1 + 16, cur ^ 1
    return out


class Norm:

    SUM, DIFF, SQ, M2, VAR, STD, RSTD, SHIFT = range(8)
    STATS = G + 4
    SCALES = 1

    def __init__(self, sb, name):
        self.bn = [sb(f"{name}_bn{s}", [P, G, 6]) for s in range(2)]
        self.st = [sb(f"{name}_st{s}", [P, 8, G]) for s in range(2)]


def ln_rows(nc, ch, norm, g, tile):
    if g.live:
        for j in range(g.w):
            ch.note(nc.vector.bn_stats(norm.bn[g.slot][:, j, :], tile(j)))


def ln_sums(nc, ch, norm, g):
    if g.live:
        bn, st, w = norm.bn[g.slot], norm.st[g.slot], g.w
        ch.settle()
        ch.note(nc.vector.tensor_tensor(st[:, norm.SUM, 0:w], bn[:, 0:w, 1], bn[:, 0:w, 4], ALU.add))
        ch.note(nc.vector.tensor_tensor(st[:, norm.DIFF, 0:w], bn[:, 0:w, 1], bn[:, 0:w, 4], ALU.subtract))
        ch.note(nc.vector.tensor_tensor(st[:, norm.M2, 0:w], bn[:, 0:w, 2], bn[:, 0:w, 5], ALU.add))


def ln_square(nc, ch, norm, g):
    if g.live:
        st, w = norm.st[g.slot], g.w
        ch.settle()
        ch.note(nc.vector.tensor_tensor(st[:, norm.SQ, 0:w], st[:, norm.DIFF, 0:w], st[:, norm.DIFF, 0:w], ALU.mult))


def ln_var(nc, ch, norm, g, done):
    if g.live:
        st, w = norm.st[g.slot], g.w
        ch.settle()
        nc.vector.scalar_tensor_tensor(st[:, norm.VAR, 0:w], st[:, norm.SQ, 0:w], D / 4, st[:, norm.M2, 0:w],
                                       ALU.mult, ALU.add).then_inc(done, 1)


def ln_stats(nc, ch, norm, g, tile, done):
    ln_rows(nc, ch, norm, g, tile)
    ln_sums(nc, ch, norm, g)
    ln_square(nc, ch, norm, g)
    ln_var(nc, ch, norm, g, done)


def ln_sqrt(nc, norm, g, eps):
    st, w = norm.st[g.slot], g.w
    return nc.scalar.activation(st[:, norm.STD, 0:w], st[:, norm.VAR, 0:w], ACT.Sqrt, bias=eps[:, 0:1], scale=1.0 / D)


def ln_inverse(nc, ch, norm, g):
    st, w = norm.st[g.slot], g.w
    ch.note(nc.vector.reciprocal(st[:, norm.RSTD, 0:w], st[:, norm.STD, 0:w]))


def ln_shift(nc, ch, norm, g):
    st, w = norm.st[g.slot], g.w
    ch.settle()
    return nc.vector.scalar_tensor_tensor(st[:, norm.SHIFT, 0:w], st[:, norm.SUM, 0:w], -0.5, st[:, norm.RSTD, 0:w],
                                          ALU.mult, ALU.mult)


def ln_scales(nc, ch, norm, g):
    ln_inverse(nc, ch, norm, g)
    return ln_shift(nc, ch, norm, g)


def ln_apply(nc, norm, g, func, out, tile, factors=None, tiles=None):
    st = norm.st[g.slot]
    by, add = (st[:, norm.RSTD, :], st[:, norm.SHIFT, :]) if factors is None else (factors[g.slot][:, 0, :], factors[g.slot][:, 1, :])
    for j in range(g.w) if tiles is None else tiles:
        last = nc.scalar.activation(out(j), tile(j), func, bias=add[:, j:j + 1], scale=by[:, j:j + 1])
    return last


def x_tile(keep, g, j):
    return keep["x"][:, bass.ds(g.num * (G * D) + j * D, D)]


def first_stage(k, a, keep):
    nc = k.nc
    k.stage = "first"
    with ExitStack() as mem:
        def sb(name, shape, dt=F32):
            return mem.enter_context(nc.sbuf_tensor(f"{k.stage}_{name}_sb", shape, dt))

        gidx = [sb(f"gidx{s}", [P, CT], I32) for s in range(2)]
        gbuf = [sb(f"gbuf{s}", [P, CT, 2], I32) for s in range(2)]
        iota_i = sb("iota_i", [P, ROWS + 1], I32)
        iota_f = sb("iota_f", [P, ROWS + 1])
        iota_lo = sb("iota_lo", [P, P], BF16)
        hi, lo, t0, t1 = (sb(n, [P, TILES]) for n in ("hi", "lo", "t0", "t1"))
        HOT = TILES // GROUPS
        assert GROUPS * HOT + 1 == TILES
        hot_lo = [sb(f"hot_lo{s}", [P, P], BF16) for s in range(HOT)]
        hot_hi = [sb(f"hot_hi{s}", [P, ROWS + 1], BF16) for s in range(HOT)]
        c1 = sb("c1", [P, ROWS + 1])
        norm = Norm(sb, "norm")
        hout = [sb(f"hout{s}", [P, G, D]) for s in range(2)]
        count = mem.enter_context(nc.psum_tensor("first_count_ps", [P, 512], F32))

        s_idx, s_out, s_alone = k.sem("idx"), k.sem("out"), k.sem("alone")
        s_gath = k.dmas("gath")
        s_iota, s_hot, s_used = k.sem("iota"), k.sem("hot"), k.sem("used")
        s_dve, s_dve2, s_c1, s_sq, s_eps = k.sem("dve"), k.sem("dve2"), k.sem("c1"), k.sem("sq"), k.sem("eps")
        s_var, s_std, s_scale, s_norm = k.sem("var"), k.sem("std"), k.sem("scale"), k.sem("norm")
        s_store, s_zfill = k.dmas("store"), k.dmas("zfill")

        with nc.Block() as block:
            @block.gpsimd
            def _(pool):
                pool.iota(iota_i[:, :], pattern=[[1, ROWS + 1]], base=0, channel_multiplier=0).then_inc(s_iota, 1)
                pool.memset(keep["eps"][:, 0:1], LN_EPS).then_inc(s_eps, 1)
                pool.memset(keep["eps"][:, 1:2], MSG_EPS)

                def gather(i, s):
                    pool.tensor_copy(gidx[s][:, :], keep["index"][:, 0, bass.ds((2 * i + s) * CT, CT)]).then_inc(s_idx, 1)
                    pool.wait_ge(s_idx, 2 * i + s + 1)
                    alone(pool, s_alone)
                    for j in range(CT):
                        pool.indirect_dma_start(gbuf[s][:, j, :], None, a["payload"],
                                                bass.IndirectOffsetOnAxis(gidx[s][:, j:j + 1], 0)).then_inc(s_gath[s], 16)

                def keep_it(i, s):
                    pool.wait_ge(s_gath[s], (i + 1) * (16 * CT))
                    pool.tensor_copy(keep["payload"][:, bass.ds((2 * i + s) * CT, CT), :], gbuf[s][:, :, :]).then_inc(s_out, 1)
                    pool.wait_ge(s_out, 2 * i + s + 1)
                gather(0, 0)
                with pool.Fori(0, CHUNKS // 2 - 1) as i:
                    gather(i, 1)
                    keep_it(i, 0)
                    gather(i + 1, 0)
                    keep_it(i, 1)
                gather(CHUNKS // 2 - 1, 1)
                keep_it(CHUNKS // 2 - 1, 0)
                keep_it(CHUNKS // 2 - 1, 1)

            @block.tensor
            def _(pe):
                def add(g, s, start, stop):
                    pe.wait_ge(s_hot, (g.num * HOT + s + 1) * 2)
                    pe.matmul(count[:, 0:ROWS + 1], hot_lo[s][:, :], hot_hi[s][:, :], start=start, stop=stop).then_inc(s_used, 1)

                def step(g):
                    if g.live:
                        for s in range(1 if g.tail else HOT):
                            add(g, s, g.known and g.num == 0 and s == 0, g.tail)
                over_groups(pe, step)

            @block.vector
            def _(dve):
                ch = Chain(dve, s_dve)
                dve.wait_ge(s_iota, 1)
                magic = 1.5 * 2 ** 23
                n = keep["dst"]
                ch.note(dve.tensor_copy(iota_f[:, :], iota_i[:, :]))
                ch.note(dve.tensor_copy(iota_lo[:, :], iota_i[:, 0:P]))
                ch.note(dve.tensor_scalar(t0[:, :], n[:, :], -(ROWS - 1) / 2, 1.0 / ROWS, ALU.add, ALU.mult))
                ch.settle()
                ch.link(dve.tensor_scalar(t1[:, :], t0[:, :], magic, None, ALU.add))
                ch.link(dve.tensor_scalar(lo[:, :], t1[:, :], -magic, None, ALU.add))
                ch.link(dve.scalar_tensor_tensor(hi[:, :], lo[:, :], float(-ROWS), n[:, :], ALU.mult, ALU.add))
                ch.note(dve.tensor_tensor(t0[:, :], hi[:, :], lo[:, :], ALU.subtract))
                ch.note(dve.tensor_scalar(t1[:, :], n[:, :], float(MAIN), None, ALU.is_ge))
                ch.settle()
                ch.link(dve.tensor_tensor(t0[:, :], t0[:, :], t1[:, :], ALU.mult))
                ch.link(dve.tensor_tensor(lo[:, :], lo[:, :], t0[:, :], ALU.add))
                ch.link(dve.tensor_scalar(t0[:, :], hi[:, :], -1.0, float(ROWS), ALU.mult, ALU.add))
                ch.link(dve.tensor_tensor(t0[:, :], t0[:, :], t1[:, :], ALU.mult))
                ch.link(dve.tensor_tensor(hi[:, :], hi[:, :], t0[:, :], ALU.add))
                ch.link(dve.tensor_scalar(t0[:, :], n[:, :], float(N), 1000.0, ALU.is_ge, ALU.mult))
                ch.link(dve.tensor_tensor(lo[:, :], lo[:, :], t0[:, :], ALU.add))
                ch.link(dve.tensor_scalar(t0[:, :], n[:, :], float(N), 1000.0, ALU.is_ge, ALU.mult))

                per = Norm.STATS
                base = ch.k

                def hots(g, slots):
                    for s in slots:
                        if g.live and not (g.tail and s > 0):
                            wait(dve, s_used, (g.num - 1) * HOT + s + 1)
                            t = g.num * HOT + s
                            dve.tensor_scalar(hot_lo[s][:, :], iota_lo[:, :], lo[:, bass.ds(t, 1)], None, ALU.is_equal).then_inc(s_hot, 1)
                            dve.tensor_scalar(hot_hi[s][:, :], iota_f[:, :], hi[:, bass.ds(t, 1)], None, ALU.is_equal).then_inc(s_hot, 1)

                def step(g):
                    hots(g, range(1))
                    p = g + -1
                    if p.live:
                        dve.wait_ge(s_std, p.num + 1)
                        wait(dve, s_norm, p.num - 1)
                        scales = Chain(dve, s_dve2, p.num)
                        ln_inverse(nc, scales, norm, p)
                    hots(g, range(1, 2))
                    if p.live:
                        ln_shift(nc, scales, norm, p).then_inc(s_scale, 1)
                    if g.live:
                        wait(dve, s_scale, g.num - 1)
                    stats = Chain(dve, s_dve, base + g.num * per)
                    ln_rows(nc, stats, norm, g, lambda j: x_tile(keep, g, j))
                    hots(g, range(2, HOT))
                    ln_sums(nc, stats, norm, g)
                    ln_square(nc, stats, norm, g)
                    ln_var(nc, stats, norm, g, s_var)
                over_groups(dve, step)
                ch = Chain(dve, s_dve, base + GROUPS * per + Norm.STATS - (G - 1))
                dve.wait_ge(s_used, TILES)
                ch.link(dve.tensor_copy(keep["cnt"][:, :], count[:, 0:ROWS + 1]))
                dve.tensor_scalar(c1[:, :], keep["cnt"][:, :], 1.0, None, ALU.add).then_inc(s_c1, 1)
                ch.link(dve.tensor_scalar(keep["deg"][:, :], keep["cnt"][:, :], 1.0, None, ALU.max))
                ch.link(dve.reciprocal(keep["inv_deg"][:, :], keep["deg"][:, :]))
                dve.wait_ge(s_sq, 1)
                ch.link(dve.reciprocal(keep["dinv"][:, :], keep["sqrt_c1"][:, :]))

            @block.scalar
            def _(act):
                act.wait_ge(s_eps, 1)

                def step(g):
                    p = g + -1
                    if p.live:
                        act.wait_ge(s_var, p.num + 1)
                        ln_sqrt(nc, norm, p, keep["eps"]).then_inc(s_std, 1)
                    p = g + -2
                    if p.live:
                        act.wait_ge(s_scale, p.num + 1)
                        wait(act, s_store[p.slot], p.uses * 16)
                        ln_apply(nc, norm, p, ACT.Relu, lambda j: hout[p.slot][:, j, :],
                                 lambda j: x_tile(keep, p, j)).then_inc(s_norm, 1)
                over_groups(act, step)
                act.wait_ge(s_c1, 1)
                act.activation(keep["sqrt_c1"][:, :], c1[:, :], ACT.Sqrt).then_inc(s_sq, 1)

            @block.sync
            def _(sp):
                def step(g):
                    if g.live:
                        rows = TAIL if g.tail else P
                        sp.dma_start(group_rows(a["agg"], g), keep["zeros"][0:rows, 0:g.w * D]).then_inc(s_zfill[g.slot], 16)
                        sp.wait_ge(s_norm, g.num + 1)
                        sp.dma_start(group_rows(a["table"], g), group_buf(hout[g.slot], g)).then_inc(s_store[g.slot], 16)
                over_groups(sp, step)
                for s in range(2):
                    sp.wait_ge(s_zfill[s], 16 * ((GROUPS + 1) // 2))
                    sp.wait_ge(s_store[s], 16 * ((GROUPS + 1) // 2))


def over_chunks(eng, step):
    for c in range(4):
        step(Chunk(0, c))
    with eng.Fori(0, (CHUNKS - 6) // 2) as i:
        step(Chunk(i, 4))
        step(Chunk(i, 5))
    for c in range(CHUNKS - 2, CHUNKS + 2):
        step(Chunk(0, c))


def alone(eng, sem):
    eng.sem_inc(sem, 1)


def edge_stage(k, a, keep, layer):
    nc = k.nc
    k.stage = f"edges{layer}"
    by = 0 if layer == 0 else 1
    soft = layer == 3
    agg = a["agg0"] if layer == 0 else a["agg"]
    with ExitStack() as mem:
        def sb(name, shape, dt=F32):
            return mem.enter_context(nc.sbuf_tensor(f"{k.stage}_{name}_sb", shape, dt))

        def two(name, shape, dt=F32):
            return [sb(f"{name}{s}", shape, dt) for s in range(2)]

        gidx, sidx = two("gidx", [P, CT], I32), two("sidx", [P, CT], I32)
        K = D + 1 if layer == 1 else D
        rows = two("rows", [P, CT, K])
        same = two("same", [K, CW], BF16)
        sums = two("sums", [K, CW]) if not soft else None
        back = two("back", [P, CT, D])
        weight = sb("weight", [K, D]) if layer == 1 else None
        turned = [mem.enter_context(nc.psum_tensor(f"{k.stage}_turned{s}_ps", [K, 1024], F32)) for s in range(2)]
        again = [mem.enter_context(nc.psum_tensor(f"{k.stage}_again{s}_ps", [P, 2, 512], F32)) for s in range(2)]
        BANK = 4
        BANKS = ((0, 0, BANK), (1, BANK, CT - BANK))
        if soft:
            most = sb("most", [D, CW + 1])
            logit = sb("logit", [D, CW])
            decay = sb("decay", [D, CW])
            ex = sb("ex", [D, CW])
            den, num = sb("den", [D, CW]), sb("num", [D, CW])
            inverse = sb("inverse", [P, CT, D])
            carry = sb("carry", [D, 2])

        s_gidx, s_sidx, s_alone = k.sem("gidx"), k.sem("sidx"), k.sem("alone")
        s_gath, s_scat, s_same = k.dmas("gath"), k.dmas("scat"), k.dmas("same")
        s_rows, s_turned, s_sums, s_again, s_back = k.sem("rows"), k.sem("turned"), k.sem("sums"), k.sem("again"), k.sem("back")
        if layer == 1:
            s_weight, s_ones = k.dma("weight"), k.sem("ones")
        if soft:
            s_logit, s_arg, s_exp, s_dve, s_inv = k.sem("logit"), k.sem("arg"), k.sem("exp"), k.sem("dve"), k.sem("inv")

        with nc.Block() as block:
            @block.gpsimd
            def _(pool):
                if layer == 1:
                    for s in range(2):
                        pool.memset(rows[s][:, :, D:K], 1.0).then_inc(s_ones, 1)

                def step(c):
                    if c.live:
                        s = c.slot
                        wait(pool, s_turned, c.num - 1)
                        pool.wait_ge(s_gidx, c.num + 1)
                        alone(pool, s_alone)
                        for j in range(CT):
                            pool.indirect_dma_start(rows[s][:, j, 0:D], None, a["table"],
                                                    bass.IndirectOffsetOnAxis(gidx[s][:, j:j + 1], 0)).then_inc(s_gath[s], 16)
                    c = c + -2
                    if c.live:
                        s = c.slot
                        pool.wait_ge(s_sidx, c.num + 1)
                        pool.wait_ge(s_back, c.num + 1)
                        alone(pool, s_alone)
                        for j in range(CT):
                            pool.indirect_dma_start(agg, bass.IndirectOffsetOnAxis(sidx[s][:, j:j + 1], 0),
                                                    back[s][:, j, :], None, bounds_check=N - 1,
                                                    oob_is_err=False).then_inc(s_scat[s], 16)
                over_chunks(pool, step)
                for s in range(2):
                    pool.wait_ge(s_scat[s], 16 * CT * CHUNKS // 2)

            @block.sync
            def _(sp):
                if layer == 1:
                    sp.dma_start(weight[0:D, :], a["L1_gnn_W"]).then_inc(s_weight, 16)
                    sp.dma_start(weight[D:K, :], a["L1_gnn_b"].rearrange("(a n) -> a n", a=1)).then_inc(s_weight, 16)

                def step(c):
                    if c.live:
                        wait(sp, s_sums, c.num - 1)
                        sp.dma_start(same[c.slot][:, :], a["same"][by:by + 1, bass.ds(c.num * CW, CW)].to_broadcast([K, CW])
                                     ).then_inc(s_same[c.slot], 16)
                over_chunks(sp, step)

            @block.tensor
            def _(pe):
                if layer == 1:
                    pe.wait_ge(s_weight, 32)
                    pe.wait_ge(s_ones, 2)

                def step(c):
                    if c.live:
                        if layer == 0:
                            pe.wait_ge(s_rows, c.num + 1)
                        else:
                            pe.wait_ge(s_gath[c.slot], (c.uses + 1) * (16 * CT))
                        wait(pe, s_logit if soft else s_sums, c.num - 1)
                        for j in range(CT):
                            last = pe.transpose(turned[c.slot][:, j * P:(j + 1) * P], rows[c.slot][:, j, :], keep["ident"][:, :])
                        last.then_inc(s_turned, 1)
                    c = c + -1
                    if c.live:
                        pe.wait_ge(s_sums, c.num + 1)
                        wait(pe, s_back, c.num if soft else c.num - 1)
                        for bank, of in ((again[0], num), (again[1], den)) if soft else ((again[c.slot], sums[c.slot]),):
                            for j in range(CT):
                                out = bank[:, j // BANK, (j % BANK) * D:(j % BANK + 1) * D]
                                tile = of[:, j * P:(j + 1) * P]
                                if layer == 1:
                                    last = pe.matmul(out, tile, weight[:, :], start=True, stop=True)
                                else:
                                    last = pe.transpose(out, tile, keep["ident"][0:D, 0:D])
                        last.then_inc(s_again, 1)
                over_chunks(pe, step)

            @block.scalar
            def _(act):
                def step(c):
                    if c.live and soft:
                        act.wait_ge(s_turned, c.num + 1)
                        wait(act, s_sums, c.num)
                        act.activation(logit[:, :], turned[c.slot][:, 0:CW], ACT.Identity,
                                       bias=keep["eps"][0:D, 1:2]).then_inc(s_logit, 1)
                        act.wait_ge(s_arg, c.num * 2 + 1)
                        act.activation(ex[:, :], ex[:, :], ACT.Exp).then_inc(s_exp, 1)
                        act.wait_ge(s_arg, c.num * 2 + 2)
                        act.activation(decay[:, :], decay[:, :], ACT.Exp).then_inc(s_exp, 1)
                    c = c + -1
                    if c.live and not soft:
                        act.wait_ge(s_again, c.num + 1)
                        wait(act, s_scat[c.slot], c.uses * (16 * CT))
                        for u, j0, m in BANKS:
                            last = act.activation(back[c.slot][:, j0:j0 + m, :].rearrange("p j d -> p (j d)"),
                                                  again[c.slot][:, u, 0:m * D], ACT.Copy)
                        last.then_inc(s_back, 1)
                over_chunks(act, step)

            @block.vector
            def _(dve):
                def gather_index(c):
                    if c.live:
                        wait(dve, s_gath[c.slot], c.uses * (16 * CT))
                        src = keep["payload"][:, c.tiles(), 0] if layer == 0 else keep["index"][:, 1, c.tiles()]
                        dve.tensor_copy(gidx[c.slot][:, :], src).then_inc(s_gidx, 1)

                def scatter_index(c):
                    if c.live:
                        wait(dve, s_scat[c.slot], c.uses * (16 * CT))
                        dve.tensor_copy(sidx[c.slot][:, :], keep["index"][:, 2 + by, c.tiles()]).then_inc(s_sidx, 1)

                gather_index(Chunk(0, 0))
                gather_index(Chunk(0, 1))
                if soft:
                    dve.memset(most[:, CW:CW + 1], 0.0).then_inc(s_dve, 1)
                    dve.memset(carry[:, :], 0.0).then_inc(s_dve, 1)

                def finish(c):
                    s = c.slot
                    dve.wait_ge(s_again, c.num + 1)
                    wait(dve, s_back, c.num)
                    for u, j0, m in BANKS:
                        dve.reciprocal(inverse[:, j0:j0 + m, :].rearrange("p j d -> p (j d)"), again[1][:, u, 0:m * D]).then_inc(s_inv, 1)
                    wait(dve, s_scat[s], c.uses * (16 * CT))
                    for u, j0, m in BANKS:
                        dve.wait_ge(s_inv, c.num * 2 + u + 1)
                        last = dve.tensor_tensor(back[s][:, j0:j0 + m, :].rearrange("p j d -> p (j d)"), again[0][:, u, 0:m * D],
                                                 inverse[:, j0:j0 + m, :].rearrange("p j d -> p (j d)"), ALU.mult)
                    last.then_inc(s_back, 1)

                def sum_up(c):
                    if not c.live:
                        if soft and (c + -1).live:
                            finish(c + -1)
                        return
                    s = c.slot
                    if layer == 0:
                        dve.wait_ge(s_gath[s], (c.uses + 1) * (16 * CT))
                        weight = keep["payload"][:, c.tiles(), 1:2].bitcast(F32).to_broadcast([P, CT, D])
                        dve.tensor_tensor(rows[s][:, :, :], rows[s][:, :, :], weight, ALU.mult).then_inc(s_rows, 1)
                    dve.wait_ge(s_same[s], (c.uses + 1) * 16)
                    if not soft:
                        dve.wait_ge(s_turned, c.num + 1)
                        wait(dve, s_again, c.num - 1)
                        before = sums[1 - s][:, CW - 1:CW]
                        if c.known and c.num == 0:
                            before = 0.0
                        else:
                            dve.wait_ge(s_sums, c.num)
                        dve.tensor_tensor_scan(sums[s][:, :], same[s][:, :], turned[s][:, 0:CW], before,
                                               ALU.mult, ALU.add).then_inc(s_sums, 1)
                        return
                    per = 8
                    ch = Chain(dve, s_dve, c.num * per + 2)
                    ch.settle()
                    ch.link(dve.tensor_copy(most[:, 0:1], most[:, CW:CW + 1]))
                    dve.wait_ge(s_logit, c.num + 1)
                    ch.link(dve.tensor_tensor_scan(most[:, 1:CW + 1], same[s][:, :], logit[:, :], most[:, 0:1], ALU.mult, ALU.max))
                    dve.tensor_tensor(ex[:, :], logit[:, :], most[:, 1:CW + 1], ALU.subtract).then_inc(s_arg, 1)
                    ch.link(dve.tensor_tensor(decay[:, :], most[:, 0:CW], same[s][:, :], ALU.mult))
                    dve.tensor_tensor(decay[:, :], decay[:, :], most[:, 1:CW + 1], ALU.subtract).then_inc(s_arg, 1)
                    indices(c)
                    if (c + -1).live:
                        finish(c + -1)
                    dve.wait_ge(s_exp, c.num * 2 + 1)
                    ch.note(dve.tensor_tensor(logit[:, :], logit[:, :], ex[:, :], ALU.mult))
                    dve.wait_ge(s_exp, c.num * 2 + 2)
                    ch.link(dve.tensor_tensor(decay[:, :], decay[:, :], same[s][:, :], ALU.mult))
                    wait(dve, s_again, c.num)
                    ch.note(dve.tensor_tensor_scan(den[:, :], decay[:, :], ex[:, :], carry[:, 0:1], ALU.mult, ALU.add))
                    dve.tensor_tensor_scan(num[:, :], decay[:, :], logit[:, :], carry[:, 1:2], ALU.mult, ALU.add).then_inc(s_sums, 1)
                    ch.settle()
                    ch.note(dve.tensor_copy(carry[:, 0:1], den[:, CW - 1:CW]))
                    dve.wait_ge(s_sums, c.num + 1)
                    ch.note(dve.tensor_copy(carry[:, 1:2], num[:, CW - 1:CW]))
                    assert ch.k == per, ch.k

                def indices(c):
                    gather_index(c + 2)
                    scatter_index(c + -1)

                def step(c):
                    sum_up(c)
                    if not (soft and c.live):
                        indices(c)
                over_chunks(dve, step)


def bcast(column, w):
    return column.unsqueeze(2).to_broadcast([P, w, D])


def node_cols(keep, name, g):
    return keep[name][:, g.tiles()]


def mean_stage(k, a, keep):
    nc = k.nc
    k.stage = "nodes1"
    with ExitStack() as mem:
        def sb(name, shape, dt=F32):
            return mem.enter_context(nc.sbuf_tensor(f"{k.stage}_{name}_sb", shape, dt))

        agg = [sb(f"agg{s}", [P, G, D]) for s in range(2)]
        y = [sb(f"y{s}", [P, G, D]) for s in range(2)]
        hout = [sb(f"hout{s}", [P, G, D]) for s in range(2)]
        scale = [sb(f"scale{s}", [P, 2, G]) for s in range(2)]
        norm = Norm(sb, "norm")
        s_agg, s_store = k.dmas("agg"), k.dmas("store")
        s_y, s_x, s_norm = k.sem("y"), k.sem("x"), k.sem("norm")
        s_dve, s_var, s_std, s_inv, s_factor, s_scale = (k.sem(n) for n in ("dve", "var", "std", "inv", "factor", "scale"))

        with nc.Block() as block:
            @block.sync
            def _(sp):
                def step(g):
                    n = g + -5
                    if n.live:
                        sp.wait_ge(s_norm, n.num + 1)
                        sp.dma_start(group_rows(a["table"], n), group_buf(hout[n.slot], n)).then_inc(s_store[n.slot], 16)
                    n = g + 2
                    if n.live:
                        wait(sp, s_y, n.num - 1)
                        sp.dma_start(group_buf(agg[n.slot], n), group_rows(a["agg"], n)).then_inc(s_agg[n.slot], 16)
                over_groups(sp, step)
                for s in range(2):
                    sp.wait_ge(s_store[s], 16 * ((GROUPS + 1) // 2))

            @block.gpsimd
            def _(pool):
                def step(g):
                    if g.live:
                        pool.wait_ge(s_y, g.num + 1)
                        xs = keep["x"][:, g.cols()]
                        pool.tensor_tensor(xs, xs, y[g.slot][:, 0:g.w, :].rearrange("p j d -> p (j d)"), ALU.add).then_inc(s_x, 1)
                over_groups(pool, step)

            @block.scalar
            def _(act):
                def step(g):
                    p = g + -3
                    if p.live:
                        act.wait_ge(s_var, p.num + 1)
                        ln_sqrt(nc, norm, p, keep["eps"]).then_inc(s_std, 1)
                    p = g + -4
                    if p.live:
                        act.wait_ge(s_scale, p.num + 1)
                        wait(act, s_store[p.slot], p.uses * 16)
                        ln_apply(nc, norm, p, ACT.Relu, lambda j: hout[p.slot][:, j, :], lambda j: x_tile(keep, p, j),
                                 factors=scale).then_inc(s_norm, 1)
                over_groups(act, step)

            @block.vector
            def _(dve):
                def divide(g):
                    if g.live:
                        s, w = g.slot, g.w
                        dve.wait_ge(s_agg[s], (g.uses + 1) * 16)
                        wait(dve, s_x, g.num - 1)
                        dve.tensor_tensor(y[s][:, 0:w, :], agg[s][:, 0:w, :], bcast(node_cols(keep, "inv_deg", g), w),
                                          ALU.mult).then_inc(s_y, 1)

                def inverse(q):
                    if q.live:
                        dve.wait_ge(s_std, q.num + 1)
                        st = norm.st[q.slot]
                        dve.reciprocal(st[:, Norm.RSTD, 0:q.w], st[:, Norm.STD, 0:q.w]).then_inc(s_inv, 1)

                def factor(q):
                    if q.live:
                        dve.wait_ge(s_inv, q.num + 1)
                        wait(dve, s_norm, q.num - 1)
                        dve.tensor_tensor(scale[q.slot][:, 0, 0:q.w], norm.st[q.slot][:, Norm.RSTD, 0:q.w],
                                          node_cols(keep, "dinv", q), ALU.mult).then_inc(s_factor, 1)

                def shift(q):
                    if q.live:
                        dve.wait_ge(s_factor, q.num + 1)
                        dve.scalar_tensor_tensor(scale[q.slot][:, 1, 0:q.w], norm.st[q.slot][:, Norm.SUM, 0:q.w], -0.5,
                                                 scale[q.slot][:, 0, 0:q.w], ALU.mult, ALU.mult).then_inc(s_scale, 1)

                def step(g):
                    p, q = g + -2, g + -3
                    if p.live:
                        dve.wait_ge(s_x, p.num + 1)
                        wait(dve, s_scale, p.num - 1)
                    stats = Chain(dve, s_dve, p.num * Norm.STATS)
                    ln_rows(nc, stats, norm, p, lambda j: x_tile(keep, p, j))
                    inverse(q)
                    ln_sums(nc, stats, norm, p)
                    factor(q)
                    ln_square(nc, stats, norm, p)
                    shift(q)
                    divide(g)
                    ln_var(nc, stats, norm, p, s_var)
                over_groups(dve, step)


def node_stage(k, a, keep, layer):
    nc = k.nc
    k.stage = f"nodes{layer}"
    final = layer == 3
    with ExitStack() as mem:
        def sb(name, shape, dt=F32):
            return mem.enter_context(nc.sbuf_tensor(f"{k.stage}_{name}_sb", shape, dt))

        def two(name, shape, dt=F32):
            return [sb(f"{name}{s}", shape, dt) for s in range(2)]

        K = D + 1
        weight = sb("weight", [K, D])
        slope = sb("slope", [P, 1])
        agg = two("agg", [P, G, D])
        total = two("total", [P, G, K])
        own = two("own", [P, G, D])
        aggT = two("aggT", [K, 2, SUB * P])
        y = two("y", [P, G, D])
        neg = sb("neg", [P, G, D]) if layer == 2 else None
        hout = two("hout", [P, G, D]) if not final else y
        norm = Norm(sb, "norm")
        turned = [mem.enter_context(nc.psum_tensor(f"{k.stage}_turned{s}_ps", [P, 2, 512], F32)) for s in range(2)]
        prod = [mem.enter_context(nc.psum_tensor(f"{k.stage}_prod{s}_ps", [P, 2, 512], F32)) for s in range(2)]

        s_weight, s_ones, s_sum = k.dma("weight"), k.sem("ones"), k.sem("sum")
        s_agg, s_own, s_store = k.dmas("agg"), k.dmas("own"), k.dmas("store")
        s_turned, s_aggT, s_prod, s_y, s_x = k.sem("turned"), k.sem("aggT"), k.sem("prod"), k.sem("y"), k.sem("x")
        s_dve, s_var, s_std, s_scale, s_norm = k.sem("dve"), k.sem("var"), k.sem("std"), k.sem("scale"), k.sem("norm")
        s_in, s_half, s_neg, s_inv = k.sem("in"), k.sem("half"), k.sem("neg"), k.sem("inv")

        def halves(g):
            return [(u, u * SUB, min(SUB, g.w - u * SUB)) for u in range(2) if g.w > u * SUB]

        a_group = 1 if layer == 2 else 2

        def y_made(g):
            return g.num * a_group + (1 if layer == 2 else len(halves(g)))

        with nc.Block() as block:
            @block.sync
            def _(sp):
                sp.dma_start(weight[0:D, :], a[f"L{layer}_gnn_W"]).then_inc(s_weight, 16)
                sp.dma_start(weight[D:K, :], a[f"L{layer}_gnn_b"].rearrange("(a n) -> a n", a=1)).then_inc(s_weight, 16)
                if layer == 2:
                    sp.dma_start(slope[:, :], a["L2_gnn_prelu_a"].rearrange("(a n) -> a n", a=1).to_broadcast([P, 1])).then_inc(s_weight, 16)

                def load(g):
                    wait(sp, s_sum, g.num - 1)
                    sp.dma_start(group_buf(agg[g.slot], g), group_rows(a["agg"], g)).then_inc(s_agg[g.slot], 16)
                    sp.dma_start(group_buf(own[g.slot], g), group_rows(a["table"], g)).then_inc(s_own[g.slot], 16)

                def step(g):
                    if (g + 4).live:
                        load(g + 4)
                    g = g + (-2 if final else -6)
                    if g.live:
                        sp.wait_ge(s_y if final else s_norm, y_made(g) if final else g.num + 1)
                        sp.dma_start(group_rows(a["out"] if final else a["table"], g), group_buf(hout[g.slot], g)
                                     ).then_inc(s_store[g.slot], 16)
                load(Group(0, 0))
                over_groups(sp, step)
                for s in range(2):
                    sp.wait_ge(s_store[s], 16 * ((GROUPS + 1) // 2))

            @block.gpsimd
            def _(pool):
                if layer == 3:
                    for s in range(2):
                        pool.memset(total[s][:, :, D:K], 1.0).then_inc(s_ones, 1)

                def factor(g):
                    if not g.live:
                        return
                    s, w = g.slot, g.w
                    wait(pool, s_turned, g.num - 1)
                    if layer == 2:
                        pool.tensor_copy(total[s][:, 0:w, D], node_cols(keep, "sqrt_c1", g)).then_inc(s_in, 1)
                    pool.wait_ge(s_agg[s], (g.uses + 1) * 16)
                    pool.wait_ge(s_own[s], (g.uses + 1) * 16)
                    pool.tensor_tensor(total[s][:, 0:w, 0:D], agg[s][:, 0:w, :], own[s][:, 0:w, :], ALU.add).then_inc(s_sum, 1)

                def step(g):
                    factor(g + 3)
                    g = g + -1
                    if g.live and not final:
                        pool.wait_ge(s_y, y_made(g))
                        xs = keep["x"][:, g.cols()]
                        pool.tensor_tensor(xs, xs, y[g.slot][:, 0:g.w, :].rearrange("p j d -> p (j d)"), ALU.add).then_inc(s_x, 1)
                over_groups(pool, step)

            @block.tensor
            def _(pe):
                pe.wait_ge(s_weight, 48 if layer == 2 else 32)
                if layer == 3:
                    pe.wait_ge(s_ones, 2)

                def step(g):
                    n = g + 2
                    if n.live:
                        if layer == 2:
                            pe.wait_ge(s_in, n.num + 1)
                        pe.wait_ge(s_sum, n.num + 1)
                        wait(pe, s_aggT, n.num - 1)
                        for u, j0, m in halves(n):
                            for j in range(m):
                                last = pe.transpose(turned[n.slot][0:K, u, j * P:(j + 1) * P], total[n.slot][:, j0 + j, :], keep["ident"][:, :])
                        last.then_inc(s_turned, 1)
                    if g.live:
                        pe.wait_ge(s_aggT, g.num + 1)
                        wait(pe, s_y, (g.num - 1) * a_group)
                        if final and g.known and g.num == 3:
                            for _ in range(WARM):
                                pe.transpose(prod[g.slot][:, 1, 0:P], keep["ident"][:, :], keep["ident"][:, :])
                        for u, j0, m in halves(g):
                            for j in range(m):
                                last = pe.matmul(prod[g.slot][:, u, j * D:(j + 1) * D], aggT[g.slot][:, u, j * P:(j + 1) * P],
                                                 weight[:, :], start=True, stop=True)
                        last.then_inc(s_prod, 1)
                over_groups(pe, step)

            @block.scalar
            def _(act):
                def step(g):
                    p = g + -4
                    if p.live and not final:
                        act.wait_ge(s_var, p.num + 1)
                        ln_sqrt(nc, norm, p, keep["eps"]).then_inc(s_std, 1)
                    n = g + 1
                    if n.live:
                        act.wait_ge(s_turned, n.num + 1)
                        wait(act, s_prod, n.num - 1)
                        if n.tail:
                            act.activation(aggT[n.slot][:, 0, 0:P], turned[n.slot][0:K, 0, 0:P], ACT.Copy).then_inc(s_aggT, 1)
                        else:
                            act.activation(aggT[n.slot][:, :, :], turned[n.slot][0:K, :, 0:SUB * P], ACT.Copy).then_inc(s_aggT, 1)
                    p = g + -5
                    if p.live and not final:
                        act.wait_ge(s_scale, p.num + 1)
                        wait(act, s_store[p.slot], p.uses * 16)
                        ln_apply(nc, norm, p, ACT.Relu, lambda j: hout[p.slot][:, j, :], lambda j: x_tile(keep, p, j)).then_inc(s_norm, 1)
                over_groups(act, step)

            @block.vector
            def _(dve):
                def half(g, u):
                    if not g.live or u >= len(halves(g)):
                        return
                    s = g.slot
                    if u == 0:
                        dve.wait_ge(s_prod, g.num + 1)
                        if final:
                            wait(dve, s_store[s], g.uses * 16)
                        else:
                            wait(dve, s_x, g.num - 1)
                    _, j0, m = halves(g)[u]
                    pr = prod[s][:, u, 0:m * D].rearrange("p (j d) -> p j d", d=D)
                    out = y[s][:, j0:j0 + m, :]
                    if final:
                        xs = keep["x"][:, g.cols()].rearrange("p (j d) -> p j d", d=D)
                        ins = dve.tensor_tensor(out, pr, xs[:, j0:j0 + m, :], ALU.add)
                    else:
                        col = keep["dinv"][:, bass.ds(g.num * G + j0, m)]
                        ins = dve.tensor_tensor(out, pr, bcast(col, m), ALU.mult)
                    ins.then_inc(s_half if layer == 2 else s_y, 1)

                def below(g):
                    if layer == 2 and g.live:
                        dve.wait_ge(s_half, g.num * 2 + len(halves(g)))
                        dve.tensor_scalar(neg[:, 0:g.w, :], y[g.slot][:, 0:g.w, :], 0.0, slope[:, 0:1],
                                          ALU.min, ALU.mult).then_inc(s_neg, 1)

                def above(g):
                    if layer == 2 and g.live:
                        dve.wait_ge(s_neg, g.num + 1)
                        ys = y[g.slot][:, 0:g.w, :]
                        dve.scalar_tensor_tensor(ys, ys, 0.0, neg[:, 0:g.w, :], ALU.max, ALU.add).then_inc(s_y, 1)

                def inverse(q):
                    if q.live and not final:
                        dve.wait_ge(s_std, q.num + 1)
                        wait(dve, s_norm, q.num - 1)
                        st = norm.st[q.slot]
                        dve.reciprocal(st[:, Norm.RSTD, 0:q.w], st[:, Norm.STD, 0:q.w]).then_inc(s_inv, 1)

                def shift(q):
                    if q.live and not final:
                        dve.wait_ge(s_inv, q.num + 1)
                        st = norm.st[q.slot]
                        dve.scalar_tensor_tensor(st[:, Norm.SHIFT, 0:q.w], st[:, Norm.SUM, 0:q.w], -0.5,
                                                 st[:, Norm.RSTD, 0:q.w], ALU.mult, ALU.mult).then_inc(s_scale, 1)

                def step(g):
                    r, p, q = g + -1, g + -3, g + -4
                    half(r, 0)
                    half(r, 1)
                    inverse(q)
                    if final:
                        return
                    if p.live:
                        dve.wait_ge(s_x, p.num + 1)
                        wait(dve, s_scale, p.num - 1)
                    stats = Chain(dve, s_dve, p.num * Norm.STATS)
                    ln_rows(nc, stats, norm, p, lambda j: x_tile(keep, p, j))
                    shift(q)
                    ln_sums(nc, stats, norm, p)
                    below(r)
                    ln_square(nc, stats, norm, p)
                    above(r)
                    ln_var(nc, stats, norm, p, s_var)
                over_groups(dve, step)


def mlp_stage(k, a, keep):
    nc = k.nc
    k.stage = "mlp"
    with ExitStack() as mem:
        def sb(name, shape, dt=F32):
            return mem.enter_context(nc.sbuf_tensor(f"{k.stage}_{name}_sb", shape, dt))

        def two(name, shape, dt=F32):
            return [sb(f"{name}{s}", shape, dt) for s in range(2)]

        def ps(name, shape):
            return mem.enter_context(nc.psum_tensor(f"{k.stage}_{name}_ps", shape, F32))

        K = D + 2
        wh = sb("wh", [D, HID])
        wa = sb("wa", [K, HID])
        wo = sb("wo", [P, 2, D])
        rows = {n: sb(n, [P, D]) for n in ("bias", "gamma", "beta")}
        agg = two("agg", [P, G, K])
        h = two("h", [P, G, D])
        hb = two("hb", [P, G, D])
        aggT, hT = two("aggT", [K, SUB * P]), two("hT", [D, SUB * P])
        hid = two("hid", [P, 2, SUB * P])
        y = two("y", [P, G, D])
        hout = two("hout", [P, G, D])
        norm1, norm2 = Norm(sb, "norm1"), Norm(sb, "norm2")
        turned_a, turned_h, prod = ([ps(f"{n}{u}", [P, 512]) for u in range(2)] for n in ("ta", "th", "prod"))
        hidp = [ps(f"hidp{v}", [P, 512]) for v in range(2)]

        s_weight, s_rows, s_ones = k.dma("weight"), k.dma("rows"), k.sem("ones")
        s_agg, s_h, s_store = k.dmas("agg"), k.dmas("h"), k.dmas("store")
        s_div, s_deg, s_hb, s_turned, s_copied = k.sem("div"), k.sem("deg"), k.sem("hb"), k.sem("turned"), k.sem("copied")
        s_hidp, s_hid, s_prod, s_y, s_z, s_xb, s_x = (k.sem(n) for n in ("hidp", "hid", "prod", "y", "z", "xb", "x"))
        s_dve, s_var1, s_std1, s_scale1 = k.sem("dve"), k.sem("var1"), k.sem("std1"), k.sem("scale1")
        s_dve2, s_gamma, s_var2, s_std2, s_scale2, s_norm = (
            k.sem(n) for n in ("dve2", "gamma", "var2", "std2", "scale2", "norm"))

        def halves(g):
            return [(u, u * SUB, min(SUB, g.w - u * SUB)) for u in range(2) if g.w > u * SUB]

        def upto(g, u):
            return g.num * 2 + u + 1

        def last(g):
            return g.num * 2 + len(halves(g))

        with nc.Block() as block:
            @block.sync
            def _(sp):
                wm = a["L0_gnn_Wm1"]
                sp.dma_start(wh[:, :], wm[0:D, :]).then_inc(s_weight, 16)
                sp.dma_start(wa[0:D, :], wm[D:2 * D, :]).then_inc(s_weight, 16)
                sp.dma_start(wa[D:D + 1, :], a["L0_gnn_bm1"].rearrange("(a n) -> a n", a=1)).then_inc(s_weight, 16)
                sp.dma_start(wa[D + 1:K, :], wm[2 * D:2 * D + 1, :]).then_inc(s_weight, 16)
                sp.dma_start(wo[:, :, :], a["L0_gnn_Wm2"].rearrange("(v p) d -> p v d", p=P)).then_inc(s_weight, 16)
                for n, name in (("bias", "bm2"), ("gamma", "gamma"), ("beta", "beta")):
                    sp.dma_start(rows[n][:, :], a[f"L0_gnn_{name}"].rearrange("(a n) -> a n", a=1).to_broadcast([P, D])).then_inc(s_rows, 16)

                def load(g):
                    wait(sp, s_turned, (g.num - 1) * 2)
                    wait(sp, s_hb, g.num - 1)
                    part = TAIL if g.tail else P
                    src = group_rows(a["agg0"], g).rearrange("p (j d) -> p j d", d=D)
                    sp.dma_start(agg[g.slot][0:part, 0:g.w, 0:D], src).then_inc(s_agg[g.slot], 16)
                    sp.dma_start(group_buf(h[g.slot], g), group_rows(a["table"], g)).then_inc(s_h[g.slot], 16)

                def step(g):
                    if (g + 2).live:
                        load(g + 2)
                    n = g + -5
                    if n.live:
                        sp.wait_ge(s_norm, last(n))
                        sp.dma_start(group_rows(a["table"], n), group_buf(hout[n.slot], n)).then_inc(s_store[n.slot], 16)
                over_groups(sp, step)
                for s in range(2):
                    sp.wait_ge(s_store[s], 16 * ((GROUPS + 1) // 2))

            @block.gpsimd
            def _(pool):
                for s in range(2):
                    pool.memset(agg[s][:, :, D:D + 1], 1.0).then_inc(s_ones, 1)
                pool.wait_ge(s_rows, 48)

                def step(g):
                    if g.live:
                        s, w = g.slot, g.w
                        pool.wait_ge(s_h[s], (g.uses + 1) * 16)
                        wait(pool, s_y, (g.num - 1) * 2)
                        pool.tensor_tensor(hb[s][:, 0:w, :], h[s][:, 0:w, :], rows["bias"][:, :].unsqueeze(1).to_broadcast([P, w, D]),
                                           ALU.add).then_inc(s_hb, 1)
                    n = g + 2
                    if n.live:
                        wait(pool, s_turned, (n.num - 1) * 2)
                        pool.tensor_copy(agg[n.slot][:, 0:n.w, D + 1], node_cols(keep, "deg", n)).then_inc(s_deg, 1)
                    n = g + -2
                    if n.live:
                        xs = keep["x"][:, n.cols()].rearrange("p (j d) -> p j d", d=D)
                        pool.tensor_tensor(xs, xs, rows["beta"][:, :].unsqueeze(1).to_broadcast([P, n.w, D]), ALU.add).then_inc(s_xb, 1)
                over_groups(pool, step)

            @block.tensor
            def _(pe):
                pe.wait_ge(s_weight, 16 * 5)
                pe.wait_ge(s_ones, 2)

                def turn(n, u):
                    if u == 0:
                        pe.wait_ge(s_div, n.num + 1)
                        pe.wait_ge(s_deg, n.num + 1)
                        pe.wait_ge(s_h[n.slot], (n.uses + 1) * 16)
                    _, j0, m = halves(n)[u]
                    wait(pe, s_copied, (n.num - 1) * 2 + u + 1)
                    for j in range(m):
                        pe.transpose(turned_a[u][0:K, j * P:(j + 1) * P], agg[n.slot][:, j0 + j, :], keep["ident"][:, :])
                    for j in range(m):
                        ins = pe.transpose(turned_h[u][0:D, j * P:(j + 1) * P], h[n.slot][:, j0 + j, :], keep["ident"][:, :])
                    ins.then_inc(s_turned, 1)

                def step(g):
                    n = g + 1
                    for u in range(2):
                        mine = g.live and u < len(halves(g))
                        if mine:
                            _, j0, m = halves(g)[u]
                            pe.wait_ge(s_copied, upto(g, u))
                            for v in range(2):
                                wait(pe, s_hid, g.num * 4 + u * 2 + v - 1)
                                pe.matmul(hidp[v][:, 0:m * P], wh[:, v * P:(v + 1) * P], hT[u][:, 0:m * P], start=True, stop=False)
                                pe.matmul(hidp[v][:, 0:m * P], wa[:, v * P:(v + 1) * P], aggT[u][:, 0:m * P],
                                          start=False, stop=True).then_inc(s_hidp, 1)
                        if n.live and u < len(halves(n)):
                            turn(n, u)
                        if mine:
                            wait(pe, s_y, (g.num - 1) * 2 + u + 1)
                            pe.wait_ge(s_hid, g.num * 4 + u * 2 + 2)
                            for j in range(m):
                                for v in range(2):
                                    ins = pe.matmul(prod[u][:, j * D:(j + 1) * D], hid[u][:, v, j * P:(j + 1) * P],
                                                    wo[:, v, :], start=(v == 0), stop=(v == 1))
                            ins.then_inc(s_prod, 1)
                over_groups(pe, step)

            @block.scalar
            def _(act):
                def normed1(n, u):
                    if n.live and u < len(halves(n)):
                        _, j0, m = halves(n)[u]
                        act.wait_ge(s_scale1, n.num + 1)
                        ys = y[n.slot]
                        ln_apply(nc, norm1, n, ACT.Identity, lambda j: ys[:, j, :], lambda j: ys[:, j, :],
                                 tiles=range(j0, j0 + m)).then_inc(s_z, 1)

                def normed2(n, u):
                    if n.live and u < len(halves(n)):
                        _, j0, m = halves(n)[u]
                        act.wait_ge(s_scale2, n.num + 1)
                        wait(act, s_store[n.slot], n.uses * 16)
                        ln_apply(nc, norm2, n, ACT.Relu, lambda j: hout[n.slot][:, j, :], lambda j: x_tile(keep, n, j),
                                 tiles=range(j0, j0 + m)).then_inc(s_norm, 1)

                def step(g):
                    z, q = g + -2, g + -4
                    if z.live:
                        act.wait_ge(s_var1, z.num + 1)
                        ln_sqrt(nc, norm1, z, keep["eps"]).then_inc(s_std1, 1)
                    if q.live:
                        act.wait_ge(s_var2, q.num + 1)
                        ln_sqrt(nc, norm2, q, keep["eps"]).then_inc(s_std2, 1)
                    n = g + 1
                    for u in range(2):
                        if g.live and u < len(halves(g)):
                            m = halves(g)[u][2]
                            wait(act, s_prod, (g.num - 1) * 2 + u + 1)
                            for v in range(2):
                                act.wait_ge(s_hidp, g.num * 4 + u * 2 + v + 1)
                                act.activation(hid[u][:, v, 0:m * P], hidp[v][:, 0:m * P], ACT.Relu).then_inc(s_hid, 1)
                        normed1(z, u)
                        if n.live and u < len(halves(n)):
                            m = halves(n)[u][2]
                            act.wait_ge(s_turned, upto(n, u))
                            wait(act, s_hidp, (n.num - 1) * 4 + u * 2 + 2)
                            act.activation(aggT[u][:, 0:m * P], turned_a[u][0:K, 0:m * P], ACT.Copy)
                            act.activation(hT[u][:, 0:m * P], turned_h[u][0:D, 0:m * P], ACT.Copy).then_inc(s_copied, 1)
                        normed2(q, u)
                over_groups(act, step)

            @block.vector
            def _(dve):
                per = Norm.STATS + Norm.SCALES

                def step(g):
                    n = g + -3
                    if n.live:
                        s = n.slot
                        dve.wait_ge(s_z, last(n))
                        dve.wait_ge(s_xb, n.num + 1)
                        ys = y[s][:, 0:n.w, :]
                        dve.tensor_tensor(ys, ys, rows["gamma"][:, :].unsqueeze(1).to_broadcast([P, n.w, D]), ALU.mult).then_inc(s_gamma, 1)
                        dve.wait_ge(s_gamma, n.num + 1)
                        xs = keep["x"][:, n.cols()]
                        dve.tensor_tensor(xs, xs, ys.rearrange("p j d -> p (j d)"), ALU.add).then_inc(s_x, 1)
                    n = g + -1
                    if n.live:
                        s = n.slot
                        dve.wait_ge(s_prod, last(n))
                        dve.wait_ge(s_hb, n.num + 1)
                        wait(dve, s_x, n.num - 1)
                        for u, j0, m in halves(n):
                            dve.tensor_tensor(y[s][:, j0:j0 + m, :], prod[u][:, 0:m * D].rearrange("p (j d) -> p j d", d=D),
                                              hb[s][:, j0:j0 + m, :], ALU.add).then_inc(s_y, 1)
                    n = g + -2
                    if n.live:
                        dve.wait_ge(s_std1, n.num + 1)
                        c = Chain(dve, s_dve, n.num * per + Norm.STATS - (G - n.w))
                        ln_scales(nc, c, norm1, n).then_inc(s_scale1, 1)
                    n = g + -4
                    if n.live:
                        dve.wait_ge(s_std2, n.num + 1)
                        c = Chain(dve, s_dve2, n.num * per + Norm.STATS - (G - n.w))
                        ln_scales(nc, c, norm2, n).then_inc(s_scale2, 1)
                    n = g + -3
                    if n.live:
                        dve.wait_ge(s_x, n.num + 1)
                        wait(dve, s_norm, (n.num - 1) * 2)
                        c = Chain(dve, s_dve2, n.num * per)
                        ln_stats(nc, c, norm2, n, lambda j: x_tile(keep, n, j), s_var2)
                    n = g + -1
                    if n.live:
                        dve.wait_ge(s_y, last(n))
                        c = Chain(dve, s_dve, n.num * per)
                        ln_stats(nc, c, norm1, n, lambda j: y[n.slot][:, j, :], s_var1)
                    n = g + 2
                    if n.live:
                        dve.wait_ge(s_agg[n.slot], (n.uses + 1) * 16)
                        v = agg[n.slot][:, 0:n.w, 0:D]
                        dve.tensor_tensor(v, v, bcast(node_cols(keep, "inv_deg", n), n.w), ALU.mult).then_inc(s_div, 1)
                over_groups(dve, step)


class Chunk:

    def __init__(self, i, c):
        self.i, self.c = i, c
        self.known = isinstance(i, int)
        self.slot = c % 2
        self.num = 2 * i + c
        self.uses = i + c // 2
        self.live = not self.known or 0 <= self.num < CHUNKS

    def __add__(self, d):
        return Chunk(self.i, self.c + d)

    def tiles(self):
        return bass.ds(self.num * CT, CT)


_WEIGHTS = ["L0_gnn_W1", "L0_gnn_b1", "L0_gnn_W2", "L0_gnn_b2", "L0_gnn_Wm1", "L0_gnn_bm1", "L0_gnn_Wm2", "L0_gnn_bm2",
            "L0_gnn_gamma", "L0_gnn_beta", "L1_gnn_W", "L1_gnn_b", "L2_gnn_W", "L2_gnn_b", "L2_gnn_prelu_a",
            "L3_gnn_W", "L3_gnn_b"]


def build(nc, a):
    a = dict(a)
    for name, shape, dt in (("table", (N, D), F32), ("agg0", (N, D), F32), ("agg", (N, D), F32),
                            ("targets", (2, SORT + 2), I32), ("same", (2, SORT), BF16),
                            ("payload", (EDGES, 2), I32), ("feat_parts", ((PARTS * PARTS + 1) * FEATS, EDGES), BF16),
                            ("w1_parts", (PARTS * FEATS, HID), BF16), ("b1_parts", (PARTS, HID), BF16)):
        a[name] = nc.dram_tensor(name, shape, dt).ap()
    with ExitStack() as ctx:
        k = Kernel(nc)
        k.turn_points = turn_points()

        def sb(name, shape, dt=F32):
            return ctx.enter_context(nc.sbuf_tensor(f"{name}_keep", shape, dt))

        keep = {
            "x": sb("x_all", [P, (ROWS + 1) * D]),
            "ident": sb("ident", [P, P]),
            "index": sb("index", [P, 4, TILES], I32),
            "dst": sb("dst_sorted", [P, TILES]),
            "payload": sb("payload", [P, TILES, 2], I32),
            "eps": sb("eps", [P, 2]),
        }
        names = ("cnt", "deg", "inv_deg", "sqrt_c1", "dinv")
        keep["node"] = sb("node", [P, len(names), ROWS + 1])
        for n, name in enumerate(names):
            keep[name] = keep["node"][:, n, :]
        keep["zeros"] = sb("zeros", [P, ROWS * D // FILLS])
        for stage in STAGES:
            stage(k, a, keep)
            k.end()


def edges(layer):
    return lambda k, a, keep: edge_stage(k, a, keep, layer)


def nodes(layer):
    return lambda k, a, keep: node_stage(k, a, keep, layer)


STAGES = [sort_stage, first_stage, edges(0), mlp_stage, edges(1), mean_stage, edges(2), nodes(2), edges(3), nodes(3)]


def kernel(**inputs):
    import numpy as _np
    import concourse.bacc as _bacc
    from concourse import mybir as _mybir
    from concourse.bass_utils import run_bass_kernel_spmd as _run

    nc = _bacc.Bacc("TRN2", target_bir_lowering=False, num_devices=1)
    pad = SORT - E
    laid = {
        "x": inputs["x"],
        "src": _np.concatenate([inputs["src"], _np.full(pad, SRC_PAD, _np.int32)]).reshape(P, COLS),
        "dst": _np.concatenate([inputs["dst"], _np.full(pad, DST_PAD, _np.int32)]).reshape(P, COLS),
        "edge_attr_T": _np.concatenate([inputs["edge_attr_3"], _np.zeros((EDGES - E, FEATS), _np.float32)]).T,
    }
    laid.update({name: inputs[name] for name in _WEIGHTS})
    arrays, args = {}, {}
    for name, value in laid.items():
        value = _np.ascontiguousarray(value)
        arrays[f"in_{name}"] = value
        args[name] = nc.dram_tensor(f"in_{name}", value.shape, _mybir.dt.from_np(value.dtype), kind="ExternalInput").ap()
    args["out"] = nc.dram_tensor("out_0", (N, D), F32, kind="ExternalOutput").ap()
    build(nc, args)
    r = _run(nc, [arrays], core_ids=[0])
    return r.results[0]["out_0"]
```
